# Optimizing a Trainium2 kernel written in Bass

```python
import numpy as np
import jax
import jax.numpy as jnp

def _softmax(x, axis=-1):
    return jax.nn.softmax(x, axis=axis)

def _gelu(x):
    return jax.nn.gelu(x, approximate=True)

def _silu(x):
    return jax.nn.silu(x)

def _sigmoid(x):
    return jax.nn.sigmoid(x)

def _layernorm(x, axis=-1, eps=1e-05):
    m = jnp.mean(x, axis=axis, keepdims=True)
    v = jnp.var(x, axis=axis, keepdims=True)
    return (x - m) / jnp.sqrt(v + eps)

def _scatter_add(tgt, idx, src, axis=0):
    return tgt.at[idx].add(src)

def _segment_sum(src, seg, n):
    return jax.ops.segment_sum(src, seg, n)
kernel_name = 'mk_seq_preln_d2_jaxref_r8_57633a'

def setup_inputs(seed: int=0):
    np.random.seed(seed)
    _w = jnp.asarray

    def _L0_attn_setup():
        import jax, jax.numpy as jnp
        import numpy as np
        B, T, D = (4, 256, 128)
        H, DK = (8, 64)
        EPS = 1e-06

        def _xavier(key, shape):
            fan_in, fan_out = (shape[1], shape[0])
            lim = float(np.sqrt(6.0 / (fan_in + fan_out)))
            return jax.random.uniform(key, shape, jnp.float32, -lim, lim)

        def _phi(u):
            return jax.nn.elu(u) + 1.0
        key = jax.random.key(seed)
        ks = jax.random.split(key, 7)
        x = jax.random.normal(ks[0], (B, T, D), jnp.float32)
        W_Q = _xavier(ks[1], (H * DK, D))
        W_K = _xavier(ks[2], (H * DK, D))
        W_V = _xavier(ks[3], (H * DK, D))
        W_g_w = _xavier(ks[4], (H * DK, D))
        W_g_b = jax.random.normal(ks[5], (H * DK,), jnp.float32) * 0.02
        W_O = _xavier(ks[6], (D, H * DK))
        decay_log = jnp.zeros((H,), jnp.float32)
        return {'x': x, 'W_Q': W_Q, 'W_K': W_K, 'W_V': W_V, 'W_g_w': W_g_w, 'W_g_b': W_g_b, 'W_O': W_O, 'decay_log': decay_log}
    _L0_attn_in = _L0_attn_setup()

    def _L0_ffn_setup():
        import jax, jax.numpy as jnp
        import numpy as np
        B, S, H, E, K = (4, 256, 128, 8, 2)
        key = jax.random.key(seed)
        k0, k1, k2, k3 = jax.random.split(key, 4)
        x = jax.random.normal(k0, (B, S, H), dtype=jnp.float32)
        router_w = jax.random.normal(k1, (E, H), dtype=jnp.float32) * np.float32(1.0 / np.sqrt(H))
        xav1 = np.float32(np.sqrt(2.0 / (2 * H + H)))
        w1 = jax.random.normal(k2, (E, 2 * H, H), dtype=jnp.float32) * xav1
        w2 = jax.random.normal(k3, (E, H, 2 * H), dtype=jnp.float32) * xav1
        return {'x': x, 'router_w': router_w, 'w1': w1, 'w2': w2}
    _L0_ffn_in = _L0_ffn_setup()

    def _L1_attn_setup():
        import jax, jax.numpy as jnp
        import numpy as np
        D_MODEL = 128
        EXP = 2
        D_IN = D_MODEL * EXP
        D_STATE = 16
        CONV_D = 4
        BATCH = 4
        SEQ = 256

        def _rmsnorm(x, w, eps=1e-06):
            return x * jax.lax.rsqrt(jnp.mean(x * x, axis=-1, keepdims=True) + eps) * w
        key = jax.random.key(seed)
        ks = jax.random.split(key, 8)
        sd = 1.0 / np.sqrt(D_MODEL)
        sdi = 1.0 / np.sqrt(D_IN)
        return {'x': jax.random.normal(ks[0], (BATCH, SEQ, D_MODEL), jnp.float32), 'norm_w': jnp.ones((D_MODEL,), jnp.float32), 'Win': jax.random.normal(ks[1], (D_MODEL, D_IN), jnp.float32) * sd, 'b_in': jnp.zeros((D_IN,), jnp.float32), 'conv_w': jax.random.normal(ks[2], (D_IN, 1, CONV_D), jnp.float32) * 0.5, 'conv_b': jnp.zeros((D_IN,), jnp.float32), 'A': jax.random.normal(ks[3], (D_IN, D_STATE, D_STATE), jnp.float32) * 0.1, 'Bm': jax.random.normal(ks[4], (D_IN, D_STATE, 1), jnp.float32), 'Cm': jax.random.normal(ks[5], (D_IN, 1, D_STATE), jnp.float32), 'Wout': jax.random.normal(ks[6], (D_IN, D_MODEL), jnp.float32) * sdi, 'b_out': jnp.zeros((D_MODEL,), jnp.float32)}
    _L1_attn_in = _L1_attn_setup()

    def _L1_ffn_setup():
        import math
        import jax, jax.numpy as jnp
        import numpy as np
        H = 128
        F = 512
        E = 8
        TOP_K = 2
        CAP_FACTOR = 1.25
        MIN_CAP = 4
        SHARED_SCALE = 0.1

        def _top2_gating(logits, capacity):
            N, nE = logits.shape
            gates = jax.nn.softmax(logits, axis=-1)
            idx1 = jnp.argmax(gates, axis=-1)
            mask1 = jax.nn.one_hot(idx1, nE, dtype=gates.dtype)
            idx2 = jnp.argmax(gates * (1.0 - mask1), axis=-1)
            mask2 = jax.nn.one_hot(idx2, nE, dtype=gates.dtype)
            pos1 = jnp.cumsum(mask1, axis=0) - mask1
            mask1 = mask1 * (pos1 < capacity)
            pos2 = jnp.cumsum(mask2, axis=0) - mask2 + jnp.sum(mask1, axis=0, keepdims=True)
            mask2 = mask2 * (pos2 < capacity)
            g1 = jnp.sum(gates * mask1, axis=-1)
            g2 = jnp.sum(gates * mask2, axis=-1)
            denom = jnp.maximum(g1 + g2, jnp.finfo(gates.dtype).eps)
            g1, g2 = (g1 / denom, g2 / denom)
            loc1 = jnp.sum(pos1 * mask1, axis=-1).astype(jnp.int32)
            loc2 = jnp.sum(pos2 * mask2, axis=-1).astype(jnp.int32)
            oh1 = jax.nn.one_hot(loc1, capacity, dtype=gates.dtype)
            oh2 = jax.nn.one_hot(loc2, capacity, dtype=gates.dtype)
            combine = (g1[:, None] * mask1)[:, :, None] * oh1[:, None, :] + (g2[:, None] * mask2)[:, :, None] * oh2[:, None, :]
            dispatch = (combine > 0).astype(gates.dtype)
            return (combine, dispatch)
        key = jax.random.key(seed)
        ks = jax.random.split(key, 10)
        s_h = 1.0 / math.sqrt(H)
        s_f = 1.0 / math.sqrt(F)
        return {'hidden_states': jax.random.normal(ks[0], (2, 256, H), jnp.float32), 'router_w': jax.random.uniform(ks[1], (H, E), jnp.float32, -s_h, s_h), 'w1': jax.random.uniform(ks[2], (E, H, F), jnp.float32, -s_h, s_h), 'b1': jax.random.uniform(ks[3], (E, F), jnp.float32, -s_h, s_h), 'w2': jax.random.uniform(ks[4], (E, F, H), jnp.float32, -s_f, s_f), 'b2': jax.random.uniform(ks[5], (E, H), jnp.float32, -s_f, s_f), 'sw1': jax.random.uniform(ks[6], (H, F), jnp.float32, -s_h, s_h), 'sb1': jax.random.uniform(ks[7], (F,), jnp.float32, -s_h, s_h), 'sw2': jax.random.uniform(ks[8], (F, H), jnp.float32, -s_f, s_f), 'sb2': jax.random.uniform(ks[9], (H,), jnp.float32, -s_f, s_f)}
    _L1_ffn_in = _L1_ffn_setup()
    _d = {'L0_attn_x': _L0_attn_in['x'], 'L0_attn_W_Q': _L0_attn_in['W_Q'], 'L0_attn_W_K': _L0_attn_in['W_K'], 'L0_attn_W_V': _L0_attn_in['W_V'], 'L0_attn_W_g_w': _L0_attn_in['W_g_w'], 'L0_attn_W_g_b': _L0_attn_in['W_g_b'], 'L0_attn_W_O': _L0_attn_in['W_O'], 'L0_attn_decay_log': _L0_attn_in['decay_log'], 'L0_ffn_router_w': _L0_ffn_in['router_w'], 'L0_ffn_w1': _L0_ffn_in['w1'], 'L0_ffn_w2': _L0_ffn_in['w2'], 'L1_attn_norm_w': _L1_attn_in['norm_w'], 'L1_attn_Win': _L1_attn_in['Win'], 'L1_attn_b_in': _L1_attn_in['b_in'], 'L1_attn_conv_w': _L1_attn_in['conv_w'], 'L1_attn_conv_b': _L1_attn_in['conv_b'], 'L1_attn_A': _L1_attn_in['A'], 'L1_attn_Bm': _L1_attn_in['Bm'], 'L1_attn_Cm': _L1_attn_in['Cm'], 'L1_attn_Wout': _L1_attn_in['Wout'], 'L1_attn_b_out': _L1_attn_in['b_out'], 'L1_ffn_router_w': _L1_ffn_in['router_w'], 'L1_ffn_w1': _L1_ffn_in['w1'], 'L1_ffn_b1': _L1_ffn_in['b1'], 'L1_ffn_w2': _L1_ffn_in['w2'], 'L1_ffn_b2': _L1_ffn_in['b2'], 'L1_ffn_sw1': _L1_ffn_in['sw1'], 'L1_ffn_sb1': _L1_ffn_in['sb1'], 'L1_ffn_sw2': _L1_ffn_in['sw2'], 'L1_ffn_sb2': _L1_ffn_in['sb2']}
    _x0 = _d['L0_attn_x']
    _d['L0_attn_x'] = jax.random.normal(jax.random.fold_in(jax.random.key(seed), 1), (4, 1024, 128), dtype=_x0.dtype)
    del _x0
    return _d

def reference(L0_attn_x, L0_attn_W_Q, L0_attn_W_K, L0_attn_W_V, L0_attn_W_g_w, L0_attn_W_g_b, L0_attn_W_O, L0_attn_decay_log, L0_ffn_router_w, L0_ffn_w1, L0_ffn_w2, L1_attn_norm_w, L1_attn_Win, L1_attn_b_in, L1_attn_conv_w, L1_attn_conv_b, L1_attn_A, L1_attn_Bm, L1_attn_Cm, L1_attn_Wout, L1_attn_b_out, L1_ffn_router_w, L1_ffn_w1, L1_ffn_b1, L1_ffn_w2, L1_ffn_b2, L1_ffn_sw1, L1_ffn_sb1, L1_ffn_sw2, L1_ffn_sb2):

    def _L0_attn_ref(x, W_Q, W_K, W_V, W_g_w, W_g_b, W_O, decay_log):
        import jax, jax.numpy as jnp
        import numpy as np
        B, T, D = (4, 256, 128)
        H, DK = (8, 64)
        EPS = 1e-06

        def _xavier(key, shape):
            fan_in, fan_out = (shape[1], shape[0])
            lim = float(np.sqrt(6.0 / (fan_in + fan_out)))
            return jax.random.uniform(key, shape, jnp.float32, -lim, lim)

        def _phi(u):
            return jax.nn.elu(u) + 1.0
        b, t, d = x.shape
        q = _phi((x @ W_Q.T).reshape(b, t, H, DK))
        k = _phi((x @ W_K.T).reshape(b, t, H, DK))
        v = (x @ W_V.T).reshape(b, t, H, DK)
        gamma = jax.nn.sigmoid(decay_log)
        g4 = gamma[None, :, None, None]
        g3 = gamma[None, :, None]
        qT = jnp.moveaxis(q, 1, 0)
        kT = jnp.moveaxis(k, 1, 0)
        vT = jnp.moveaxis(v, 1, 0)
        S0 = jnp.zeros((b, H, DK, DK), x.dtype)
        z0 = jnp.zeros((b, H, DK), x.dtype)

        def step(carry, inp):
            S, z = carry
            qt, kt, vt = inp
            S = g4 * S + jnp.einsum('bhi,bhj->bhij', kt, vt)
            z = g3 * z + kt
            num = jnp.einsum('bhij,bhi->bhj', S, qt)
            den = jnp.sum(z * qt, axis=-1, keepdims=True) + EPS
            return ((S, z), num / den)
        _, ys = jax.lax.scan(step, (S0, z0), (qT, kT, vT))
        outputs = jnp.moveaxis(ys, 0, 1)
        gate = jax.nn.sigmoid(x @ W_g_w.T + W_g_b).reshape(b, t, H, DK)
        y = (outputs * gate).reshape(b, t, H * DK)
        return y @ W_O.T

    def _L0_ffn_ref(x, router_w, w1, w2):
        import jax, jax.numpy as jnp
        import numpy as np
        B, S, H, E, K = (4, 256, 128, 8, 2)
        bsz, seq, hidden = x.shape
        n_experts = w1.shape[0]
        tokens = x.reshape(-1, hidden)
        T = tokens.shape[0]
        logits = tokens @ router_w.T
        topv, topi = jax.lax.top_k(logits, K)
        w = jax.nn.softmax(topv, axis=-1).astype(tokens.dtype)
        gate = jnp.zeros((T, n_experts), tokens.dtype).at[jnp.arange(T)[:, None], topi].add(w)
        out = jnp.zeros_like(tokens)
        for e in range(n_experts):
            h = jax.nn.gelu(tokens @ w1[e].T, approximate=False)
            y = h @ w2[e].T
            out = out + gate[:, e:e + 1] * y
        return out.reshape(bsz, seq, hidden)

    def _L1_attn_ref(x, norm_w, Win, b_in, conv_w, conv_b, A, Bm, Cm, Wout, b_out):
        import jax, jax.numpy as jnp
        import numpy as np
        D_MODEL = 128
        EXP = 2
        D_IN = D_MODEL * EXP
        D_STATE = 16
        CONV_D = 4
        BATCH = 4
        SEQ = 256

        def _rmsnorm(x, w, eps=1e-06):
            return x * jax.lax.rsqrt(jnp.mean(x * x, axis=-1, keepdims=True) + eps) * w
        res = x
        h = _rmsnorm(x, norm_w)
        u = h @ Win + b_in
        u = u.transpose(0, 2, 1)
        u = jax.lax.conv_general_dilated(u, conv_w, window_strides=(1,), padding=[(CONV_D - 1, 0)], feature_group_count=D_IN, dimension_numbers=('NCH', 'OIH', 'NCH')) + conv_b[None, :, None]
        u = u.transpose(0, 2, 1)
        Bv = Bm[:, :, 0]
        Cv = Cm[:, 0, :]

        def step(hc, u_t):
            hc = jnp.einsum('bdr,drs->bds', hc, A) + u_t[:, :, None] * Bv[None]
            y = jnp.einsum('bds,ds->bd', hc, Cv)
            return (hc, y)
        h0 = jnp.zeros((x.shape[0], D_IN, D_STATE), u.dtype)
        _, ys = jax.lax.scan(step, h0, u.transpose(1, 0, 2))
        y = ys.transpose(1, 0, 2)
        return y @ Wout + b_out + res

    def _L1_ffn_ref(hidden_states, router_w, w1, b1, w2, b2, sw1, sb1, sw2, sb2):
        import math
        import jax, jax.numpy as jnp
        import numpy as np
        H = 128
        F = 512
        E = 8
        TOP_K = 2
        CAP_FACTOR = 1.25
        MIN_CAP = 4
        SHARED_SCALE = 0.1

        def _top2_gating(logits, capacity):
            N, nE = logits.shape
            gates = jax.nn.softmax(logits, axis=-1)
            idx1 = jnp.argmax(gates, axis=-1)
            mask1 = jax.nn.one_hot(idx1, nE, dtype=gates.dtype)
            idx2 = jnp.argmax(gates * (1.0 - mask1), axis=-1)
            mask2 = jax.nn.one_hot(idx2, nE, dtype=gates.dtype)
            pos1 = jnp.cumsum(mask1, axis=0) - mask1
            mask1 = mask1 * (pos1 < capacity)
            pos2 = jnp.cumsum(mask2, axis=0) - mask2 + jnp.sum(mask1, axis=0, keepdims=True)
            mask2 = mask2 * (pos2 < capacity)
            g1 = jnp.sum(gates * mask1, axis=-1)
            g2 = jnp.sum(gates * mask2, axis=-1)
            denom = jnp.maximum(g1 + g2, jnp.finfo(gates.dtype).eps)
            g1, g2 = (g1 / denom, g2 / denom)
            loc1 = jnp.sum(pos1 * mask1, axis=-1).astype(jnp.int32)
            loc2 = jnp.sum(pos2 * mask2, axis=-1).astype(jnp.int32)
            oh1 = jax.nn.one_hot(loc1, capacity, dtype=gates.dtype)
            oh2 = jax.nn.one_hot(loc2, capacity, dtype=gates.dtype)
            combine = (g1[:, None] * mask1)[:, :, None] * oh1[:, None, :] + (g2[:, None] * mask2)[:, :, None] * oh2[:, None, :]
            dispatch = (combine > 0).astype(gates.dtype)
            return (combine, dispatch)
        B, S, h = hidden_states.shape
        x = hidden_states.reshape(-1, h)
        N = x.shape[0]
        capacity = min(max(MIN_CAP, math.ceil(TOP_K * CAP_FACTOR * N / E)), N)
        logits = x @ router_w
        combine, dispatch = _top2_gating(logits, capacity)
        expert_in = jnp.einsum('nec,nh->ech', dispatch, x)
        hmid = jax.nn.silu(jnp.einsum('ech,ehf->ecf', expert_in, w1) + b1[:, None, :])
        expert_out = jnp.einsum('ecf,efh->ech', hmid, w2) + b2[:, None, :]
        y = jnp.einsum('nec,ech->nh', combine, expert_out)
        shared = jax.nn.silu(x @ sw1 + sb1) @ sw2 + sb2
        out = y + SHARED_SCALE * shared
        return out.reshape(B, S, h)
    x = L0_attn_x
    x = x + _L0_attn_ref(_layernorm(x, axis=-1), L0_attn_W_Q, L0_attn_W_K, L0_attn_W_V, L0_attn_W_g_w, L0_attn_W_g_b, L0_attn_W_O, L0_attn_decay_log)
    x = x + _L0_ffn_ref(_layernorm(x, axis=-1), L0_ffn_router_w, L0_ffn_w1, L0_ffn_w2)
    x = x + _L1_attn_ref(_layernorm(x, axis=-1), L1_attn_norm_w, L1_attn_Win, L1_attn_b_in, L1_attn_conv_w, L1_attn_conv_b, L1_attn_A, L1_attn_Bm, L1_attn_Cm, L1_attn_Wout, L1_attn_b_out)
    x = x + _L1_ffn_ref(_layernorm(x, axis=-1), L1_ffn_router_w, L1_ffn_w1, L1_ffn_b1, L1_ffn_w2, L1_ffn_b2, L1_ffn_sw1, L1_ffn_sb1, L1_ffn_sw2, L1_ffn_sb2)
    return x

_drawn_inputs = setup_inputs


def setup_inputs(seed=0):
    import zlib

    import numpy as np

    out = dict(_drawn_inputs(seed))
    spreads = {'L0_attn_decay_log': (0.0, 0.3),
     'L1_attn_norm_w': (1.0, 0.2),
     'L1_attn_b_in': (0.0, 0.1),
     'L1_attn_conv_b': (0.0, 0.1),
     'L1_attn_b_out': (0.0, 0.424)}
    factors = {'L0_attn_W_g_b': 4.005,
     'L1_ffn_b1': 24.388,
     'L1_ffn_b2': 8.0,
     'L1_ffn_sw1': 8.0,
     'L1_ffn_sb1': 8.0,
     'L1_ffn_sw2': 8.0,
     'L1_ffn_sb2': 64.0,
     'L0_attn_W_Q': 2.766}
    for name, (base, spread) in spreads.items():
        noise = np.random.default_rng([zlib.crc32(name.encode()), seed]).standard_normal(out[name].shape)
        drawn = base * np.exp(spread * noise) if base else spread * noise
        out[name] = jnp.asarray(drawn.astype(out[name].dtype))
    for name, factor in factors.items():
        out[name] = (out[name] * factor).astype(out[name].dtype)
    return out
```

```python
from contextlib import ExitStack

import numpy as np
import concourse.bass as bass
from concourse import mybir

F32 = mybir.dt.float32
ALU = mybir.AluOpType
ACT = mybir.ActivationFunctionType
AX = mybir.AxisListType

P = 128
BATCH, SEQ, D = 4, 1024, 128
CHUNKS = SEQ // P
WIDE = BATCH * P
HEADS, DK = 8, 64
HD = HEADS * DK
PAIRS = HEADS // 2
LN_EPS = 1e-5
DEN_EPS = 1e-6


def at(i, per_turn, k):
    return i * per_turn + k


def wide(ap, n=BATCH):
    return ap.rearrange("p (b f) -> p b f", b=n)


class Scope:

    def __init__(self, nc, ctx, name):
        self.nc, self.ctx, self.name = nc, ctx, name

    def sb(self, name, cols, parts=P):
        return self.ctx.enter_context(self.nc.sbuf_tensor(f"{self.name}_{name}", [parts, cols], F32))

    def bank(self, name):
        return self.ctx.enter_context(self.nc.psum_tensor(f"{self.name}_{name}", [P, 512], F32))

    def sem(self, name):
        return self.ctx.enter_context(self.nc.semaphore(f"{self.name}_{name}"))


def attention_phase(nc, xs, x, wq, wk, wv, wg, bg, wo, decay_all, decay_pair, ident_d, lag_d, causal_d, tpos_d, left_d):
    with ExitStack() as ctx:
        S = Scope(nc, ctx, "attn")
        ident, lag, causal, tpos = S.sb("ident", P), S.sb("lag", P), S.sb("causal", P), S.sb("tpos", P)
        left = S.sb("left", 1)
        WQ, WK, WV, WG, WO = (S.sb(n, HD) for n in ("WQ", "WK", "WV", "WG", "WO"))
        half_bg, bgc = S.sb("half_bg", PAIRS), S.sb("bgc", PAIRS)
        dl = S.sb("dl", HEADS + PAIRS)
        tmp, lg = S.sb("tmp", HEADS + PAIRS), S.sb("lg", HEADS + PAIRS)
        mask = S.sb("mask", HEADS * P)
        qpow = S.sb("qpow", PAIRS * P)
        kpow = S.sb("kpow", HEADS)
        gchunk = S.sb("gchunk", PAIRS)
        mhalf = S.sb("mhalf", BATCH)
        stats, mv, vpe, rstd = S.sb("stats", 6 * BATCH), S.sb("mv", 2 * BATCH), S.sb("vpe", BATCH), S.sb("rstd", BATCH)
        xn, xT = S.sb("xn", WIDE), S.sb("xT", WIDE)
        e = [S.sb(f"e{k}", WIDE) for k in range(2)]
        e1 = [S.sb(f"e1{k}", WIDE) for k in range(2)]
        qT, kT, qd, gate = (S.sb(n, PAIRS * WIDE) for n in ("qT", "kT", "qd", "gate"))
        kd = S.sb("kd", BATCH * HD)
        v1 = S.sb("v1", BATCH * HEADS * (DK + 1))
        a = [S.sb(f"a{k}", WIDE) for k in range(2)]
        state = S.sb("state", PAIRS * BATCH * (DK + 1))
        den, rden = S.sb("den", BATCH), S.sb("rden", BATCH)
        y, yT = S.sb("y", BATCH * HD), S.sb("yT", PAIRS * WIDE)
        proj = [S.bank(f"proj{k}") for k in range(2)]
        score = [S.bank(f"score{k}") for k in range(2)]
        av = [S.bank(f"av{k}") for k in range(2)]
        stp, turn = S.bank("stp"), S.bank("turn")

        names = ("loaded x_loaded consts neg_abs exped logged lg_ready tables gmul mean_var var_eps rstd xn xTp xT proj "
                 "exp capped phi gate v ktr kd qd score a av den rden y stp state ytr yT out res held").split()
        s = {n: S.sem(n) for n in names}
        x_view = x.rearrange("b (c p) f -> p c b f", p=P)
        v4 = v1[:, :].rearrange("p (b h j) -> p b h j", b=BATCH, h=HEADS)
        y3, kd3 = wide(y[:, :]), wide(kd[:, :])
        st4 = state[:, :].rearrange("p (q b j) -> p q b j", q=PAIRS, b=BATCH)
        NSETUP = 14

        block = ctx.enter_context(nc.Block())

        @block.sync
        def _(sp):
            for c in range(CHUNKS):
                sp.dma_start(xs[:, c * WIDE:(c + 1) * WIDE].rearrange("p (b f) -> p b f", b=BATCH),
                             x_view[:, c]).then_inc(s["x_loaded"], 16)

        @block.scalar
        def _(act):
            for dst, src in ((dl[:, 0:HEADS], decay_all), (dl[:, HEADS:], decay_pair), (lag[:, :], lag_d),
                             (causal[:, :], causal_d), (tpos[:, :], tpos_d), (left[:, :], left_d),
                             (bgc[:, :], bg), (ident[:, :], ident_d), (WQ[:, :], wq), (WK[:, :], wk),
                             (WG[:, :], wg), (WV[:, :], wv), (WO[:, :], wo)):
                act.dma_start(dst, src).then_inc(s["loaded"], 16)
            act.wait_ge(s["neg_abs"], 1)
            act.activation(tmp[:, :], tmp[:, :], ACT.Exp).then_inc(s["exped"], 1)
            act.wait_ge(s["exped"], 1)
            act.activation(tmp[:, :], tmp[:, :], ACT.Ln, bias=1.0).then_inc(s["logged"], 1)
            act.wait_ge(s["lg_ready"], 1)
            for h in range(HEADS):
                act.activation(mask[:, h * P:(h + 1) * P], lag[:, :], ACT.Exp,
                               scale=lg[:, h:h + 1]).then_inc(s["tables"], 1)
            for p in range(PAIRS):
                act.activation(qpow[:, p * P:(p + 1) * P], tpos[:, :], ACT.Exp,
                               scale=lg[:, HEADS + p:HEADS + p + 1]).then_inc(s["tables"], 1)
            act.activation(kpow[:, :], lg[:, 0:HEADS], ACT.Exp, scale=left[:, 0:1]).then_inc(s["tables"], 1)
            act.activation(gchunk[:, :], lg[:, HEADS:], ACT.Exp, scale=float(P)).then_inc(s["tables"], 1)

            def token_columns(i):
                act.wait_ge(s["xTp"], at(i, 1, 1))
                act.activation(xT[:, :], turn[:, :], ACT.Copy).then_inc(s["xT"], 1)

            def turn_of(i, last):
                for k in range(2 * PAIRS):
                    act.wait_ge(s["proj"], at(i, 16, k + 1))
                    if k >= 2:
                        act.wait_ge(s["capped"], at(i, 8, k - 1))
                    act.activation(e[k % 2][:, :], proj[k % 2][:, :], ACT.Exp).then_inc(s["exp"], 1)
                for p in range(PAIRS):
                    act.wait_ge(s["proj"], at(i, 16, 9 + p))
                    act.activation(gate[:, p * WIDE:(p + 1) * WIDE], proj[p % 2][:, :], ACT.Tanh,
                                   bias=half_bg[:, p:p + 1], scale=0.5).then_inc(s["gate"], 1)
                for b in range(BATCH):
                    act.wait_ge(s["proj"], at(i, 16, 13 + b))
                    act.activation(v4[:, b, :, 0:DK], proj[b % 2][:, :].rearrange("p (h j) -> p h j", h=HEADS),
                                   ACT.Copy).then_inc(s["v"], 1)
                if not last:
                    token_columns(i + 1)

            act.wait_ge(s["gmul"], 2)
            token_columns(0)
            with act.Fori(0, CHUNKS - 1) as i:
                turn_of(i, False)
            turn_of(CHUNKS - 1, True)

        @block.gpsimd
        def _(pool):
            pool.memset(mhalf[:, :], -0.5).then_inc(s["consts"], 1)
            pool.wait_ge(s["consts"], 1)
            pool.wait_ge(s["tables"], NSETUP)

            def inverse_deviation(i):
                pool.wait_ge(s["var_eps"], at(i, 1, 1))
                pool.tensor_tensor(rstd[:, :], vpe[:, :], mhalf[:, :], ALU.pow).then_inc(s["rstd"], 1)

            def turn_of(i, last):
                for k in range(2 * PAIRS):
                    pool.wait_ge(s["exp"], at(i, 8, k + 1))
                    if k >= 2:
                        pool.wait_ge(s["phi"], at(i, 8, k - 1))
                    pool.sem_inc(s["held"], 1)
                    pool.tensor_scalar(e1[k % 2][:, :], e[k % 2][:, :], 1.0, None, ALU.min).then_inc(s["capped"], 1)
                for p in range(PAIRS):
                    pool.wait_ge(s["phi"], at(i, 8, p + 1))
                    pool.tensor_tensor(wide(qd[:, p * WIDE:(p + 1) * WIDE]), wide(qT[:, p * WIDE:(p + 1) * WIDE]),
                                       qpow[:, p * P:(p + 1) * P].unsqueeze(1).to_broadcast([P, BATCH, P]),
                                       ALU.mult).then_inc(s["qd"], 1)
                if not last:
                    inverse_deviation(i + 1)

            inverse_deviation(0)
            with pool.Fori(0, CHUNKS - 1) as i:
                turn_of(i, False)
            turn_of(CHUNKS - 1, True)

        @block.tensor
        def _(pe):
            def token_columns(i):
                pe.wait_ge(s["xn"], at(i, 1, 1))
                for b in range(BATCH):
                    mm = pe.transpose(turn[:, b * P:(b + 1) * P], xn[:, b * P:(b + 1) * P], ident[:, :])
                mm.then_inc(s["xTp"], 1)

            def turn_of(i, last):
                pe.wait_ge(s["xT"], at(i, 1, 1))
                k = 0
                for W in (WQ, WK, WG):
                    for p in range(PAIRS):
                        if k < 2:
                            pe.wait_ge(s["res"], i + 1)
                        elif k < 10:
                            pe.wait_ge(s["phi"], at(i, 8, k - 1))
                        else:
                            pe.wait_ge(s["gate"], at(i, 4, k - 9))
                        pe.matmul(proj[k % 2][:, :], W[:, p * P:(p + 1) * P], xT[:, :], start=True,
                                  stop=True).then_inc(s["proj"], 1)
                        k += 1
                for b in range(BATCH):
                    if b < 2:
                        pe.wait_ge(s["gate"], at(i, 4, b + 3))
                    else:
                        pe.wait_ge(s["v"], at(i, 4, b - 1))
                    pe.matmul(proj[b % 2][:, :], xT[:, b * P:(b + 1) * P], WV[:, :], start=True,
                              stop=True).then_inc(s["proj"], 1)

                for p in range(PAIRS):
                    if p == 0:
                        pe.wait_ge(s["phi"], at(i, 8, 8))
                    else:
                        pe.wait_ge(s["kd"], at(i, 4, p))
                    for b in range(BATCH):
                        mm = pe.transpose(turn[:, b * P:(b + 1) * P],
                                          kT[:, p * WIDE + b * P:p * WIDE + (b + 1) * P], ident[:, :])
                    mm.then_inc(s["ktr"], 1)

                def scores(h):
                    p, lo = h // 2, DK * (h % 2)
                    if h >= 2:
                        pe.wait_ge(s["a"], at(i, 8, h - 1))
                    for b in range(BATCH):
                        cols = slice(p * WIDE + b * P, p * WIDE + (b + 1) * P)
                        mm = pe.matmul(score[h % 2][:, b * P:(b + 1) * P], kT[lo:lo + DK, cols], qT[lo:lo + DK, cols],
                                       start=True, stop=True)
                    mm.then_inc(s["score"], 1)

                def values(h):
                    p, lo = h // 2, DK * (h % 2)
                    pe.wait_ge(s["a"], at(i, 8, h + 1))
                    if h % 2 == 0:
                        pe.wait_ge(s["qd"], at(i, 4, p + 1))
                    if h == 0:
                        pe.wait_ge(s["v"], at(i, 4, 4))
                    pe.wait_ge(s["state"], at(i, 4, 1))
                    if h >= 2:
                        pe.wait_ge(s["y"], at(i, 8, h - 1))
                    for b in range(BATCH):
                        cols = slice(p * WIDE + b * P, p * WIDE + (b + 1) * P)
                        o = av[h % 2][:, b * (DK + 1):(b + 1) * (DK + 1)]
                        pe.matmul(o, a[h % 2][:, b * P:(b + 1) * P], v4[:, b, h, :], start=True, stop=False)
                        mm = pe.matmul(o, qd[lo:lo + DK, cols], st4[lo:lo + DK, p, b, :], start=False, stop=True)
                    mm.then_inc(s["av"], 1)

                def new_state(p):
                    if p == 0:
                        pe.wait_ge(s["kd"], at(i, 4, 4))
                    else:
                        pe.wait_ge(s["state"], at(i, 4, 1 + p))
                    for h in (2 * p, 2 * p + 1):
                        lo = DK * (h % 2)
                        for b in range(BATCH):
                            mm = pe.matmul(stp[lo:lo + DK, b * (DK + 1):(b + 1) * (DK + 1)],
                                           kd3[:, b, h * DK:(h + 1) * DK], v4[:, b, h, :], start=True, stop=True)
                    mm.then_inc(s["stp"], 1)

                scores(0)
                scores(1)
                for h in range(HEADS):
                    values(h)
                    if h + 2 < HEADS:
                        scores(h + 2)
                    if h % 2 == 1:
                        new_state(h // 2)

                for p in range(PAIRS):
                    if p % 2 == 0:
                        pe.wait_ge(s["y"], at(i, 8, 8))
                    if p >= 1:
                        pe.wait_ge(s["yT"], at(i, 4, p))
                    for b in range(BATCH):
                        mm = pe.transpose(turn[:, b * P:(b + 1) * P], y3[:, b, p * P:(p + 1) * P], ident[:, :])
                    mm.then_inc(s["ytr"], 1)
                pe.wait_ge(s["yT"], at(i, 4, 4))
                for b in range(BATCH):
                    for p in range(PAIRS):
                        cols = slice(p * WIDE + b * P, p * WIDE + (b + 1) * P)
                        mm = pe.matmul(proj[0][:, b * P:(b + 1) * P], yT[:, cols], WO[:, p * P:(p + 1) * P],
                                       start=(p == 0), stop=(p == PAIRS - 1))
                mm.then_inc(s["out"], 1)
                if not last:
                    token_columns(i + 1)

            pe.wait_ge(s["loaded"], 16 * 13)
            token_columns(0)
            with pe.Fori(0, CHUNKS - 1) as i:
                turn_of(i, False)
            turn_of(CHUNKS - 1, True)

        @block.vector
        def _(dve):
            dve.wait_ge(s["loaded"], 16 * 13)
            dve.tensor_scalar(tmp[:, :], dl[:, :], -1.0, None, ALU.mult).then_inc(s["gmul"], 1)
            dve.wait_ge(s["gmul"], 1)
            dve.tensor_tensor(tmp[:, :], tmp[:, :], dl[:, :], ALU.min).then_inc(s["neg_abs"], 1)
            dve.memset(v1[:, :], 1.0)
            dve.tensor_scalar(half_bg[:, :], bgc[:, :], 0.5, None, ALU.mult).then_inc(s["gmul"], 1)
            dve.memset(state[:, :], 0.0).then_inc(s["state"], 1)
            dve.wait_ge(s["logged"], 1)
            dve.scalar_tensor_tensor(lg[:, :], dl[:, :], 0.0, tmp[:, :], ALU.min, ALU.subtract).then_inc(s["lg_ready"], 1)
            dve.wait_ge(s["tables"], NSETUP)
            m3 = wide(mask[:, :], HEADS)
            dve.tensor_tensor(m3, m3, causal[:, :].unsqueeze(1).to_broadcast([P, HEADS, P]), ALU.mult).then_inc(s["gmul"], 1)

            def normalize(i):
                xc = wide(xs[:, bass.ds(i * WIDE, WIDE)])
                for b in range(BATCH):
                    last = dve.bn_stats(stats[:, 6 * b:6 * b + 6], xc[:, b, :])
                last.then_inc(s["mean_var"], 1)
                dve.wait_ge(s["mean_var"], at(i, 2, 1))
                dve.sem_inc(s["held"], 1)
                for b in range(BATCH):
                    last = dve.bn_aggr(mv[:, 2 * b:2 * b + 2], stats[:, 6 * b:6 * b + 6])
                last.then_inc(s["mean_var"], 1)
                dve.wait_ge(s["mean_var"], at(i, 2, 2))
                dve.tensor_scalar(vpe[:, :], mv[:, 1:2 * BATCH:2], LN_EPS, None, ALU.add).then_inc(s["var_eps"], 1)
                dve.wait_ge(s["rstd"], at(i, 1, 1))
                for b in range(BATCH):
                    last = dve.tensor_scalar(xn[:, b * P:(b + 1) * P], xc[:, b, :], mv[:, 2 * b:2 * b + 1],
                                             rstd[:, b:b + 1], ALU.subtract, ALU.mult)
                last.then_inc(s["xn"], 1)

            def turn_of(i, last):
                for k in range(2 * PAIRS):
                    dst = qT if k < PAIRS else kT
                    p = k % PAIRS
                    dve.wait_ge(s["capped"], at(i, 8, k + 1))
                    dve.scalar_tensor_tensor(dst[:, p * WIDE:(p + 1) * WIDE], proj[k % 2][:, :], 1.0, e1[k % 2][:, :],
                                             ALU.add, ALU.max).then_inc(s["phi"], 1)
                for p in range(PAIRS):
                    dve.wait_ge(s["ktr"], at(i, 4, p + 1))
                    dve.tensor_tensor(kd3[:, :, p * P:(p + 1) * P].rearrange("p b (h j) -> p b h j", h=2),
                                      turn[:, :].rearrange("p (b h j) -> p b h j", b=BATCH, h=2),
                                      kpow[:, 2 * p:2 * p + 2].unsqueeze(1).unsqueeze(3).to_broadcast([P, BATCH, 2, DK]),
                                      ALU.mult).then_inc(s["kd"], 1)

                def masked(h):
                    dve.wait_ge(s["score"], at(i, 8, h + 1))
                    dve.tensor_tensor(wide(a[h % 2][:, :]), wide(score[h % 2][:, :]),
                                      mask[:, h * P:(h + 1) * P].unsqueeze(1).to_broadcast([P, BATCH, P]),
                                      ALU.mult).then_inc(s["a"], 1)

                def divided(h):
                    dve.wait_ge(s["av"], at(i, 8, h + 1))
                    o = av[h % 2][:, 0:BATCH * (DK + 1)].rearrange("p (b j) -> p b j", b=BATCH)
                    dve.tensor_scalar(den[:, :], o[:, :, DK], DEN_EPS, 2.0, ALU.add, ALU.mult).then_inc(s["den"], 1)
                    dve.wait_ge(s["den"], at(i, 8, h + 1))
                    dve.reciprocal(rden[:, :], den[:, :]).then_inc(s["rden"], 1)
                    dve.wait_ge(s["rden"], at(i, 8, h + 1))
                    dve.tensor_tensor(y3[:, :, h * DK:(h + 1) * DK], o[:, :, 0:DK],
                                      rden[:, :].unsqueeze(2).to_broadcast([P, BATCH, DK]), ALU.mult).then_inc(s["y"], 1)

                masked(0)
                masked(1)
                for h in range(HEADS):
                    divided(h)
                    if h + 2 < HEADS:
                        masked(h + 2)
                    if h % 2 == 1:
                        p = h // 2
                        dve.wait_ge(s["stp"], at(i, 4, p + 1))
                        dve.scalar_tensor_tensor(st4[:, p], st4[:, p], gchunk[:, p:p + 1],
                                                 stp[:, 0:BATCH * (DK + 1)].rearrange("p (b j) -> p b j", b=BATCH),
                                                 ALU.mult, ALU.add).then_inc(s["state"], 1)
                if not last:
                    normalize(i + 1)
                for p in range(PAIRS):
                    dve.wait_ge(s["ytr"], at(i, 4, p + 1))
                    dve.scalar_tensor_tensor(yT[:, p * WIDE:(p + 1) * WIDE], gate[:, p * WIDE:(p + 1) * WIDE], 1.0,
                                             turn[:, :], ALU.add, ALU.mult).then_inc(s["yT"], 1)
                dve.wait_ge(s["out"], at(i, 1, 1))
                xc = xs[:, bass.ds(i * WIDE, WIDE)]
                dve.tensor_tensor(xc, proj[0][:, :], xc, ALU.add).then_inc(s["res"], 1)

            dve.sem_inc(s["res"], 1)
            dve.wait_ge(s["x_loaded"], 16 * CHUNKS)
            normalize(0)
            with dve.Fori(0, CHUNKS - 1) as i:
                turn_of(i, False)
            turn_of(CHUNKS - 1, True)


EXPERTS = 8
HID0, HID1 = 256, 512
CAPACITY = int(np.ceil(2 * 1.25 * BATCH * SEQ / EXPERTS))
TILES = BATCH * CHUNKS
BIG = 3.0e38


class Front:

    def __init__(self, S, ident):
        self.ident = ident
        self.stats, self.mv = S.sb("stats", 6 * BATCH), S.sb("mv", 2 * BATCH)
        self.vpe, self.rstd, self.mhalf = S.sb("vpe", BATCH), S.sb("rstd", BATCH), S.sb("mhalf", BATCH)
        self.xn, self.turn = S.sb("xn", WIDE), S.bank("turn")
        self.filled, self.stat, self.var_eps, self.rstd_ready, self.normal, self.turned, self.columns, self.held = (
            S.sem(n) for n in "filled stat var_eps rstd_ready normal turned columns held".split())

    def exponents(self, pool):
        pool.memset(self.mhalf[:, :], -0.5).then_inc(self.filled, 1)
        pool.wait_ge(self.filled, 1)

    def inverse_deviation(self, pool, i):
        pool.wait_ge(self.var_eps, at(i, 1, 1))
        pool.tensor_tensor(self.rstd[:, :], self.vpe[:, :], self.mhalf[:, :], ALU.pow).then_inc(self.rstd_ready, 1)

    def normalize(self, dve, xs, i):
        xc = wide(xs[:, bass.ds(i * WIDE, WIDE)])
        for b in range(BATCH):
            last = dve.bn_stats(self.stats[:, 6 * b:6 * b + 6], xc[:, b, :])
        last.then_inc(self.stat, 1)
        dve.wait_ge(self.stat, at(i, 2, 1))
        dve.sem_inc(self.held, 1)
        for b in range(BATCH):
            last = dve.bn_aggr(self.mv[:, 2 * b:2 * b + 2], self.stats[:, 6 * b:6 * b + 6])
        last.then_inc(self.stat, 1)
        dve.wait_ge(self.stat, at(i, 2, 2))
        dve.tensor_scalar(self.vpe[:, :], self.mv[:, 1:2 * BATCH:2], LN_EPS, None, ALU.add).then_inc(self.var_eps, 1)
        dve.wait_ge(self.rstd_ready, at(i, 1, 1))
        for b in range(BATCH):
            last = dve.tensor_scalar(self.xn[:, b * P:(b + 1) * P], xc[:, b, :], self.mv[:, 2 * b:2 * b + 1],
                                     self.rstd[:, b:b + 1], ALU.subtract, ALU.mult)
        last.then_inc(self.normal, 1)

    def transpose(self, pe, i):
        pe.wait_ge(self.normal, at(i, 1, 1))
        for b in range(BATCH):
            mm = pe.transpose(self.turn[:, b * P:(b + 1) * P], self.xn[:, b * P:(b + 1) * P], self.ident[:, :])
        mm.then_inc(self.turned, 1)


def first_largest(dve, values, rank, best, eq, mask, chain):
    by_expert = lambda t: t.rearrange("p e n -> p n e")
    spread = lambda t: t.unsqueeze(1).to_broadcast([P, EXPERTS, TILES])
    chain(dve.tensor_reduce(best, by_expert(values), AX.X, ALU.max))
    chain(dve.tensor_tensor(eq, values, spread(best), ALU.is_equal))
    chain(dve.tensor_tensor(eq, eq, rank, ALU.mult))
    chain(dve.tensor_reduce(best, by_expert(eq), AX.X, ALU.max))
    chain(dve.tensor_tensor(mask, eq, spread(best), ALU.is_equal))


def mixture_phase(nc, xs, name, hidden, act_fn, capacity, router, w1, w2, ident_d, rank_d, b1=None, b2=None,
                  before_d=None, restart_d=None):
    with ExitStack() as ctx:
        S = Scope(nc, ctx, name)
        biased = b1 is not None
        nexp = EXPERTS + 1 if biased else EXPERTS
        HB = hidden // P
        ident, rank = S.sb("ident", P), S.sb("rank", EXPERTS * TILES)
        R = S.sb("router", EXPERTS)
        W1, W2 = S.sb("W1", nexp * hidden), S.sb("W2", nexp * HB * P)
        XT = S.sb("XT", CHUNKS * WIDE)
        NE = EXPERTS * TILES
        logits, eq, rest = S.sb("logits", NE), S.sb("eq", NE), S.sb("rest", NE)
        masks, gates = S.sb("masks", 2 * NE), S.sb("gates", NE)
        best, second, w_a, w_b = (S.sb(n, TILES) for n in ("best", "second", "w_a", "w_b"))
        hT = [S.sb(f"hT{k}", HB * WIDE) for k in range(2)]
        gcol = S.sb("gcol", BATCH * nexp)
        front = Front(S, ident)
        small = S.bank("small")
        hid = [S.bank(f"hid{k}") for k in range(4)]
        outp = [S.bank(f"outp{k}") for k in range(2)]
        s = {n: S.sem(n) for n in "loaded lg_mm lg_out chain expd summed recip prefix gcol hid act outp acc gT gTs bias bias_in".split()}
        if biased:
            B1, B2 = S.sb("B1", nexp * HB), S.sb("B2", P, nexp)
            before, restart = S.sb("before", P), S.sb("restart", 2 * NE)
            ones = S.sb("ones", P)
            incl, pos = S.sb("incl", 2 * NE), S.sb("pos", 2 * NE)
            gT = S.sb("gT", WIDE, nexp)
        loads = [(ident, ident_d), (rank, rank_d), (R, router)]
        late = [(W1, w1), (W2, w2)]
        if biased:
            loads += [(before, before_d), (restart, restart_d)]
            late += [(B1, b1), (B2, b2)]
        late_in = S.sem("late_in")

        by_tile = lambda t: t.rearrange("p (e n) -> p e n", e=EXPERTS)
        by_chunk = lambda t: t.rearrange("p (e b c) -> p b e c", e=EXPERTS, b=BATCH)
        g3 = gcol[:, :].rearrange("p (b e) -> p b e", b=BATCH)

        block = ctx.enter_context(nc.Block())

        @block.sync
        def _(sp):
            for dst, src in loads:
                sp.dma_start(dst[:, :], src).then_inc(s["loaded"], 16)
            for dst, src in late:
                sp.dma_start(dst[:, :], src).then_inc(late_in, 16)

        @block.gpsimd
        def _(pool):
            front.exponents(pool)
            with pool.Fori(0, CHUNKS) as i:
                front.inverse_deviation(pool, i)

        @block.tensor
        def _(pe):
            pe.wait_ge(s["loaded"], 16 * len(loads))
            with pe.Fori(0, CHUNKS) as i:
                front.transpose(pe, i)
                pe.wait_ge(front.columns, at(i, 1, 1))
                pe.wait_ge(s["lg_out"], at(i, 1, 1))
                for b in range(BATCH):
                    mm = pe.matmul(small[:, b * EXPERTS:(b + 1) * EXPERTS], hT[0][:, b * P:(b + 1) * P], R[:, :],
                                   start=True, stop=True)
                mm.then_inc(s["lg_mm"], 1)
            pe.wait_ge(late_in, 16 * len(late))
            if biased:
                pe.wait_ge(s["prefix"], 1)
                pe.matmul(hid[0][:, :], before[:, :], masks[:, :], start=True, stop=True)
                pe.matmul(hid[1][:, :], ones[:, :], masks[:, :], start=True, stop=True).then_inc(s["hid"], 1)
            base = 1 if biased else 0

            with pe.Fori(0, CHUNKS) as i:
                def hidden_of(e):
                    for m in range(HB):
                        k = e * HB + m
                        pe.wait_ge(s["act"], at(i, nexp * HB, k + 1))
                        pe.matmul(hid[k % 4][:, :], W1[:, (e * HB + m) * P:(e * HB + m + 1) * P],
                                  XT[:, bass.ds(i * WIDE, WIDE)], start=True, stop=True).then_inc(s["hid"], 1)

                def output_of(e):
                    pe.wait_ge(s["act"], at(i, nexp * HB, 4 + (e + 1) * HB))
                    pe.wait_ge(s["acc"], at(i, nexp, e + 1))
                    for b in range(BATCH):
                        for m in range(HB):
                            mm = pe.matmul(outp[e % 2][:, b * P:(b + 1) * P],
                                           hT[e % 2][:, m * WIDE + b * P:m * WIDE + (b + 1) * P],
                                           W2[:, (e * HB + m) * P:(e * HB + m + 1) * P],
                                           start=(m == 0), stop=(m == HB - 1))
                    mm.then_inc(s["outp"], 1)

                hidden_of(0)
                if biased:
                    pe.wait_ge(s["gcol"], at(i, 1, 1))
                    for b in range(BATCH):
                        mm = pe.transpose(front.turn[0:nexp, b * P:(b + 1) * P], g3[:, b, :], ident[:, :])
                    mm.then_inc(s["gT"], 1)
                for e in range(1, nexp):
                    hidden_of(e)
                    output_of(e - 1)
                if biased:
                    pe.wait_ge(s["gTs"], at(i, 1, 1))
                    pe.wait_ge(s["bias_in"], at(i, 1, 1))
                    for b in range(BATCH):
                        mm = pe.matmul(small[:, b * P:(b + 1) * P], gT[:, b * P:(b + 1) * P], B2[:, :],
                                       start=True, stop=True)
                    mm.then_inc(s["bias"], 1)
                output_of(nexp - 1)

        @block.scalar
        def _(act):
            with act.Fori(0, CHUNKS) as i:
                act.wait_ge(front.turned, at(i, 1, 1))
                act.activation(XT[:, bass.ds(i * WIDE, WIDE)], front.turn[:, :], ACT.Copy)
                act.wait_ge(s["lg_out"], at(i, 1, 1))
                act.activation(hT[0][:, 0:WIDE], front.turn[:, :], ACT.Copy).then_inc(front.columns, 1)
            act.wait_ge(s["expd"], 1)
            if biased:
                act.activation(logits[:, :], logits[:, :], ACT.Exp).then_inc(s["recip"], 1)
            else:
                act.activation(w_b[:, :], w_b[:, :], ACT.Exp).then_inc(s["recip"], 1)
            base = 1 if biased else 0
            act.wait_ge(s["gcol"], 1)
            act.sem_inc(s["act"], 4)
            with act.Fori(0, CHUNKS) as i:
                for e in range(nexp):
                    for m in range(HB):
                        k = e * HB + m
                        act.wait_ge(s["hid"], at(i, nexp * HB, base + k + 1))
                        if m == 0:
                            act.wait_ge(s["acc"], at(i, nexp, e + 1))
                        act.activation(hT[e % 2][:, m * WIDE:(m + 1) * WIDE], hid[k % 4][:, :], act_fn,
                                       **({"bias": B1[:, k:k + 1]} if biased else {})).then_inc(s["act"], 1)
                    if biased and e == 0:
                        act.wait_ge(s["gT"], at(i, 1, 1))
                        act.activation(gT[:, :], front.turn[0:nexp, :], ACT.Copy).then_inc(s["gTs"], 1)

        @block.vector
        def _(dve):
            count = [0]

            def chain(ins):
                count[0] += 1
                ins.then_inc(s["chain"], 1)
                dve.wait_ge(s["chain"], count[0])

            dve.sem_inc(s["lg_out"], 1)
            with dve.Fori(0, CHUNKS) as i:
                front.normalize(dve, xs, i)
                dve.wait_ge(s["lg_mm"], at(i, 1, 1))
                dve.tensor_copy(by_chunk(logits[:, :])[:, :, :, bass.ds(i, 1)],
                                small[:, 0:BATCH * EXPERTS].rearrange("p (b e c) -> p b e c", b=BATCH, c=1)
                                ).then_inc(s["lg_out"], 1)
            dve.wait_ge(s["loaded"], 16 * len(loads))
            dve.wait_ge(s["lg_out"], CHUNKS + 1)
            L, EQ, RK = by_tile(logits[:, :]), by_tile(eq[:, :]), by_tile(rank[:, :])
            M1, M2 = by_tile(masks[:, 0:NE]), by_tile(masks[:, NE:])
            RS, G = by_tile(rest[:, :]), by_tile(gates[:, :])
            experts_inside = lambda t: t.rearrange("p e n -> p n e")
            spread = lambda t: t[:, :].unsqueeze(1).to_broadcast([P, EXPERTS, TILES])
            if not biased:
                first_largest(dve, L, RK, best[:, :], EQ, M1, chain)
                chain(dve.scalar_tensor_tensor(RS, M1, -BIG, L, ALU.mult, ALU.add))
                first_largest(dve, RS, RK, second[:, :], EQ, M2, chain)
                chain(dve.tensor_reduce(best[:, :], experts_inside(L), AX.X, ALU.max))
                chain(dve.tensor_reduce(second[:, :], experts_inside(RS), AX.X, ALU.max))
                dve.tensor_tensor(w_b[:, :], second[:, :], best[:, :], ALU.subtract).then_inc(s["expd"], 1)
                dve.wait_ge(s["recip"], 1)
                chain(dve.tensor_scalar(w_a[:, :], w_b[:, :], 1.0, None, ALU.add))
                chain(dve.reciprocal(w_a[:, :], w_a[:, :]))
                chain(dve.tensor_tensor(w_b[:, :], w_a[:, :], w_b[:, :], ALU.mult))
            else:
                chain(dve.memset(ones[:, :], 1.0))
                chain(dve.tensor_reduce(best[:, :], experts_inside(L), AX.X, ALU.max))
                dve.tensor_tensor(L, L, spread(best), ALU.subtract).then_inc(s["expd"], 1)
                dve.wait_ge(s["recip"], 1)
                chain(dve.tensor_reduce(w_a[:, :], experts_inside(L), AX.X, ALU.add))
                chain(dve.reciprocal(w_a[:, :], w_a[:, :]))
                chain(dve.tensor_tensor(L, L, spread(w_a), ALU.mult))
                first_largest(dve, L, RK, best[:, :], EQ, M1, chain)
                chain(dve.tensor_tensor(RS, L, M1, ALU.mult))
                chain(dve.tensor_tensor(RS, L, RS, ALU.subtract))
                first_largest(dve, RS, RK, second[:, :], EQ, M2, chain)
                dve.sem_inc(s["prefix"], 1)
                dve.wait_ge(s["hid"], 1)
                chain(dve.tensor_tensor_scan(incl[:, :], restart[:, :], hid[1][:, :], 0.0, ALU.mult, ALU.add))
                chain(dve.tensor_tensor(pos[:, :], incl[:, :], hid[1][:, :], ALU.subtract))
                chain(dve.tensor_tensor(pos[:, :], pos[:, :], hid[0][:, :], ALU.add))
                taken = eq[:, 0:EXPERTS]
                chain(dve.tensor_scalar(taken, incl[:, TILES - 1:NE:TILES], float(capacity), None, ALU.min))
                P2 = by_tile(pos[:, NE:])
                chain(dve.tensor_tensor(P2, P2, taken.unsqueeze(2).to_broadcast([P, EXPERTS, TILES]), ALU.add))
                chain(dve.scalar_tensor_tensor(masks[:, :], pos[:, :], float(capacity), masks[:, :], ALU.is_lt, ALU.mult))
                chain(dve.tensor_tensor(RS, L, M1, ALU.mult))
                chain(dve.tensor_reduce(w_a[:, :], experts_inside(RS), AX.X, ALU.add))
                chain(dve.tensor_tensor(RS, L, M2, ALU.mult))
                chain(dve.tensor_reduce(w_b[:, :], experts_inside(RS), AX.X, ALU.add))
                chain(dve.tensor_tensor(best[:, :], w_a[:, :], w_b[:, :], ALU.add))
                chain(dve.tensor_scalar(best[:, :], best[:, :], float(np.finfo(np.float32).eps), None, ALU.max))
                chain(dve.reciprocal(best[:, :], best[:, :]))
                chain(dve.tensor_tensor(w_a[:, :], w_a[:, :], best[:, :], ALU.mult))
                chain(dve.tensor_tensor(w_b[:, :], w_b[:, :], best[:, :], ALU.mult))
                chain(dve.memset(gcol[:, :], 0.1))
            chain(dve.tensor_tensor(G, M1, spread(w_a), ALU.mult))
            chain(dve.tensor_tensor(RS, M2, spread(w_b), ALU.mult))
            chain(dve.tensor_tensor(G, G, RS, ALU.add))
            dve.sem_inc(s["acc"], 2)
            dve.sem_inc(s["bias_in"], 1)

            with dve.Fori(0, CHUNKS) as i:
                dve.wait_ge(s["acc"], at(i, nexp, 2))
                dve.tensor_copy(g3[:, :, 0:EXPERTS].unsqueeze(3), by_chunk(gates[:, :])[:, :, :, bass.ds(i, 1)]
                                ).then_inc(s["gcol"], 1)
                dve.wait_ge(s["gcol"], at(i, 1, 1))
                for e in range(nexp):
                    dve.wait_ge(s["outp"], at(i, nexp, e + 1))
                    dve.wait_ge(s["acc"], at(i, nexp, e + 2))
                    for b in range(BATCH):
                        xb = xs[:, bass.ds(i * WIDE + b * P, P)]
                        last = dve.scalar_tensor_tensor(xb, outp[e % 2][:, b * P:(b + 1) * P],
                                                        gcol[:, b * nexp + e:b * nexp + e + 1], xb, ALU.mult, ALU.add)
                    last.then_inc(s["acc"], 1)
                if biased:
                    dve.wait_ge(s["bias"], at(i, 1, 1))
                    dve.wait_ge(s["acc"], at(i, nexp, nexp + 2))
                    xc = xs[:, bass.ds(i * WIDE, WIDE)]
                    dve.tensor_tensor(xc, small[:, :], xc, ALU.add).then_inc(s["bias_in"], 1)


D_IN, STATES, TAPS = 256, 16, 4
POS = 16
GC = P // POS
GROUPS = D_IN // GC
HALVES = D_IN // P
SUPER = 4
SUPERS = SEQ // (SUPER * POS)
COLS = BATCH * SUPERS
LEVELS = 6
RMS_EPS = 1e-6


def state_space_phase(nc, xs, scratch, norm_w, win, b_in, conv_w, conv_b, a_rows_c, a_cols_b, wout, b_out,
                      ident_d, own_d):
    with ExitStack() as ctx:
        S = Scope(nc, ctx, "ssm")
        PAD = TAPS - 1
        ident, own = S.sb("ident", P), S.sb("own", GC)
        NW, WIN, BIN = S.sb("NW", 1), S.sb("WIN", D_IN), S.sb("BIN", HALVES)
        CW, CB, WOUT, BOUT = S.sb("CW", HALVES * TAPS), S.sb("CB", HALVES), S.sb("WOUT", HALVES * D), S.sb("BOUT", D)
        RB, RC = S.sb("RB", GROUPS * (16 + 64)), S.sb("RC", GROUPS * (16 + 65))
        big_a, big_b = S.sb("big_a", HALVES * BATCH * (SEQ + PAD)), S.sb("big_b", HALVES * BATCH * SEQ)
        turn_buf = S.sb("turn_buf", 2 * GROUPS * P)
        diag = S.sb("diag", GROUPS * P)
        TW = S.sb("TW", GROUPS * SUPER * POS)
        H = S.sb("H", GROUPS * BATCH * (SUPERS + 1))
        b_own = S.sb("b_own", GROUPS * GC)
        gsb = S.sb("gsb", GROUPS * (POS - 1 + 64), GC)
        hn, hT = S.sb("hn", WIDE), S.sb("hT", WIDE)
        msq, r2 = S.sb("msq", BATCH), S.sb("r2", BATCH)
        front = Front(S, ident)
        pb = [S.bank(f"pb{k}") for k in range(7)] + [front.turn]

        u = big_a[:, :].rearrange("p (h b t) -> p h b t", h=HALVES, b=BATCH)
        u2 = big_a[:, 0:GROUPS * 256].rearrange("p (g c) -> p g c", g=GROUPS)
        yT = big_a[:, 0:HALVES * BATCH * SEQ].rearrange("p (h t) -> p h t", h=HALVES)
        v = big_b[:, :].rearrange("p (h b t) -> p h b t", h=HALVES, b=BATCH)
        ys = big_b[:, :].rearrange("p (g c) -> p g c", g=GROUPS)
        diagT = turn_buf[:, 0:GROUPS * P]
        tb = [turn_buf[:, k * GROUPS * P:(k + 1) * GROUPS * P] for k in range(2)]
        expB, weightX, expO, expT = ([turn_buf[:, (2 * n + k) * 512:(2 * n + k + 1) * 512] for k in range(2)]
                                     for n in range(4))
        rb = RB[:, :].rearrange("p (g n) -> p g n", g=GROUPS)
        rc = RC[:, :].rearrange("p (g n) -> p g n", g=GROUPS)
        h4 = H[:, :].rearrange("p (g b s) -> p g b s", g=GROUPS, b=BATCH)
        tw = TW[:, :].rearrange("p (g n) -> p g n", g=GROUPS)
        g3 = gsb[:, :].rearrange("p (g n) -> p g n", g=GROUPS)

        loads = [(ident[:, :], ident_d), (own[:, :], own_d), (rb[:, :, 0:17], a_cols_b),
                 (rc[:, :, 0:17], a_rows_c), (NW[:, :], norm_w), (WIN[:, :], win),
                 (BIN[:, :], b_in), (CW[:, :], conv_w), (CB[:, :], conv_b), (WOUT[:, :], wout), (BOUT[:, :], b_out)]
        s = {n: S.sem(n) for n in ("loaded diag diagT lev_mm lev_out own g_mm g_out g_saved windows zeroed msq r2 hn hT "
                                   "u_mm u v0 conv1 conv2 conv3 kept t1 t1_out t2 t2_out expB xT xW x_mm x_out rec rec_out "
                                   "expO expT y_mm y_out t3 t3_out t4 t4_out w_mm w_out").split()}

        def own_block(n):
            return own[:, :].unsqueeze(1).unsqueeze(3).to_broadcast([P, n, GC, 16])

        def expanded(ap):
            return ap.unsqueeze(2).to_broadcast([P, ap.shape[1], GC, 16])

        def channel_form(ap, n):
            return ap.rearrange("p (n d s) -> p n d s", n=n, d=GC)

        block = ctx.enter_context(nc.Block())
        Q = 8

        @block.sync
        def _(sp):
            for dst, src in loads:
                sp.dma_start(dst, src).then_inc(s["loaded"], 16)
            sp.wait_ge(s["g_out"], 4)
            width = POS - 1 + 64
            sp.dma_start(scratch.rearrange("(d g n) -> d g n", d=GC, g=GROUPS), g3).then_inc(s["g_saved"], 16)
            sp.wait_ge(s["g_saved"], 16)
            for d in range(GC):
                window = bass.AP(tensor=scratch.tensor, offset=scratch.offset + d * GROUPS * width,
                                 ap=[[1, POS], [width, GROUPS], [1, 64]])
                sp.dma_start(tw[d * POS:(d + 1) * POS, :, :], window).then_inc(s["windows"], 16)

        @block.gpsimd
        def _(pool):
            front.exponents(pool)
            pool.wait_ge(s["loaded"], 16 * len(loads))
            for k in range(LEVELS):
                for q in range(4):
                    if k:
                        pool.wait_ge(s["lev_out"], 4 + 8 * (k - 1) + 2 * q + 2)
                    gs = slice(q * Q, (q + 1) * Q)
                    pool.tensor_tensor(channel_form(diagT[:, q * Q * P:(q + 1) * Q * P], Q), expanded(rb[:, gs, 0:16]),
                                       own_block(Q), ALU.mult).then_inc(s["diagT"], 1)
            with pool.Fori(0, CHUNKS) as i:
                front.inverse_deviation(pool, i)
                pool.wait_ge(s["msq"], at(i, 3, 3))
                pool.tensor_tensor(r2[:, :], msq[:, :], front.mhalf[:, :], ALU.pow).then_inc(s["r2"], 1)
                xc = xs[:, bass.ds(i * WIDE, WIDE)]
                pool.wait_ge(front.normal, at(i, 1, 1))
                pool.sem_inc(front.held, 1)
                pool.tensor_tensor(xc, xc, front.xn[:, :], ALU.add).then_inc(s["kept"], 1)
                pool.wait_ge(s["kept"], at(i, 2, 1))
                pool.sem_inc(front.held, 1)
                pool.tensor_tensor(wide(xc), wide(xc), BOUT[:, :].unsqueeze(1).to_broadcast([P, BATCH, D]),
                                   ALU.add).then_inc(s["kept"], 1)
            pool.wait_ge(s["windows"], 16 * GC)
            with pool.Fori(0, GROUPS // 2) as i:
                for k in range(2):
                    pool.wait_ge(s["y_mm"], at(i, 2, k + 1))
                    pool.sem_inc(front.held, 1)
                    pool.tensor_tensor(channel_form(expT[k], SUPER),
                                       expanded(TW[:, bass.ds(i * 128 + k * 64, 64)].rearrange("p (n s) -> p n s", n=SUPER)),
                                       own_block(SUPER), ALU.mult).then_inc(s["expT"], 1)

        @block.tensor
        def _(pe):
            pe.wait_ge(s["loaded"], 16 * len(loads))
            for q in range(4):
                pe.wait_ge(s["diagT"], q + 1)
                for g in range(q * Q, (q + 1) * Q):
                    mm = pe.matmul(pb[q][:, g % Q:g % Q + 1], diagT[:, g * P:(g + 1) * P], rc[:, g, 16:17],
                                   start=True, stop=True)
                mm.then_inc(s["lev_mm"], 1)
            for k in range(LEVELS):
                n = 2 ** k
                for q in range(4):
                    pe.wait_ge(s["diag"], 4 * k + q + 1)
                    if k == 0:
                        pe.wait_ge(s["lev_out"], q + 1)
                    for g in range(q * Q, (q + 1) * Q):
                        mm = pe.matmul(pb[q][:, (g % Q) * (16 + n):(g % Q + 1) * (16 + n)], diag[:, g * P:(g + 1) * P],
                                       rb[:, g, 0:16 + n], start=True, stop=True)
                    mm.then_inc(s["lev_mm"], 1)
                    pe.wait_ge(s["diagT"], 4 * k + q + 1)
                    for g in range(q * Q, (q + 1) * Q):
                        o = pb[4 + q][:, (g % Q) * (16 + n):(g % Q + 1) * (16 + n)]
                        pe.matmul(o[:, 0:16], diagT[:, g * P:(g + 1) * P], rc[:, g, 0:16], start=True, stop=True)
                        mm = pe.matmul(o[:, 16:16 + n], diagT[:, g * P:(g + 1) * P], rc[:, g, 17:17 + n],
                                       start=True, stop=True)
                    mm.then_inc(s["lev_mm"], 1)
            pe.wait_ge(s["own"], 1)
            for q in range(4):
                pe.wait_ge(s["lev_out"], 4 + 8 * LEVELS)
                for g in range(q * Q, (q + 1) * Q):
                    mm = pe.matmul(pb[q][0:GC, (g % Q) * 64:(g % Q + 1) * 64], b_own[:, g * GC:(g + 1) * GC],
                                   rc[:, g, 16:80], start=True, stop=True)
                mm.then_inc(s["g_mm"], 1)

            pe.wait_ge(s["g_out"], 4)
            with pe.Fori(0, CHUNKS) as i:
                pe.wait_ge(s["hn"], at(i, 1, 1))
                for b in range(BATCH):
                    mm = pe.transpose(front.turn[:, b * P:(b + 1) * P], hn[:, b * P:(b + 1) * P], ident[:, :])
                mm.then_inc(front.turned, 1)
                pe.wait_ge(s["hT"], at(i, 1, 1))
                for h in range(HALVES):
                    pe.matmul(pb[h][:, :], WIN[:, h * P:(h + 1) * P], hT[:, :], start=True,
                              stop=True).then_inc(s["u_mm"], 1)

            pe.wait_ge(s["conv3"], HALVES * CHUNKS)
            v_blocks = big_b[:, :].rearrange("p (h c j) -> p h j c", h=HALVES, j=POS)
            n1 = n2 = 0
            for mh in range(2):
                for h in range(HALVES):
                    for jq in range(4):
                        if n1 >= 4:
                            pe.wait_ge(s["t1_out"], n1 - 3)
                        for k in range(4):
                            mm = pe.transpose(pb[n1 % 4][:, k * P:(k + 1) * P],
                                              v_blocks[:, h, 4 * jq + 3 - k, mh * P:(mh + 1) * P], ident[:, :])
                        mm.then_inc(s["t1"], 1)
                        n1 += 1
            for mh in range(2):
                for gq in range(GROUPS // 4):
                    pe.wait_ge(s["t1_out"], 8 * (mh + 1))
                    if n2 >= 4:
                        pe.wait_ge(s["t2_out"], n2 - 3)
                    for k in range(4):
                        g = 4 * gq + k
                        mm = pe.transpose(pb[4 + n2 % 4][:, k * P:(k + 1) * P], tb[mh][:, g * P:(g + 1) * P], ident[:, :])
                    mm.then_inc(s["t2"], 1)
                    n2 += 1

            pe.wait_ge(s["t2_out"], n2)
            with pe.Fori(0, GROUPS // 2) as i:
                for k in range(2):
                    pe.wait_ge(s["expB"], at(i, 2, k + 1))
                    pe.wait_ge(s["xW"], at(i, 2, k + 1))
                    for m in range(SUPER):
                        mm = pe.transpose(pb[k][:, m * P:(m + 1) * P], expB[k][:, m * P:(m + 1) * P], ident[:, :])
                    mm.then_inc(s["xT"], 1)
                for k in range(2):
                    pe.wait_ge(s["xW"], at(i, 2, k + 3))
                    pe.wait_ge(s["x_out"], at(i, 2, k + 1))
                    for m in range(SUPER):
                        r = SUPER - 1 - m
                        mm = pe.matmul(pb[2 + k][:, 0:COLS], weightX[k][:, r * P:(r + 1) * P],
                                       big_a[:, bass.ds(i * 512 + k * 256 + m * COLS, COLS)],
                                       start=(m == 0), stop=(m == SUPER - 1))
                    mm.then_inc(s["x_mm"], 1)

            pe.wait_ge(s["x_out"], GROUPS + 2)
            with pe.Fori(0, SUPERS - 2) as i:
                pe.wait_ge(s["rec_out"], at(i, 1, 1))
                for g in range(GROUPS):
                    mm = pe.matmul(pb[4][:, g * BATCH:(g + 1) * BATCH], diag[:, g * P:(g + 1) * P],
                                   h4[:, g, :, bass.ds(i + 1, 1)].rearrange("p b s -> p (b s)"), start=True, stop=True)
                mm.then_inc(s["rec"], 1)

            pe.wait_ge(s["rec_out"], SUPERS - 1)
            with pe.Fori(0, GROUPS // 2) as i:
                for k in range(2):
                    pe.wait_ge(s["expT"], at(i, 2, k + 1))
                    pe.wait_ge(s["y_out"], at(i, 2, k + 1))
                    for m in range(SUPER):
                        n = (SUPER - m) * COLS
                        pe.matmul(pb[k][:, m * COLS:SUPER * COLS], expT[k][:, m * P:(m + 1) * P],
                                  big_a[:, bass.ds(i * 512 + k * 256, n)], start=(m == 0), stop=False,
                                  skip_group_check=True)
                    pe.wait_ge(s["expO"], at(i, 2, k + 1))
                    for m in range(SUPER):
                        mm = pe.matmul(pb[k][:, m * COLS:(m + 1) * COLS], expO[k][:, m * P:(m + 1) * P],
                                       h4[:, bass.ds(i * 2 + k, 1), :, 0:SUPERS].rearrange("p g b s -> p (g b) s"),
                                       start=False, stop=(m == SUPER - 1), skip_group_check=True)
                    mm.then_inc(s["y_mm"], 1)

            pe.wait_ge(s["y_out"], GROUPS + 2)
            n3 = n4 = 0
            for mh in range(2):
                for gq in range(GROUPS // 4):
                    if n3 >= 4:
                        pe.wait_ge(s["t3_out"], n3 - 3)
                    for k in range(4):
                        mm = pe.transpose(pb[n3 % 4][:, k * P:(k + 1) * P],
                                          ys[:, 4 * gq + k, mh * P:(mh + 1) * P], ident[:, :])
                    mm.then_inc(s["t3"], 1)
                    n3 += 1
            for mh in range(2):
                rows = tb[mh].rearrange("p (h d j) -> p h j d", h=HALVES, j=POS)
                pe.wait_ge(s["t3_out"], 8 * (mh + 1))
                for h in range(HALVES):
                    for jq in range(4):
                        if n4 >= 4:
                            pe.wait_ge(s["t4_out"], n4 - 3)
                        for k in range(4):
                            mm = pe.transpose(pb[4 + n4 % 4][:, k * P:(k + 1) * P], rows[:, h, 4 * jq + k, :], ident[:, :])
                        mm.then_inc(s["t4"], 1)
                        n4 += 1
            pe.wait_ge(s["t4_out"], n4)
            for c in range(CHUNKS):
                if c >= 2:
                    pe.wait_ge(s["w_out"], c - 1)
                for b in range(BATCH):
                    t0 = b * SEQ + c * P
                    for h in range(HALVES):
                        mm = pe.matmul(pb[c % 2][:, b * P:(b + 1) * P], yT[:, h, t0:t0 + P],
                                       WOUT[:, h * D:(h + 1) * D], start=(h == 0), stop=(h == HALVES - 1))
                mm.then_inc(s["w_mm"], 1)

        @block.scalar
        def _(act):
            for q in range(4):
                act.wait_ge(s["lev_mm"], q + 1)
                act.activation(rc[:, q * Q:(q + 1) * Q, 17:18], pb[q][:, 0:Q].unsqueeze(2), ACT.Copy).then_inc(s["lev_out"], 1)
            for k in range(LEVELS):
                n = 2 ** k
                for q in range(4):
                    gs = slice(q * Q, (q + 1) * Q)
                    for side, (dst, first, bank) in enumerate(((rb, 16 + n, pb[q]), (rc, 17 + n, pb[4 + q]))):
                        act.wait_ge(s["lev_mm"], 4 + 8 * k + 2 * q + side + 1)
                        if side == 0:
                            act.wait_ge(s["diagT"], 4 * k + q + 1)
                        else:
                            act.wait_ge(s["diag"], 4 * k + q + 1)
                        src = bank[:, 0:Q * (16 + n)].rearrange("p (g n) -> p g n", g=Q)
                        act.activation(dst[:, gs, 0:16], src[:, :, 0:16], ACT.Copy)
                        act.activation(dst[:, gs, first:first + n], src[:, :, 16:], ACT.Copy).then_inc(s["lev_out"], 1)
            act.wait_ge(s["zeroed"], 3)
            for q in range(4):
                act.wait_ge(s["g_mm"], q + 1)
                act.activation(g3[:, q * Q:(q + 1) * Q, POS - 1:],
                               pb[q][0:GC, :].rearrange("p (g n) -> p g n", g=Q), ACT.Copy).then_inc(s["g_out"], 1)

            with act.Fori(0, CHUNKS) as i:
                act.wait_ge(front.turned, at(i, 1, 1))
                act.activation(hT[:, :], front.turn[:, :], ACT.Copy, scale=NW[:, 0:1]).then_inc(s["hT"], 1)
                for h in range(HALVES):
                    act.wait_ge(s["u_mm"], at(i, 2, h + 1))
                    act.activation(u[:, h, :, bass.ds(i * P + PAD, P)], wide(pb[h][:, :]), ACT.Identity,
                                   bias=BIN[:, h:h + 1]).then_inc(s["u"], 1)
                for h in range(HALVES):
                    act.wait_ge(s["u"], at(i, 2, h + 1))
                    act.activation(v[:, h, :, bass.ds(i * P, P)], u[:, h, :, bass.ds(i * P + PAD, P)], ACT.Identity,
                                   bias=CB[:, h:h + 1], scale=CW[:, h * TAPS + PAD:h * TAPS + PAD + 1]
                                   ).then_inc(s["v0"], 1)

            n1 = n2 = 0
            for mh in range(2):
                for h in range(HALVES):
                    for jq in range(4):
                        act.wait_ge(s["t1"], n1 + 1)
                        dst = tb[mh].rearrange("p (h d j) -> p h j d", h=HALVES, j=POS)[:, h, 12 - 4 * jq:16 - 4 * jq, :]
                        act.activation(dst, wide(pb[n1 % 4][:, :], 4), ACT.Copy).then_inc(s["t1_out"], 1)
                        n1 += 1

            act.sem_inc(s["xW"], 2)
            with act.Fori(0, GROUPS // 2) as i:
                for k in range(2):
                    act.wait_ge(s["xT"], at(i, 2, k + 3))
                    act.wait_ge(s["x_mm"], at(i, 2, k + 1))
                    act.activation(weightX[k], pb[k][:, :], ACT.Copy).then_inc(s["xW"], 1)
            act.sem_inc(s["y_out"], 2)
            with act.Fori(0, GROUPS // 2) as i:
                for k in range(2):
                    act.wait_ge(s["y_mm"], at(i, 2, k + 3))
                    act.activation(big_b[:, bass.ds(i * 512 + k * 256, 256)].rearrange("p (c m) -> p m c", m=SUPER),
                                   pb[k][:, 0:256].rearrange("p (m c) -> p m c", m=SUPER), ACT.Copy
                                   ).then_inc(s["y_out"], 1)
            n3 = n4 = 0
            for mh in range(2):
                for h in range(HALVES):
                    for jq in range(4):
                        act.wait_ge(s["t4"], n4 + 1)
                        dst = yT[:, h, :].rearrange("p (c j) -> p j c", j=POS)[
                            :, 4 * jq:4 * jq + 4, mh * P:(mh + 1) * P]
                        act.activation(dst, wide(pb[4 + n4 % 4][:, :], 4), ACT.Copy
                                       ).then_inc(s["t4_out"], 1)
                        n4 += 1

        @block.vector
        def _(dve):
            dve.memset(gsb[:, :], 0.0).then_inc(s["zeroed"], 1)
            dve.memset(H[:, :], 0.0).then_inc(s["zeroed"], 1)
            dve.memset(u[:, :, :, 0:PAD], 0.0).then_inc(s["zeroed"], 1)
            dve.wait_ge(s["loaded"], 16 * len(loads))
            dve.tensor_tensor(b_own[:, :].rearrange("p (g d) -> p g d", g=GROUPS),
                              rb[:, :, 16:17].to_broadcast([P, GROUPS, GC]),
                              own[:, :].unsqueeze(1).to_broadcast([P, GROUPS, GC]), ALU.mult).then_inc(s["own"], 1)
            for k in range(LEVELS + 1):
                for q in range(4):
                    if k:
                        dve.wait_ge(s["lev_out"], 4 + 8 * (k - 1) + 2 * q + 2)
                    gs = slice(q * Q, (q + 1) * Q)
                    dve.tensor_tensor(channel_form(diag[:, q * Q * P:(q + 1) * Q * P], Q), expanded(rc[:, gs, 0:16]),
                                      own_block(Q), ALU.mult).then_inc(s["diag"], 1)

            with dve.Fori(0, CHUNKS) as i:
                front.normalize(dve, xs, i)
                dve.tensor_tensor(msq[:, :], front.mv[:, 1:2 * BATCH:2], front.rstd[:, :], ALU.mult).then_inc(s["msq"], 1)
                dve.wait_ge(s["msq"], at(i, 3, 1))
                dve.tensor_tensor(msq[:, :], msq[:, :], front.rstd[:, :], ALU.mult).then_inc(s["msq"], 1)
                dve.wait_ge(s["msq"], at(i, 3, 2))
                dve.tensor_scalar(msq[:, :], msq[:, :], RMS_EPS, None, ALU.add).then_inc(s["msq"], 1)
                dve.wait_ge(s["r2"], at(i, 1, 1))
                dve.wait_ge(front.normal, at(i, 1, 1))
                for b in range(BATCH):
                    last = dve.tensor_scalar(hn[:, b * P:(b + 1) * P], front.xn[:, b * P:(b + 1) * P], r2[:, b:b + 1],
                                             None, ALU.mult)
                last.then_inc(s["hn"], 1)
                for tap, before, after in ((2, "v0", "conv1"), (1, "conv1", "conv2"), (0, "conv2", "conv3")):
                    for h in range(HALVES):
                        dve.wait_ge(s[before], at(i, 2, h + 1))
                        out = v[:, h, :, bass.ds(i * P, P)]
                        dve.scalar_tensor_tensor(out, u[:, h, :, bass.ds(i * P + tap, P)],
                                                 CW[:, h * TAPS + tap:h * TAPS + tap + 1], out, ALU.mult,
                                                 ALU.add).then_inc(s[after], 1)
                dve.wait_ge(s["kept"], at(i, 2, 2))

            n2 = 0
            for mh in range(2):
                for gq in range(GROUPS // 4):
                    dve.wait_ge(s["t2"], n2 + 1)
                    dve.tensor_copy(u2[:, 4 * gq:4 * gq + 4, :].rearrange("p g (m c) -> p g c m", m=SUPER)[
                                        :, :, mh * COLS // 2:(mh + 1) * COLS // 2, :],
                                    pb[4 + n2 % 4][:, :].rearrange("p (g c m) -> p g c m", g=4, m=SUPER)
                                    ).then_inc(s["t2_out"], 1)
                    n2 += 1

            def state_part(i, k):
                dve.wait_ge(s["x_mm"], at(i, 2, k + 3))
                dve.tensor_copy(h4[:, bass.ds(i * 2 + k, 1), :, 1:SUPERS + 1].rearrange("p g b s -> p (g b) s"),
                                pb[2 + k][:, 0:COLS].rearrange("p (b s) -> p b s", b=BATCH)).then_inc(s["x_out"], 1)

            dve.sem_inc(s["xT"], 2)
            dve.sem_inc(s["x_mm"], 2)
            dve.sem_inc(s["x_out"], 2)
            dve.wait_ge(s["t2_out"], n2)
            with dve.Fori(0, GROUPS // 2) as i:
                for k in range(2):
                    dve.wait_ge(s["xT"], at(i, 2, k + 1))
                    dve.tensor_tensor(channel_form(expB[k], SUPER),
                                      expanded(rb[:, bass.ds(i * 2 + k, 1), 16:80].rearrange("p g (n s) -> p (g n) s", n=SUPER)),
                                      own_block(SUPER), ALU.mult).then_inc(s["expB"], 1)
                for k in range(2):
                    state_part(i, k)

            dve.sem_inc(s["rec_out"], 1)
            with dve.Fori(0, SUPERS - 2) as i:
                dve.wait_ge(s["rec"], at(i, 1, 1))
                nxt = h4[:, :, :, bass.ds(i + 2, 1)].rearrange("p g b s -> p g (b s)")
                dve.tensor_tensor(nxt, pb[4][:, 0:GROUPS * BATCH].rearrange("p (g b) -> p g b", g=GROUPS), nxt,
                                  ALU.add).then_inc(s["rec_out"], 1)

            dve.sem_inc(s["y_mm"], 2)
            with dve.Fori(0, GROUPS // 2) as i:
                for k in range(2):
                    dve.wait_ge(s["y_mm"], at(i, 2, k + 1))
                    dve.tensor_tensor(channel_form(expO[k], SUPER),
                                      expanded(rc[:, bass.ds(i * 2 + k, 1), 17:81].rearrange("p g (n s) -> p (g n) s", n=SUPER)),
                                      own_block(SUPER), ALU.mult).then_inc(s["expO"], 1)

            n3 = 0
            for mh in range(2):
                for gq in range(GROUPS // 4):
                    dve.wait_ge(s["t3"], n3 + 1)
                    dve.tensor_copy(tb[mh][:, gq * 512:(gq + 1) * 512], pb[n3 % 4][:, :]).then_inc(s["t3_out"], 1)
                    n3 += 1
            for c in range(CHUNKS):
                dve.wait_ge(s["w_mm"], c + 1)
                xc = xs[:, c * WIDE:(c + 1) * WIDE]
                dve.tensor_tensor(xc, pb[c % 2][:, :], xc, ALU.add).then_inc(s["w_out"], 1)


def store_phase(nc, xs, out):
    with ExitStack() as ctx:
        S = Scope(nc, ctx, "store")
        stored = S.sem("stored")
        block = ctx.enter_context(nc.Block())
        out_view = out.rearrange("b (c p) f -> p c b f", p=P)

        @block.sync
        def _(sp):
            for c in range(CHUNKS):
                sp.dma_start(out_view[:, c], xs[:, c * WIDE:(c + 1) * WIDE].rearrange("p (b f) -> p b f", b=BATCH)
                             ).then_inc(stored, 16)
            sp.wait_ge(stored, 16 * CHUNKS)


def build(nc, t, out):
    with ExitStack() as ctx:
        xs = ctx.enter_context(nc.sbuf_tensor("xs", [P, CHUNKS * WIDE], F32))
        attention_phase(nc, xs, t["x"], t["wq"], t["wk"], t["wv"], t["wg"], t["bg"], t["wo"], t["decay_all"],
                        t["decay_pair"], t["ident"], t["lag"], t["causal"], t["tpos"], t["left"])
        mixture_phase(nc, xs, "moe0", HID0, ACT.Gelu, None, t["router0"], t["m0w1"], t["m0w2"], t["ident"], t["rank"])
        scratch = nc.dram_tensor("responses", (GC * GROUPS * (POS - 1 + 64),), F32, kind="Internal").ap()
        state_space_phase(nc, xs, scratch, t["norm_w"], t["win"], t["b_in"], t["conv_w"], t["conv_b"], t["a_rows_c"],
                          t["a_cols_b"], t["wout"], t["b_out"], t["ident"], t["own"])
        mixture_phase(nc, xs, "moe1", HID1, ACT.Silu, CAPACITY, t["router1"], t["m1w1"], t["m1w2"], t["ident"], t["rank"],
                      t["m1b1"], t["m1b2"], t["before"], t["restart"])
        store_phase(nc, xs, out)


def laid_out(i):
    def T(w):
        return np.ascontiguousarray(np.swapaxes(w, -1, -2))

    def pair_rows(w, n):
        return np.ascontiguousarray(w.reshape(n, P, -1).transpose(1, 0, 2).reshape(P, -1))

    def by_group(matrices, vectors):
        both = np.concatenate([matrices, vectors.reshape(D_IN, STATES, 1)], axis=2)
        return np.ascontiguousarray(both.reshape(GROUPS, P, STATES + 1).transpose(1, 0, 2))

    a = {k: np.asarray(v) for k, v in i.items()}
    dl = a["L0_attn_decay_log"]
    s_, t_ = np.meshgrid(np.arange(P), np.arange(P), indexing="ij")
    return {
        "x": a["L0_attn_x"],
        "wq": T(a["L0_attn_W_Q"]), "wk": T(a["L0_attn_W_K"]), "wv": T(a["L0_attn_W_V"]), "wg": T(a["L0_attn_W_g_w"]),
        "bg": T(a["L0_attn_W_g_b"].reshape(PAIRS, P)), "wo": pair_rows(T(a["L0_attn_W_O"]), PAIRS),
        "decay_all": np.ascontiguousarray(np.broadcast_to(dl[None], (P, HEADS))),
        "decay_pair": T(np.repeat(dl.reshape(PAIRS, 2), DK, axis=1)),
        "ident": np.eye(P, dtype=np.float32),
        "lag": np.maximum(t_ - s_, 0).astype(np.float32), "causal": (t_ >= s_).astype(np.float32),
        "tpos": np.broadcast_to(np.arange(1, P + 1, dtype=np.float32), (P, P)).copy(),
        "norm_w": a["L1_attn_norm_w"].reshape(D, 1), "win": a["L1_attn_Win"],
        "b_in": T(a["L1_attn_b_in"].reshape(HALVES, P)), "conv_b": T(a["L1_attn_conv_b"].reshape(HALVES, P)),
        "conv_w": pair_rows(a["L1_attn_conv_w"].reshape(D_IN, TAPS), HALVES),
        "a_rows_c": by_group(a["L1_attn_A"], a["L1_attn_Cm"]), "a_cols_b": by_group(T(a["L1_attn_A"]), a["L1_attn_Bm"]),
        "wout": pair_rows(a["L1_attn_Wout"], HALVES),
        "b_out": np.broadcast_to(a["L1_attn_b_out"][None], (P, D)).copy(),
        "own": np.repeat(np.eye(GC, dtype=np.float32), POS, axis=0),
        "router0": T(a["L0_ffn_router_w"]), "m0w1": T(a["L0_ffn_w1"].reshape(-1, D)),
        "m0w2": pair_rows(T(a["L0_ffn_w2"]).reshape(-1, D), EXPERTS * HID0 // P),
        "router1": a["L1_ffn_router_w"],
        "m1w1": pair_rows(np.concatenate([a["L1_ffn_w1"], a["L1_ffn_sw1"][None]]).reshape(-1, HID1), EXPERTS + 1),
        "m1w2": pair_rows(np.concatenate([a["L1_ffn_w2"], a["L1_ffn_sw2"][None]]).reshape(-1, D),
                          (EXPERTS + 1) * HID1 // P),
        "m1b1": T(np.concatenate([a["L1_ffn_b1"], a["L1_ffn_sb1"][None]]).reshape(-1, P)),
        "m1b2": np.concatenate([a["L1_ffn_b2"], a["L1_ffn_sb2"][None]]),
        "rank": np.broadcast_to(np.repeat(np.arange(EXPERTS, 0, -1), TILES).astype(np.float32),
                                (P, EXPERTS * TILES)).copy(),
        "before": (s_ < t_).astype(np.float32),
        "restart": np.broadcast_to((np.arange(2 * EXPERTS * TILES) % TILES != 0).astype(np.float32),
                                   (P, 2 * EXPERTS * TILES)).copy(),
        "left": np.arange(P - 1, -1, -1, dtype=np.float32).reshape(P, 1),
    }


def kernel(**inputs):
    import concourse.bacc as bacc
    from concourse.bass_utils import run_bass_kernel_spmd

    nc = bacc.Bacc("TRN2", target_bir_lowering=False, num_devices=1)
    arrays = laid_out(inputs)
    t = {n: nc.dram_tensor(n, a.shape, mybir.dt.from_np(a.dtype), kind="ExternalInput").ap()
         for n, a in arrays.items()}
    out = nc.dram_tensor("out", (BATCH, SEQ, D), F32, kind="ExternalOutput").ap()
    build(nc, t, out)
    r = run_bass_kernel_spmd(nc, [arrays], core_ids=[0])
    return r.results[0]["out"]
```

```python
from contextlib import ExitStack

import numpy as np
import concourse.bass as bass
from concourse import mybir

F32 = mybir.dt.float32
ALU = mybir.AluOpType
ACT = mybir.ActivationFunctionType
AX = mybir.AxisListType

P = 128
BATCH, SEQ, D = 4, 1024, 128
CHUNKS = SEQ // P
WIDE = BATCH * P
HEADS, DK = 8, 64
HD = HEADS * DK
PAIRS = HEADS // 2
LN_EPS = 1e-5
DEN_EPS = 1e-6


PROJECTIONS = [(w, p) for p in range(PAIRS) for w in "qkv"] + [("g", p) for p in range(PAIRS)]


def at(i, per_turn, k):
    return i * per_turn + k


def wide(ap, n=BATCH):
    return ap.rearrange("p (b f) -> p b f", b=n)


class Scope:

    def __init__(self, nc, ctx, name):
        self.nc, self.ctx, self.name = nc, ctx, name

    def sb(self, name, cols, parts=P):
        return self.ctx.enter_context(self.nc.sbuf_tensor(f"{self.name}_{name}", [parts, cols], F32))

    def bank(self, name):
        return self.ctx.enter_context(self.nc.psum_tensor(f"{self.name}_{name}", [P, 512], F32))

    def sem(self, name):
        return self.ctx.enter_context(self.nc.semaphore(f"{self.name}_{name}"))


TILES = BATCH * CHUNKS


class Front:

    def __init__(self, S, ident, turns=2):
        self.ident = ident
        self.stats = S.sb("stats", 6 * TILES)
        self.mean, self.var, self.vpe, self.rstd, self.mhalf, self.apart = (
            S.sb(n, TILES) for n in "mean var vpe rstd mhalf apart".split())
        self.xn = [S.sb(f"xn{k}", WIDE) for k in range(turns)]
        self.turn = [S.bank(f"turn{k}") for k in range(turns)]
        self.filled, self.stat, self.moments, self.var_eps, self.rstd_ready, self.normal, self.turned, self.held = (
            S.sem(n) for n in "filled stat moments var_eps rstd_ready normal turned held".split())

    def inverse_deviation(self, pool):
        pool.memset(self.mhalf[:, :], -0.5).then_inc(self.filled, 1)
        pool.wait_ge(self.filled, 1)
        pool.wait_ge(self.var_eps, 1)
        pool.tensor_tensor(self.rstd[:, :], self.vpe[:, :], self.mhalf[:, :], ALU.pow).then_inc(self.rstd_ready, 1)

    def moments_of(self, dve, xs):
        with dve.Fori(0, CHUNKS) as i:
            for b in range(BATCH):
                last = dve.bn_stats(self.stats[:, bass.ds(i * 6 * BATCH + 6 * b, 6)], xs[:, bass.ds(i * WIDE + b * P, P)])
            last.then_inc(self.stat, 1)
        dve.wait_ge(self.stat, CHUNKS)
        even, odd = self.stats[:, 1:6 * TILES:6], self.stats[:, 4:6 * TILES:6]
        dve.tensor_tensor(self.apart[:, :], even, odd, ALU.subtract).then_inc(self.moments, 1)
        dve.tensor_tensor(self.mean[:, :], even, odd, ALU.add).then_inc(self.moments, 1)
        dve.tensor_tensor(self.var[:, :], self.stats[:, 2:6 * TILES:6], self.stats[:, 5:6 * TILES:6],
                          ALU.add).then_inc(self.moments, 1)
        dve.wait_ge(self.moments, 3)
        dve.scalar_tensor_tensor(self.apart[:, :], self.apart[:, :], 0.25, self.apart[:, :], ALU.mult,
                                 ALU.mult).then_inc(self.moments, 1)
        dve.tensor_scalar(self.mean[:, :], self.mean[:, :], 0.5, None, ALU.mult).then_inc(self.moments, 1)
        dve.wait_ge(self.moments, 5)
        dve.scalar_tensor_tensor(self.var[:, :], self.var[:, :], 1.0 / D, self.apart[:, :], ALU.mult,
                                 ALU.add).then_inc(self.moments, 1)
        dve.wait_ge(self.moments, 6)
        dve.tensor_scalar(self.vpe[:, :], self.var[:, :], LN_EPS, None, ALU.add).then_inc(self.var_eps, 1)
        dve.wait_ge(self.rstd_ready, 1)

    def normalize(self, dve, xs, i, k):
        for b in range(BATCH):
            last = dve.tensor_scalar(self.xn[k][:, b * P:(b + 1) * P], xs[:, bass.ds(i * WIDE + b * P, P)],
                                     self.mean[:, bass.ds(i * BATCH + b, 1)], self.rstd[:, bass.ds(i * BATCH + b, 1)],
                                     ALU.subtract, ALU.mult)
        last.then_inc(self.normal, 1)

    def transpose(self, pe, i, k):
        pe.wait_ge(self.normal, i + 1)
        for b in range(BATCH):
            mm = pe.transpose(self.turn[k][:, b * P:(b + 1) * P], self.xn[k][:, b * P:(b + 1) * P], self.ident[:, :])
        mm.then_inc(self.turned, 1)


def attention_phase(nc, xs, x, wq, wk, wv, wg, bg, wo, decay_all, decay_pair, ident_d, lag_d, causal_d, tpos_d, left_d):
    with ExitStack() as ctx:
        S = Scope(nc, ctx, "attn")
        ident, lag, causal, tpos = S.sb("ident", P), S.sb("lag", P), S.sb("causal", P), S.sb("tpos", P)
        left = S.sb("left", 1)
        WQ, WK, WV, WG, WO = (S.sb(n, HD) for n in ("WQ", "WK", "WV", "WG", "WO"))
        half_bg, bgc = S.sb("half_bg", PAIRS), S.sb("bgc", PAIRS)
        dl = S.sb("dl", HEADS + PAIRS)
        tmp, lg = S.sb("tmp", HEADS + PAIRS), S.sb("lg", HEADS + PAIRS)
        mask = S.sb("mask", HEADS * P)
        qpow = S.sb("qpow", PAIRS * P)
        kpow = S.sb("kpow", HEADS)
        gchunk = S.sb("gchunk", PAIRS)
        xT = S.sb("xT", WIDE)
        e = [S.sb(f"e{k}", WIDE) for k in range(2)]
        r = [S.sb(f"r{k}", WIDE) for k in range(2)]
        qT, kT, qd, gate = (S.sb(n, PAIRS * WIDE) for n in ("qT", "kT", "qd", "gate"))
        kd = S.sb("kd", BATCH * HD)
        v1 = S.sb("v1", BATCH * HEADS * (DK + 1))
        a = [S.sb(f"a{k}", WIDE) for k in range(2)]
        state = S.sb("state", PAIRS * BATCH * (DK + 1))
        den, rden = S.sb("den", BATCH), S.sb("rden", BATCH)
        y, yT = S.sb("y", BATCH * HD), S.sb("yT", PAIRS * WIDE)
        proj = [S.bank(f"proj{k}") for k in range(2)]
        score = [S.bank(f"score{k}") for k in range(2)]
        av = [S.bank(f"av{k}") for k in range(2)]
        front = Front(S, ident, 1)
        turn, stp = front.turn[0], S.bank("stp")

        names = ("loaded x_loaded neg_abs exped logged lg_ready tables gmul xT proj "
                 "exp phi gate v ktr kd qd score a av den rden y stp state ytr yT out res").split()
        s = {n: S.sem(n) for n in names}
        x_view = x.rearrange("b (c p) f -> p c b f", p=P)
        v4 = v1[:, :].rearrange("p (b h j) -> p b h j", b=BATCH, h=HEADS)
        y3, kd3 = wide(y[:, :]), wide(kd[:, :])
        st4 = state[:, :].rearrange("p (q b j) -> p q b j", q=PAIRS, b=BATCH)
        NSETUP = 14

        block = ctx.enter_context(nc.Block())

        @block.sync
        def _(sp):
            for c in range(CHUNKS):
                sp.dma_start(xs[:, c * WIDE:(c + 1) * WIDE].rearrange("p (b f) -> p b f", b=BATCH),
                             x_view[:, c]).then_inc(s["x_loaded"], 16)

        @block.scalar
        def _(act):
            for dst, src in ((dl[:, 0:HEADS], decay_all), (dl[:, HEADS:], decay_pair), (lag[:, :], lag_d),
                             (causal[:, :], causal_d), (tpos[:, :], tpos_d), (left[:, :], left_d),
                             (bgc[:, :], bg), (ident[:, :], ident_d), (WQ[:, :], wq), (WK[:, :], wk),
                             (WG[:, :], wg), (WV[:, :], wv), (WO[:, :], wo)):
                act.dma_start(dst, src).then_inc(s["loaded"], 16)
            act.wait_ge(s["neg_abs"], 1)
            act.activation(tmp[:, :], tmp[:, :], ACT.Exp).then_inc(s["exped"], 1)
            act.wait_ge(s["exped"], 1)
            act.activation(tmp[:, :], tmp[:, :], ACT.Ln, bias=1.0).then_inc(s["logged"], 1)
            act.wait_ge(s["lg_ready"], 1)
            for h in range(HEADS):
                act.activation(mask[:, h * P:(h + 1) * P], lag[:, :], ACT.Exp,
                               scale=lg[:, h:h + 1]).then_inc(s["tables"], 1)
            for p in range(PAIRS):
                act.activation(qpow[:, p * P:(p + 1) * P], tpos[:, :], ACT.Exp,
                               scale=lg[:, HEADS + p:HEADS + p + 1]).then_inc(s["tables"], 1)
            act.activation(kpow[:, :], lg[:, 0:HEADS], ACT.Exp, scale=left[:, 0:1]).then_inc(s["tables"], 1)
            act.activation(gchunk[:, :], lg[:, HEADS:], ACT.Exp, scale=float(P)).then_inc(s["tables"], 1)

            def token_columns(i):
                act.wait_ge(front.turned, at(i, 1, 1))
                act.activation(xT[:, :], turn[:, :], ACT.Copy).then_inc(s["xT"], 1)

            def turn_of(i, last):
                k = 0
                for n, (what, p) in enumerate(PROJECTIONS):
                    act.wait_ge(s["proj"], at(i, 16, n + 1))
                    bank = proj[n % 2]
                    if what in "qk":
                        if k >= 2:
                            act.wait_ge(s["phi"], at(i, 8, k - 1))
                        act.activation(e[k % 2][:, :], bank[:, :], ACT.Exp)
                        act.activation(r[k % 2][:, :], bank[:, :], ACT.Relu).then_inc(s["exp"], 1)
                        k += 1
                    elif what == "g":
                        act.activation(gate[:, p * WIDE:(p + 1) * WIDE], bank[:, :], ACT.Tanh,
                                       bias=half_bg[:, p:p + 1], scale=0.5).then_inc(s["gate"], 1)
                    else:
                        act.activation(v4[:, p, :, 0:DK], bank[:, :].rearrange("p (h j) -> p h j", h=HEADS),
                                       ACT.Copy).then_inc(s["v"], 1)
                if not last:
                    token_columns(i + 1)

            act.wait_ge(s["gmul"], 2)
            token_columns(0)
            with act.Fori(0, CHUNKS - 1) as i:
                turn_of(i, False)
            turn_of(CHUNKS - 1, True)

        @block.gpsimd
        def _(pool):
            front.inverse_deviation(pool)
            pool.wait_ge(s["tables"], NSETUP)

            def turn_of(i, last):
                for p in range(PAIRS):
                    pool.wait_ge(s["phi"], at(i, 8, 2 * p + 1))
                    pool.tensor_tensor(wide(qd[:, p * WIDE:(p + 1) * WIDE]), wide(qT[:, p * WIDE:(p + 1) * WIDE]),
                                       qpow[:, p * P:(p + 1) * P].unsqueeze(1).to_broadcast([P, BATCH, P]),
                                       ALU.mult).then_inc(s["qd"], 1)

            with pool.Fori(0, CHUNKS - 1) as i:
                turn_of(i, False)
            turn_of(CHUNKS - 1, True)

        @block.tensor
        def _(pe):
            def token_columns(i):
                front.transpose(pe, i, 0)

            def turn_of(i, last):
                pe.wait_ge(s["xT"], at(i, 1, 1))
                for n, (what, p) in enumerate(PROJECTIONS):
                    if n >= 2:
                        before, b = PROJECTIONS[n - 2]
                        if before == "v":
                            pe.wait_ge(s["v"], at(i, 4, b + 1))
                        elif before == "g":
                            pe.wait_ge(s["gate"], at(i, 4, b + 1))
                        else:
                            pe.wait_ge(s["exp"], at(i, 8, 2 * b + 1 + (before == "k")))
                    if what == "v":
                        pe.matmul(proj[n % 2][:, :], xT[:, p * P:(p + 1) * P], WV[:, :], start=True,
                                  stop=True).then_inc(s["proj"], 1)
                    else:
                        W = {"q": WQ, "k": WK, "g": WG}[what]
                        pe.matmul(proj[n % 2][:, :], W[:, p * P:(p + 1) * P], xT[:, :], start=True,
                                  stop=True).then_inc(s["proj"], 1)

                def keys_turned(p):
                    if p == 1:
                        pe.wait_ge(s["kd"], at(i, 4, 1))
                    elif p >= 2:
                        pe.wait_ge(s["yT"], at(i, 4, p - 1))
                    for b in range(BATCH):
                        mm = pe.transpose(turn[:, b * P:(b + 1) * P],
                                          kT[:, p * WIDE + b * P:p * WIDE + (b + 1) * P], ident[:, :])
                    mm.then_inc(s["ktr"], 1)

                def outputs_turned(p):
                    pe.wait_ge(s["y"], at(i, 8, 2 * p + 2))
                    if p < PAIRS - 1:
                        pe.wait_ge(s["kd"], at(i, 4, p + 2))
                    elif not last:
                        pe.wait_ge(s["xT"], at(i, 1, 2))
                    else:
                        pe.wait_ge(s["yT"], at(i, 4, 3))
                    for b in range(BATCH):
                        mm = pe.transpose(turn[:, b * P:(b + 1) * P], y3[:, b, p * P:(p + 1) * P], ident[:, :])
                    mm.then_inc(s["ytr"], 1)

                def scores(h):
                    p, lo = h // 2, DK * (h % 2)
                    if h >= 2:
                        pe.wait_ge(s["a"], at(i, 8, h - 1))
                    pe.wait_ge(s["phi"], at(i, 8, 2 * p + 2))
                    for b in range(BATCH):
                        cols = slice(p * WIDE + b * P, p * WIDE + (b + 1) * P)
                        mm = pe.matmul(score[h % 2][:, b * P:(b + 1) * P], kT[lo:lo + DK, cols], qT[lo:lo + DK, cols],
                                       start=True, stop=True)
                    mm.then_inc(s["score"], 1)

                def values(h):
                    p, lo = h // 2, DK * (h % 2)
                    pe.wait_ge(s["a"], at(i, 8, h + 1))
                    if h % 2 == 0:
                        pe.wait_ge(s["qd"], at(i, 4, p + 1))
                    if h == 0:
                        pe.wait_ge(s["v"], at(i, 4, 4))
                    pe.wait_ge(s["state"], at(i, 4, 1))
                    if h >= 2:
                        pe.wait_ge(s["y"], at(i, 8, h - 1))
                    for b in range(BATCH):
                        cols = slice(p * WIDE + b * P, p * WIDE + (b + 1) * P)
                        o = av[h % 2][:, b * (DK + 1):(b + 1) * (DK + 1)]
                        pe.matmul(o, a[h % 2][:, b * P:(b + 1) * P], v4[:, b, h, :], start=True, stop=False)
                        mm = pe.matmul(o, qd[lo:lo + DK, cols], st4[lo:lo + DK, p, b, :], start=False, stop=True)
                    mm.then_inc(s["av"], 1)

                def new_state(p):
                    pe.wait_ge(s["kd"], at(i, 4, p + 1))
                    if p == 0:
                        pe.wait_ge(s["res"], i + 1)
                    else:
                        pe.wait_ge(s["state"], at(i, 4, 1 + p))
                    for h in (2 * p, 2 * p + 1):
                        lo = DK * (h % 2)
                        for b in range(BATCH):
                            mm = pe.matmul(stp[lo:lo + DK, b * (DK + 1):(b + 1) * (DK + 1)],
                                           kd3[:, b, h * DK:(h + 1) * DK], v4[:, b, h, :], start=True, stop=True)
                    mm.then_inc(s["stp"], 1)

                scores(0)
                scores(1)
                for h in range(HEADS):
                    p = h // 2
                    values(h)
                    if h + 2 < HEADS:
                        scores(h + 2)
                    if h % 2 == 0:
                        keys_turned(p)
                    else:
                        new_state(p)
                        if p >= 1:
                            outputs_turned(p - 1)
                if not last:
                    pe.wait_ge(s["yT"], at(i, 4, 3))
                    token_columns(i + 1)
                outputs_turned(PAIRS - 1)
                pe.wait_ge(s["state"], at(i, 4, 5))
                pe.wait_ge(s["yT"], at(i, 4, 4))
                for b in range(BATCH):
                    for p in range(PAIRS):
                        cols = slice(p * WIDE + b * P, p * WIDE + (b + 1) * P)
                        mm = pe.matmul(stp[:, b * P:(b + 1) * P], yT[:, cols], WO[:, p * P:(p + 1) * P],
                                       start=(p == 0), stop=(p == PAIRS - 1))
                mm.then_inc(s["out"], 1)

            pe.wait_ge(s["loaded"], 16 * 13)
            token_columns(0)
            with pe.Fori(0, CHUNKS - 1) as i:
                turn_of(i, False)
            turn_of(CHUNKS - 1, True)

        @block.vector
        def _(dve):
            dve.wait_ge(s["loaded"], 16 * 13)
            dve.tensor_scalar(tmp[:, :], dl[:, :], -1.0, None, ALU.mult).then_inc(s["gmul"], 1)
            dve.wait_ge(s["gmul"], 1)
            dve.tensor_tensor(tmp[:, :], tmp[:, :], dl[:, :], ALU.min).then_inc(s["neg_abs"], 1)
            dve.memset(v1[:, :], 1.0)
            dve.tensor_scalar(half_bg[:, :], bgc[:, :], 0.5, None, ALU.mult).then_inc(s["gmul"], 1)
            dve.memset(state[:, :], 0.0).then_inc(s["state"], 1)
            dve.wait_ge(s["logged"], 1)
            dve.scalar_tensor_tensor(lg[:, :], dl[:, :], 0.0, tmp[:, :], ALU.min, ALU.subtract).then_inc(s["lg_ready"], 1)
            dve.wait_ge(s["tables"], NSETUP)
            m3 = wide(mask[:, :], HEADS)
            dve.tensor_tensor(m3, m3, causal[:, :].unsqueeze(1).to_broadcast([P, HEADS, P]), ALU.mult).then_inc(s["gmul"], 1)

            def turn_of(i, last):
                for k in range(2 * PAIRS):
                    dst = kT if k % 2 else qT
                    p = k // 2
                    dve.wait_ge(s["exp"], at(i, 8, k + 1))
                    dve.scalar_tensor_tensor(dst[:, p * WIDE:(p + 1) * WIDE], e[k % 2][:, :], 1.0, r[k % 2][:, :],
                                             ALU.min, ALU.add).then_inc(s["phi"], 1)

                def weighted_keys(p):
                    dve.wait_ge(s["ktr"], at(i, 4, p + 1))
                    dve.tensor_tensor(kd3[:, :, p * P:(p + 1) * P].rearrange("p b (h j) -> p b h j", h=2),
                                      turn[:, :].rearrange("p (b h j) -> p b h j", b=BATCH, h=2),
                                      kpow[:, 2 * p:2 * p + 2].unsqueeze(1).unsqueeze(3).to_broadcast([P, BATCH, 2, DK]),
                                      ALU.mult).then_inc(s["kd"], 1)

                def gated(p):
                    dve.wait_ge(s["gate"], at(i, 4, p + 1))
                    dve.wait_ge(s["ytr"], at(i, 4, p + 1))
                    dve.scalar_tensor_tensor(yT[:, p * WIDE:(p + 1) * WIDE], gate[:, p * WIDE:(p + 1) * WIDE], 1.0,
                                             turn[:, :], ALU.add, ALU.mult).then_inc(s["yT"], 1)

                def masked(h):
                    dve.wait_ge(s["score"], at(i, 8, h + 1))
                    dve.tensor_tensor(wide(a[h % 2][:, :]), wide(score[h % 2][:, :]),
                                      mask[:, h * P:(h + 1) * P].unsqueeze(1).to_broadcast([P, BATCH, P]),
                                      ALU.mult).then_inc(s["a"], 1)

                def divided(h):
                    dve.wait_ge(s["av"], at(i, 8, h + 1))
                    o = av[h % 2][:, 0:BATCH * (DK + 1)].rearrange("p (b j) -> p b j", b=BATCH)
                    dve.tensor_scalar(den[:, :], o[:, :, DK], DEN_EPS, 2.0, ALU.add, ALU.mult).then_inc(s["den"], 1)
                    dve.wait_ge(s["den"], at(i, 8, h + 1))
                    dve.reciprocal(rden[:, :], den[:, :]).then_inc(s["rden"], 1)
                    dve.wait_ge(s["rden"], at(i, 8, h + 1))
                    dve.tensor_tensor(y3[:, :, h * DK:(h + 1) * DK], o[:, :, 0:DK],
                                      rden[:, :].unsqueeze(2).to_broadcast([P, BATCH, DK]), ALU.mult).then_inc(s["y"], 1)

                masked(0)
                masked(1)
                for h in range(HEADS):
                    divided(h)
                    if h + 2 < HEADS:
                        masked(h + 2)
                    p = h // 2
                    if h % 2 == 0:
                        weighted_keys(p)
                    else:
                        dve.wait_ge(s["stp"], at(i, 4, p + 1))
                        dve.scalar_tensor_tensor(st4[:, p], st4[:, p], gchunk[:, p:p + 1],
                                                 stp[:, 0:BATCH * (DK + 1)].rearrange("p (b j) -> p b j", b=BATCH),
                                                 ALU.mult, ALU.add).then_inc(s["state"], 1)
                        if p >= 1:
                            gated(p - 1)
                    if h == 2 and not last:
                        front.normalize(dve, xs, i + 1, 0)
                gated(PAIRS - 1)
                dve.wait_ge(s["out"], at(i, 1, 1))
                xc = xs[:, bass.ds(i * WIDE, WIDE)]
                dve.tensor_tensor(xc, stp[:, :], xc, ALU.add).then_inc(s["res"], 1)

            dve.sem_inc(s["res"], 1)
            dve.wait_ge(s["x_loaded"], 16 * CHUNKS)
            front.moments_of(dve, xs)
            front.normalize(dve, xs, 0, 0)
            with dve.Fori(0, CHUNKS - 1) as i:
                turn_of(i, False)
            turn_of(CHUNKS - 1, True)


EXPERTS = 8
HID0, HID1 = 256, 512
CAPACITY = int(np.ceil(2 * 1.25 * BATCH * SEQ / EXPERTS))
BIG = 3.0e38


def first_largest(dve, values, rank, best, eq, mask, chain):
    by_expert = lambda t: t.rearrange("p e n -> p n e")
    spread = lambda t: t.unsqueeze(1).to_broadcast([P, EXPERTS, TILES])
    chain(dve.tensor_reduce(best, by_expert(values), AX.X, ALU.max))
    chain(dve.tensor_tensor(eq, values, spread(best), ALU.is_equal))
    chain(dve.tensor_tensor(eq, eq, rank, ALU.mult))
    chain(dve.tensor_reduce(best, by_expert(eq), AX.X, ALU.max))
    chain(dve.tensor_tensor(mask, eq, spread(best), ALU.is_equal))


def mixture_phase(nc, xs, name, hidden, act_fn, capacity, router, w1, w2, ident_d, rank_d, b1=None, b2=None,
                  before_d=None, restart_d=None):
    with ExitStack() as ctx:
        S = Scope(nc, ctx, name)
        biased = b1 is not None
        nexp = EXPERTS + 1 if biased else EXPERTS
        HB = hidden // P
        ident, rank = S.sb("ident", P), S.sb("rank", EXPERTS * TILES)
        R = S.sb("router", EXPERTS)
        W1, W2 = S.sb("W1", nexp * hidden), S.sb("W2", nexp * HB * P)
        XT = S.sb("XT", CHUNKS * WIDE)
        NE = EXPERTS * TILES
        logits, eq, rest = S.sb("logits", NE), S.sb("eq", NE), S.sb("rest", NE)
        masks, gates = S.sb("masks", 2 * NE), S.sb("gates", NE)
        best, second, w_a, w_b = (S.sb(n, TILES) for n in ("best", "second", "w_a", "w_b"))
        hT = [S.sb(f"hT{k}", HB * WIDE) for k in range(2)]
        xc = [S.sb(f"xc{k}", WIDE) for k in range(2)]
        gcol = S.sb("gcol", BATCH * nexp)
        front = Front(S, ident)
        small = S.bank("small")
        hid = [S.bank(f"hid{k}") for k in range(3)]
        outp = [S.bank(f"outp{k}") for k in range(2)]
        s = {n: S.sem(n) for n in "loaded columns kept lg_mm lg_out chain expd summed recip prefix gcol hid act outp acc gT gTs bias bias_in".split()}
        if biased:
            B1, B2 = S.sb("B1", nexp * HB), S.sb("B2", P, nexp)
            before, restart = S.sb("before", P), S.sb("restart", 2 * NE)
            ones = S.sb("ones", P)
            incl, pos = S.sb("incl", 2 * NE), S.sb("pos", 2 * NE)
            gT = S.sb("gT", WIDE, nexp)
        loads = [(ident, ident_d), (rank, rank_d), (R, router)]
        late = [(W1, w1), (W2, w2)]
        if biased:
            loads += [(before, before_d), (restart, restart_d)]
            late += [(B1, b1), (B2, b2)]
        late_in = S.sem("late_in")

        by_tile = lambda t: t.rearrange("p (e n) -> p e n", e=EXPERTS)
        by_chunk = lambda t: t.rearrange("p (e b c) -> p b e c", e=EXPERTS, b=BATCH)
        g3 = gcol[:, :].rearrange("p (b e) -> p b e", b=BATCH)

        block = ctx.enter_context(nc.Block())

        @block.sync
        def _(sp):
            for dst, src in loads:
                sp.dma_start(dst[:, :], src).then_inc(s["loaded"], 16)
            for dst, src in late:
                sp.dma_start(dst[:, :], src).then_inc(late_in, 16)

        @block.gpsimd
        def _(pool):
            front.inverse_deviation(pool)
            with pool.Fori(0, CHUNKS // 2) as i:
                for k in range(2):
                    pool.wait_ge(s["columns"], at(i, 2, k + 1))
                    pool.sem_inc(front.held, 1)
                    pool.tensor_copy(XT[:, bass.ds(i * 2 * WIDE + k * WIDE, WIDE)], xc[k][:, :]).then_inc(s["kept"], 1)

        @block.tensor
        def _(pe):
            pe.wait_ge(s["loaded"], 16 * len(loads))
            def logits_of(i, k):
                pe.wait_ge(s["columns"], at(i, 2, k + 1))
                pe.wait_ge(s["lg_out"], at(i, 2, k + 1))
                for b in range(BATCH):
                    mm = pe.matmul(small[:, b * EXPERTS:(b + 1) * EXPERTS], xc[k][:, b * P:(b + 1) * P], R[:, :],
                                   start=True, stop=True)
                mm.then_inc(s["lg_mm"], 1)

            with pe.Fori(0, CHUNKS // 2) as i:
                front.transpose(pe, i * 2, 0)
                front.transpose(pe, i * 2 + 1, 1)
                logits_of(i, 0)
                logits_of(i, 1)
            pe.wait_ge(s["kept"], CHUNKS + 2)
            pe.wait_ge(late_in, 16 * len(late))
            if biased:
                pe.wait_ge(s["prefix"], 1)
                pe.matmul(hid[0][:, :], before[:, :], masks[:, :], start=True, stop=True)
                pe.matmul(hid[1][:, :], ones[:, :], masks[:, :], start=True, stop=True).then_inc(s["hid"], 1)
            base = 1 if biased else 0

            with pe.Fori(0, CHUNKS) as i:
                def hidden_of(e):
                    for m in range(HB):
                        k = e * HB + m
                        pe.wait_ge(s["act"], at(i, nexp * HB, k + 1))
                        pe.matmul(hid[k % 3][:, :], W1[:, (e * HB + m) * P:(e * HB + m + 1) * P],
                                  XT[:, bass.ds(i * WIDE, WIDE)], start=True, stop=True).then_inc(s["hid"], 1)

                def output_of(e):
                    pe.wait_ge(s["act"], at(i, nexp * HB, 3 + (e + 1) * HB))
                    pe.wait_ge(s["acc"], at(i, nexp, e + 1))
                    for b in range(BATCH):
                        for m in range(HB):
                            mm = pe.matmul(outp[e % 2][:, b * P:(b + 1) * P],
                                           hT[e % 2][:, m * WIDE + b * P:m * WIDE + (b + 1) * P],
                                           W2[:, (e * HB + m) * P:(e * HB + m + 1) * P],
                                           start=(m == 0), stop=(m == HB - 1))
                    mm.then_inc(s["outp"], 1)

                hidden_of(0)
                if biased:
                    pe.wait_ge(s["gcol"], at(i, 1, 1))
                    for b in range(BATCH):
                        mm = pe.transpose(front.turn[0][0:nexp, b * P:(b + 1) * P], g3[:, b, :], ident[:, :])
                    mm.then_inc(s["gT"], 1)
                for e in range(1, nexp):
                    hidden_of(e)
                    output_of(e - 1)
                if biased:
                    pe.wait_ge(s["gTs"], at(i, 1, 1))
                    pe.wait_ge(s["bias_in"], at(i, 1, 1))
                    for b in range(BATCH):
                        mm = pe.matmul(small[:, b * P:(b + 1) * P], gT[:, b * P:(b + 1) * P], B2[:, :],
                                       start=True, stop=True)
                    mm.then_inc(s["bias"], 1)
                output_of(nexp - 1)

        @block.scalar
        def _(act):
            act.sem_inc(s["lg_mm"], 2)
            act.sem_inc(s["kept"], 2)
            with act.Fori(0, CHUNKS // 2) as i:
                for k in range(2):
                    act.wait_ge(front.turned, at(i, 2, k + 1))
                    act.wait_ge(s["lg_mm"], at(i, 2, k + 1))
                    act.wait_ge(s["kept"], at(i, 2, k + 1))
                    act.activation(xc[k][:, :], front.turn[k][:, :], ACT.Copy).then_inc(s["columns"], 1)
            act.wait_ge(s["expd"], 1)
            if biased:
                act.activation(logits[:, :], logits[:, :], ACT.Exp).then_inc(s["recip"], 1)
            else:
                act.activation(w_b[:, :], w_b[:, :], ACT.Exp).then_inc(s["recip"], 1)
            base = 1 if biased else 0
            act.wait_ge(s["gcol"], 1)
            act.sem_inc(s["act"], 3)
            with act.Fori(0, CHUNKS) as i:
                for e in range(nexp):
                    for m in range(HB):
                        k = e * HB + m
                        act.wait_ge(s["hid"], at(i, nexp * HB, base + k + 1))
                        if m == 0:
                            act.wait_ge(s["acc"], at(i, nexp, e + 1))
                        act.activation(hT[e % 2][:, m * WIDE:(m + 1) * WIDE], hid[k % 3][:, :], act_fn,
                                       **({"bias": B1[:, k:k + 1]} if biased else {})).then_inc(s["act"], 1)
                    if biased and e == 0:
                        act.wait_ge(s["gT"], at(i, 1, 1))
                        act.activation(gT[:, :], front.turn[0][0:nexp, :], ACT.Copy).then_inc(s["gTs"], 1)

        @block.vector
        def _(dve):
            count = [0]

            def chain(ins):
                count[0] += 1
                ins.then_inc(s["chain"], 1)
                dve.wait_ge(s["chain"], count[0])

            dve.sem_inc(s["lg_out"], 1)
            front.moments_of(dve, xs)
            front.normalize(dve, xs, 0, 0)
            front.normalize(dve, xs, 1, 1)

            def logits_kept(i, k):
                dve.wait_ge(s["lg_mm"], at(i, 2, k + 3))
                dve.tensor_copy(by_chunk(logits[:, :])[:, :, :, bass.ds(i * 2 + k, 1)],
                                small[:, 0:BATCH * EXPERTS].rearrange("p (b e c) -> p b e c", b=BATCH, c=1)
                                ).then_inc(s["lg_out"], 1)

            with dve.Fori(0, CHUNKS // 2 - 1) as i:
                for k in range(2):
                    dve.wait_ge(front.turned, at(i, 2, k + 1))
                    front.normalize(dve, xs, i * 2 + 2 + k, k)
                for k in range(2):
                    logits_kept(i, k)
            for k in range(2):
                logits_kept(CHUNKS // 2 - 1, k)
            dve.wait_ge(s["loaded"], 16 * len(loads))
            dve.wait_ge(s["lg_out"], CHUNKS + 1)
            L, EQ, RK = by_tile(logits[:, :]), by_tile(eq[:, :]), by_tile(rank[:, :])
            M1, M2 = by_tile(masks[:, 0:NE]), by_tile(masks[:, NE:])
            RS, G = by_tile(rest[:, :]), by_tile(gates[:, :])
            experts_inside = lambda t: t.rearrange("p e n -> p n e")
            spread = lambda t: t[:, :].unsqueeze(1).to_broadcast([P, EXPERTS, TILES])
            if not biased:
                first_largest(dve, L, RK, best[:, :], EQ, M1, chain)
                chain(dve.scalar_tensor_tensor(RS, M1, -BIG, L, ALU.mult, ALU.add))
                first_largest(dve, RS, RK, second[:, :], EQ, M2, chain)
                chain(dve.tensor_reduce(best[:, :], experts_inside(L), AX.X, ALU.max))
                chain(dve.tensor_reduce(second[:, :], experts_inside(RS), AX.X, ALU.max))
                dve.tensor_tensor(w_b[:, :], second[:, :], best[:, :], ALU.subtract).then_inc(s["expd"], 1)
                dve.wait_ge(s["recip"], 1)
                chain(dve.tensor_scalar(w_a[:, :], w_b[:, :], 1.0, None, ALU.add))
                chain(dve.reciprocal(w_a[:, :], w_a[:, :]))
                chain(dve.tensor_tensor(w_b[:, :], w_a[:, :], w_b[:, :], ALU.mult))
            else:
                chain(dve.memset(ones[:, :], 1.0))
                chain(dve.tensor_reduce(best[:, :], experts_inside(L), AX.X, ALU.max))
                dve.tensor_tensor(L, L, spread(best), ALU.subtract).then_inc(s["expd"], 1)
                dve.wait_ge(s["recip"], 1)
                chain(dve.tensor_reduce(w_a[:, :], experts_inside(L), AX.X, ALU.add))
                chain(dve.reciprocal(w_a[:, :], w_a[:, :]))
                chain(dve.tensor_tensor(L, L, spread(w_a), ALU.mult))
                first_largest(dve, L, RK, best[:, :], EQ, M1, chain)
                chain(dve.tensor_tensor(RS, L, M1, ALU.mult))
                chain(dve.tensor_tensor(RS, L, RS, ALU.subtract))
                first_largest(dve, RS, RK, second[:, :], EQ, M2, chain)
                dve.sem_inc(s["prefix"], 1)
                dve.wait_ge(s["hid"], 1)
                chain(dve.tensor_tensor_scan(incl[:, :], restart[:, :], hid[1][:, :], 0.0, ALU.mult, ALU.add))
                chain(dve.tensor_tensor(pos[:, :], incl[:, :], hid[1][:, :], ALU.subtract))
                chain(dve.tensor_tensor(pos[:, :], pos[:, :], hid[0][:, :], ALU.add))
                taken = eq[:, 0:EXPERTS]
                chain(dve.tensor_scalar(taken, incl[:, TILES - 1:NE:TILES], float(capacity), None, ALU.min))
                P2 = by_tile(pos[:, NE:])
                chain(dve.tensor_tensor(P2, P2, taken.unsqueeze(2).to_broadcast([P, EXPERTS, TILES]), ALU.add))
                chain(dve.scalar_tensor_tensor(masks[:, :], pos[:, :], float(capacity), masks[:, :], ALU.is_lt, ALU.mult))
                chain(dve.tensor_tensor(RS, L, M1, ALU.mult))
                chain(dve.tensor_reduce(w_a[:, :], experts_inside(RS), AX.X, ALU.add))
                chain(dve.tensor_tensor(RS, L, M2, ALU.mult))
                chain(dve.tensor_reduce(w_b[:, :], experts_inside(RS), AX.X, ALU.add))
                chain(dve.tensor_tensor(best[:, :], w_a[:, :], w_b[:, :], ALU.add))
                chain(dve.tensor_scalar(best[:, :], best[:, :], float(np.finfo(np.float32).eps), None, ALU.max))
                chain(dve.reciprocal(best[:, :], best[:, :]))
                chain(dve.tensor_tensor(w_a[:, :], w_a[:, :], best[:, :], ALU.mult))
                chain(dve.tensor_tensor(w_b[:, :], w_b[:, :], best[:, :], ALU.mult))
                chain(dve.memset(gcol[:, :], 0.1))
            chain(dve.tensor_tensor(G, M1, spread(w_a), ALU.mult))
            chain(dve.tensor_tensor(RS, M2, spread(w_b), ALU.mult))
            chain(dve.tensor_tensor(G, G, RS, ALU.add))
            dve.sem_inc(s["acc"], 2)
            dve.sem_inc(s["bias_in"], 1)

            with dve.Fori(0, CHUNKS) as i:
                dve.wait_ge(s["acc"], at(i, nexp, 2))
                dve.tensor_copy(g3[:, :, 0:EXPERTS].unsqueeze(3), by_chunk(gates[:, :])[:, :, :, bass.ds(i, 1)]
                                ).then_inc(s["gcol"], 1)
                dve.wait_ge(s["gcol"], at(i, 1, 1))
                for e in range(nexp):
                    dve.wait_ge(s["outp"], at(i, nexp, e + 1))
                    dve.wait_ge(s["acc"], at(i, nexp, e + 2))
                    for b in range(BATCH):
                        xb = xs[:, bass.ds(i * WIDE + b * P, P)]
                        last = dve.scalar_tensor_tensor(xb, outp[e % 2][:, b * P:(b + 1) * P],
                                                        gcol[:, b * nexp + e:b * nexp + e + 1], xb, ALU.mult, ALU.add)
                    last.then_inc(s["acc"], 1)
                if biased:
                    dve.wait_ge(s["bias"], at(i, 1, 1))
                    dve.wait_ge(s["acc"], at(i, nexp, nexp + 2))
                    xc = xs[:, bass.ds(i * WIDE, WIDE)]
                    dve.tensor_tensor(xc, small[:, :], xc, ALU.add).then_inc(s["bias_in"], 1)


D_IN, STATES, TAPS = 256, 16, 4
POS = 16
GC = P // POS
GROUPS = D_IN // GC
HALVES = D_IN // P
SUPER = 4
SUPERS = SEQ // (SUPER * POS)
COLS = BATCH * SUPERS
LEVELS = 6
SCANS = 4
AHEAD = 4
RMS_EPS = 1e-6


def state_space_phase(nc, xs, scratch, norm_w, win, b_in, conv_w, conv_b, a_rows_c, a_cols_b, wout, b_out,
                      ident_d, own_d):
    with ExitStack() as ctx:
        S = Scope(nc, ctx, "ssm")
        PAD = TAPS - 1
        ident, own = S.sb("ident", P), S.sb("own", GC)
        NW, WIN, BIN = S.sb("NW", 1), S.sb("WIN", D_IN), S.sb("BIN", HALVES)
        CW, CB, WOUT, BOUT = S.sb("CW", HALVES * TAPS), S.sb("CB", HALVES), S.sb("WOUT", HALVES * D), S.sb("BOUT", D)
        RB, RC, C0 = S.sb("RB", GROUPS * (16 + 64)), S.sb("RC", GROUPS * (16 + 64)), S.sb("C0", GROUPS)
        AB, AC = S.sb("AB", GROUPS * (STATES + 1)), S.sb("AC", GROUPS * (STATES + 1))
        big_a, big_b = S.sb("big_a", HALVES * BATCH * (SEQ + PAD)), S.sb("big_b", HALVES * BATCH * SEQ)
        turn_buf = S.sb("turn_buf", 2 * GROUPS * P)
        diag = S.sb("diag", GROUPS * P)
        TW = S.sb("TW", GROUPS * SUPER * POS)
        H = S.sb("H", GROUPS * BATCH * (SUPERS + 1))
        b_own = S.sb("b_own", GROUPS * GC)
        gsb = S.sb("gsb", GROUPS * (POS - 1 + 64), GC)
        hn, hT = ([S.sb(f"{n}{k}", WIDE) for k in range(2)] for n in ("hn", "hT"))
        msq, r2 = S.sb("msq", TILES), S.sb("r2", TILES)
        front = Front(S, ident)
        pb = front.turn + [S.bank(f"pb{k}") for k in range(2, 8)]

        u = big_a[:, :].rearrange("p (h b t) -> p h b t", h=HALVES, b=BATCH)
        u2 = big_a[:, 0:GROUPS * 256].rearrange("p (g c) -> p g c", g=GROUPS)
        yT = big_a[:, 0:HALVES * BATCH * SEQ].rearrange("p (h t) -> p h t", h=HALVES)
        v = big_b[:, :].rearrange("p (h b t) -> p h b t", h=HALVES, b=BATCH)
        ys = big_b[:, :].rearrange("p (g c) -> p g c", g=GROUPS)
        diagT = turn_buf[:, 0:GROUPS * P]
        tb = [turn_buf[:, k * GROUPS * P:(k + 1) * GROUPS * P] for k in range(2)]
        expB, weightX, expO, expT = ([turn_buf[:, (AHEAD * n + k) * 512:(AHEAD * n + k + 1) * 512]
                                      for k in range(AHEAD)] for n in range(4))
        rb = RB[:, :].rearrange("p (g n) -> p g n", g=GROUPS)
        rc = RC[:, :].rearrange("p (g n) -> p g n", g=GROUPS)
        h4 = H[:, :].rearrange("p (g b s) -> p g b s", g=GROUPS, b=BATCH)
        tw = TW[:, :].rearrange("p (g n) -> p g n", g=GROUPS)
        ab = AB[:, :].rearrange("p (g n) -> p g n", g=GROUPS)
        ac = AC[:, :].rearrange("p (g n) -> p g n", g=GROUPS)
        g3 = gsb[:, :].rearrange("p (g n) -> p g n", g=GROUPS)

        loads = [(ident[:, :], ident_d), (own[:, :], own_d), (AB[:, :], a_cols_b), (AC[:, :], a_rows_c), (NW[:, :], norm_w), (WIN[:, :], win),
                 (BIN[:, :], b_in), (CW[:, :], conv_w), (CB[:, :], conv_b), (WOUT[:, :], wout), (BOUT[:, :], b_out)]
        s = {n: S.sem(n) for n in ("loaded laid diag diagT lev_mm lev_out own g_mm g_out g_saved windows zeroed msq r2 hn hT "
                                   "u_mm u v0 conv1 conv2 conv3 kept t1 t1_out t2 t2_out expB xT xW x_mm x_out "
                                   "scan scanned expO expT y_mm y_out t3 t3_out t4 t4_out w_mm w_out").split()}

        def own_block(n):
            return own[:, :].unsqueeze(1).unsqueeze(3).to_broadcast([P, n, GC, 16])

        def expanded(ap):
            return ap.unsqueeze(2).to_broadcast([P, ap.shape[1], GC, 16])

        def channel_form(ap, n):
            return ap.rearrange("p (n d s) -> p n d s", n=n, d=GC)

        block = ctx.enter_context(nc.Block())
        Q = 8

        @block.sync
        def _(sp):
            for dst, src in loads:
                sp.dma_start(dst, src).then_inc(s["loaded"], 16)
            sp.wait_ge(s["g_out"], 4)
            width = POS - 1 + 64
            sp.dma_start(scratch.rearrange("(d g n) -> d g n", d=GC, g=GROUPS), g3).then_inc(s["g_saved"], 16)
            sp.wait_ge(s["g_saved"], 16)
            for d in range(GC):
                window = bass.AP(tensor=scratch.tensor, offset=scratch.offset + d * GROUPS * width,
                                 ap=[[1, POS], [width, GROUPS], [1, 64]])
                sp.dma_start(tw[d * POS:(d + 1) * POS, :, :], window).then_inc(s["windows"], 16)

        def quarter(q):
            return slice(q * Q, (q + 1) * Q)

        def counts(step, q, side):
            if step < LEVELS:
                return 4 + 8 * step + 2 * q + side + 1
            return 4 + 8 * step + (q + 1 if side else 4 + q + 1)

        @block.gpsimd
        def _(pool):
            front.inverse_deviation(pool)
            pool.wait_ge(s["laid"], 4)

            def transposed_power(k):
                for q in range(4):
                    if k:
                        pool.wait_ge(s["lev_out"], counts(k - 1, q, 1 if k <= LEVELS else 0))
                    pool.tensor_tensor(channel_form(diagT[:, q * Q * P:(q + 1) * Q * P], Q),
                                       expanded(rb[:, quarter(q), 0:16]), own_block(Q), ALU.mult).then_inc(s["diagT"], 1)

            for k in range(LEVELS):
                transposed_power(k)
            pool.wait_ge(s["msq"], 3)
            pool.tensor_tensor(r2[:, :], msq[:, :], front.mhalf[:, :], ALU.pow).then_inc(s["r2"], 1)
            with pool.Fori(0, CHUNKS // 2) as i:
                for k in range(2):
                    xc = xs[:, bass.ds(i * 2 * WIDE + k * WIDE, WIDE)]
                    pool.wait_ge(front.normal, at(i, 2, k + 1))
                    pool.wait_ge(s["hn"], at(i, 2, k + 1))
                    pool.sem_inc(front.held, 1)
                    pool.tensor_tensor(xc, xc, front.xn[k][:, :], ALU.add).then_inc(s["kept"], 1)
                    pool.wait_ge(s["kept"], at(i, 4, 2 * k + 1))
                    pool.sem_inc(front.held, 1)
                    pool.tensor_tensor(wide(xc), wide(xc), BOUT[:, :].unsqueeze(1).to_broadcast([P, BATCH, D]),
                                       ALU.add).then_inc(s["kept"], 1)
            pool.wait_ge(s["x_out"], GROUPS + AHEAD)
            for k in range(LEVELS, LEVELS + SCANS - 1):
                transposed_power(k)
            pool.wait_ge(s["windows"], 16 * GC)
            with pool.Fori(0, GROUPS // AHEAD) as i:
                for k in range(AHEAD):
                    pool.wait_ge(s["y_mm"], at(i, AHEAD, k + 1))
                    pool.sem_inc(front.held, 1)
                    pool.tensor_tensor(channel_form(expT[k], SUPER),
                                       expanded(TW[:, bass.ds(i * AHEAD * 64 + k * 64, 64)]
                                                .rearrange("p (n s) -> p n s", n=SUPER)),
                                       own_block(SUPER), ALU.mult).then_inc(s["expT"], 1)

        @block.tensor
        def _(pe):
            pe.wait_ge(s["loaded"], 16 * len(loads))

            def power_batch(k, q, side):
                weights, vectors, bank = ((diag, rb, pb[q]), (diagT, rc, pb[4 + q]))[side]
                for g in range(q * Q, (q + 1) * Q):
                    mm = pe.matmul(bank[:, (g % Q) * 64:(g % Q + 1) * 64], weights[:, g * P:(g + 1) * P],
                                   vectors[:, g, 0:64], start=True, stop=True)
                mm.then_inc(s["lev_mm"], 1)

            for q in range(4):
                pe.wait_ge(s["diagT"], q + 1)
                for g in range(q * Q, (q + 1) * Q):
                    mm = pe.matmul(pb[q][:, g % Q:g % Q + 1], diagT[:, g * P:(g + 1) * P], C0[:, g:g + 1],
                                   start=True, stop=True)
                mm.then_inc(s["lev_mm"], 1)
            for k in range(LEVELS):
                for q in range(4):
                    pe.wait_ge(s["diag"], 4 * k + q + 1)
                    if k == 0:
                        pe.wait_ge(s["lev_out"], q + 1)
                    power_batch(k, q, 0)
                    pe.wait_ge(s["diagT"], 4 * k + q + 1)
                    power_batch(k, q, 1)
            pe.wait_ge(s["own"], 1)
            for q in range(4):
                pe.wait_ge(s["lev_out"], counts(LEVELS - 1, 3, 1))
                for g in range(q * Q, (q + 1) * Q):
                    weights = b_own[:, g * GC:(g + 1) * GC]
                    pe.matmul(pb[q][0:GC, (g % Q) * 64:(g % Q) * 64 + 1], weights, C0[:, g:g + 1], start=True, stop=True)
                    mm = pe.matmul(pb[q][0:GC, (g % Q) * 64 + 1:(g % Q + 1) * 64], weights, rc[:, g, 16:79],
                                   start=True, stop=True)
                mm.then_inc(s["g_mm"], 1)

            def columns(i, k):
                pe.wait_ge(s["hn"], i + 1)
                for b in range(BATCH):
                    mm = pe.transpose(front.turn[k][:, b * P:(b + 1) * P], hn[k][:, b * P:(b + 1) * P], ident[:, :])
                mm.then_inc(front.turned, 1)

            def input_product(i, k):
                pe.wait_ge(s["hT"], i + 1)
                for h in range(HALVES):
                    pe.wait_ge(s["u"], i * 2 + h + 1)
                    pe.matmul(pb[4 + h][:, :], WIN[:, h * P:(h + 1) * P], hT[k][:, :], start=True,
                              stop=True).then_inc(s["u_mm"], 1)

            pe.wait_ge(s["g_out"], 4)
            columns(0, 0)
            with pe.Fori(0, CHUNKS // 2 - 1) as i:
                columns(i * 2 + 1, 1)
                input_product(i * 2, 0)
                columns(i * 2 + 2, 0)
                input_product(i * 2 + 1, 1)
            columns(CHUNKS - 1, 1)
            input_product(CHUNKS - 2, 0)
            input_product(CHUNKS - 1, 1)

            pe.wait_ge(s["conv3"], HALVES * CHUNKS)
            v_blocks = big_b[:, :].rearrange("p (h c j) -> p h j c", h=HALVES, j=POS)
            n1 = n2 = 0
            for mh in range(2):
                for h in range(HALVES):
                    for jq in range(4):
                        if n1 >= 4:
                            pe.wait_ge(s["t1_out"], n1 - 3)
                        for k in range(4):
                            mm = pe.transpose(pb[n1 % 4][:, k * P:(k + 1) * P],
                                              v_blocks[:, h, 4 * jq + 3 - k, mh * P:(mh + 1) * P], ident[:, :])
                        mm.then_inc(s["t1"], 1)
                        n1 += 1
            for mh in range(2):
                for gq in range(GROUPS // 4):
                    pe.wait_ge(s["t1_out"], 8 * (mh + 1))
                    if n2 >= 4:
                        pe.wait_ge(s["t2_out"], n2 - 3)
                    for k in range(4):
                        g = 4 * gq + k
                        mm = pe.transpose(pb[4 + n2 % 4][:, k * P:(k + 1) * P], tb[mh][:, g * P:(g + 1) * P], ident[:, :])
                    mm.then_inc(s["t2"], 1)
                    n2 += 1

            pe.wait_ge(s["t2_out"], n2)
            with pe.Fori(0, GROUPS // AHEAD) as i:
                for k in range(AHEAD):
                    pe.wait_ge(s["expB"], at(i, AHEAD, k + 1))
                    pe.wait_ge(s["xW"], at(i, AHEAD, k + 1))
                    for m in range(SUPER):
                        mm = pe.transpose(pb[k][:, m * P:(m + 1) * P], expB[k][:, m * P:(m + 1) * P], ident[:, :])
                    mm.then_inc(s["xT"], 1)
                for k in range(AHEAD):
                    pe.wait_ge(s["xW"], at(i, AHEAD, AHEAD + k + 1))
                    pe.wait_ge(s["x_out"], at(i, AHEAD, k + 1))
                    for m in range(SUPER):
                        r = SUPER - 1 - m
                        mm = pe.matmul(pb[4 + k][:, 0:COLS], weightX[k][:, r * P:(r + 1) * P],
                                       big_a[:, bass.ds(i * AHEAD * 256 + k * 256 + m * COLS, COLS)],
                                       start=(m == 0), stop=(m == SUPER - 1))
                    mm.then_inc(s["x_mm"], 1)

            pe.wait_ge(s["x_out"], GROUPS + AHEAD)
            for j in range(SCANS):
                k = LEVELS + j
                n = SUPERS - 2 ** j
                for q in range(4):
                    pe.wait_ge(s["diag"], 4 * k + q + 1)
                    for g in range(q * Q, (q + 1) * Q):
                        mm = pe.matmul(pb[q][:, (g % Q) * BATCH * n:(g % Q + 1) * BATCH * n], diag[:, g * P:(g + 1) * P],
                                       h4[:, g, :, 1:1 + n], start=True, stop=True)
                    mm.then_inc(s["scan"], 1)
                    if j < SCANS - 1:
                        pe.wait_ge(s["diagT"], 4 * k + q + 1)
                        power_batch(k, q, 1)
                if j < SCANS - 2:
                    for q in range(4):
                        pe.wait_ge(s["scanned"], 4 * j + q + 1)
                        power_batch(k, q, 0)

            pe.wait_ge(s["scanned"], 4 * SCANS)
            with pe.Fori(0, GROUPS // AHEAD) as i:
                for k in range(AHEAD):
                    pe.wait_ge(s["expT"], at(i, AHEAD, k + 1))
                    pe.wait_ge(s["y_out"], at(i, AHEAD, k + 1))
                    for m in range(SUPER):
                        n = (SUPER - m) * COLS
                        pe.matmul(pb[k][:, m * COLS:SUPER * COLS], expT[k][:, m * P:(m + 1) * P],
                                  big_a[:, bass.ds(i * AHEAD * 256 + k * 256, n)], start=(m == 0), stop=False,
                                  skip_group_check=True)
                    pe.wait_ge(s["expO"], at(i, AHEAD, k + 1))
                    for m in range(SUPER):
                        mm = pe.matmul(pb[k][:, m * COLS:(m + 1) * COLS], expO[k][:, m * P:(m + 1) * P],
                                       h4[:, bass.ds(i * AHEAD + k, 1), :, 0:SUPERS].rearrange("p g b s -> p (g b) s"),
                                       start=False, stop=(m == SUPER - 1), skip_group_check=True)
                    mm.then_inc(s["y_mm"], 1)

            pe.wait_ge(s["y_out"], GROUPS + AHEAD)
            n3 = n4 = 0
            for mh in range(2):
                for gq in range(GROUPS // 4):
                    if n3 >= 4:
                        pe.wait_ge(s["t3_out"], n3 - 3)
                    for k in range(4):
                        mm = pe.transpose(pb[n3 % 4][:, k * P:(k + 1) * P],
                                          ys[:, 4 * gq + k, mh * P:(mh + 1) * P], ident[:, :])
                    mm.then_inc(s["t3"], 1)
                    n3 += 1
            for mh in range(2):
                rows = tb[mh].rearrange("p (h d j) -> p h j d", h=HALVES, j=POS)
                pe.wait_ge(s["t3_out"], 8 * (mh + 1))
                for h in range(HALVES):
                    for jq in range(4):
                        if n4 >= 4:
                            pe.wait_ge(s["t4_out"], n4 - 3)
                        for k in range(4):
                            mm = pe.transpose(pb[4 + n4 % 4][:, k * P:(k + 1) * P], rows[:, h, 4 * jq + k, :], ident[:, :])
                        mm.then_inc(s["t4"], 1)
                        n4 += 1
            pe.wait_ge(s["t4_out"], n4)
            for c in range(CHUNKS):
                if c >= 2:
                    pe.wait_ge(s["w_out"], c - 1)
                for b in range(BATCH):
                    t0 = b * SEQ + c * P
                    for h in range(HALVES):
                        mm = pe.matmul(pb[c % 2][:, b * P:(b + 1) * P], yT[:, h, t0:t0 + P],
                                       WOUT[:, h * D:(h + 1) * D], start=(h == 0), stop=(h == HALVES - 1))
                mm.then_inc(s["w_mm"], 1)

        @block.scalar
        def _(act):
            act.wait_ge(s["laid"], 4)
            for q in range(4):
                act.wait_ge(s["lev_mm"], q + 1)
                act.activation(rc[:, quarter(q), 16:17], pb[q][:, 0:Q].unsqueeze(2), ACT.Copy).then_inc(s["lev_out"], 1)

            def squared(k, q, side):
                n = 2 ** k if k < LEVELS else 0
                act.wait_ge(s["lev_mm"], counts(k, q, side))
                act.wait_ge(s["diagT"] if side == 0 else s["diag"], 4 * k + q + 1)
                dst, bank = (rb, pb[q]) if side == 0 else (rc, pb[4 + q])
                first = 16 + n
                src = bank[:, :].rearrange("p (g n) -> p g n", g=Q)
                if n:
                    act.activation(dst[:, quarter(q), first:first + n], src[:, :, 16:16 + n], ACT.Copy)
                act.activation(dst[:, quarter(q), 0:16], src[:, :, 0:16], ACT.Copy).then_inc(s["lev_out"], 1)

            for k in range(LEVELS):
                for q in range(4):
                    squared(k, q, 0)
                    squared(k, q, 1)
            act.wait_ge(s["zeroed"], 3)
            for q in range(4):
                act.wait_ge(s["g_mm"], q + 1)
                act.activation(g3[:, quarter(q), POS - 1:],
                               pb[q][0:GC, :].rearrange("p (g n) -> p g n", g=Q), ACT.Copy).then_inc(s["g_out"], 1)

            def columns(i, k):
                act.wait_ge(front.turned, i + 1)
                act.wait_ge(s["u_mm"], i * 2 + 2)
                act.activation(hT[k][:, :], front.turn[k][:, :], ACT.Copy, scale=NW[:, 0:1]).then_inc(s["hT"], 1)

            def channels(i):
                for h in range(HALVES):
                    act.wait_ge(s["u_mm"], i * 2 + h + 5)
                    act.activation(u[:, h, :, bass.ds(i * P + PAD, P)], wide(pb[4 + h][:, :]), ACT.Identity,
                                   bias=BIN[:, h:h + 1]).then_inc(s["u"], 1)
                for h in range(HALVES):
                    act.wait_ge(s["u"], i * 2 + h + 3)
                    act.activation(v[:, h, :, bass.ds(i * P, P)], u[:, h, :, bass.ds(i * P + PAD, P)], ACT.Identity,
                                   bias=CB[:, h:h + 1], scale=CW[:, h * TAPS + PAD:h * TAPS + PAD + 1]
                                   ).then_inc(s["v0"], 1)

            act.sem_inc(s["u"], 2)
            act.sem_inc(s["u_mm"], 4)
            columns(0, 0)
            with act.Fori(0, CHUNKS // 2 - 1) as i:
                columns(i * 2 + 1, 1)
                channels(i * 2)
                columns(i * 2 + 2, 0)
                channels(i * 2 + 1)
            columns(CHUNKS - 1, 1)
            channels(CHUNKS - 2)
            channels(CHUNKS - 1)

            n1 = 0
            for mh in range(2):
                for h in range(HALVES):
                    for jq in range(4):
                        act.wait_ge(s["t1"], n1 + 1)
                        dst = tb[mh].rearrange("p (h d j) -> p h j d", h=HALVES, j=POS)[:, h, 12 - 4 * jq:16 - 4 * jq, :]
                        act.activation(dst, wide(pb[n1 % 4][:, :], 4), ACT.Copy).then_inc(s["t1_out"], 1)
                        n1 += 1

            act.sem_inc(s["xW"], AHEAD)
            with act.Fori(0, GROUPS // AHEAD) as i:
                for k in range(AHEAD):
                    act.wait_ge(s["xT"], at(i, AHEAD, AHEAD + k + 1))
                    act.wait_ge(s["x_mm"], at(i, AHEAD, k + 1))
                    act.activation(weightX[k], pb[k][:, :], ACT.Copy).then_inc(s["xW"], 1)
            for k in range(LEVELS, LEVELS + SCANS - 1):
                for q in range(4):
                    squared(k, q, 1)
                for q in range(4):
                    if k < LEVELS + SCANS - 2:
                        squared(k, q, 0)
            act.sem_inc(s["y_out"], AHEAD)
            with act.Fori(0, GROUPS // AHEAD) as i:
                for k in range(AHEAD):
                    act.wait_ge(s["y_mm"], at(i, AHEAD, AHEAD + k + 1))
                    act.activation(big_b[:, bass.ds(i * AHEAD * 256 + k * 256, 256)].rearrange("p (c m) -> p m c", m=SUPER),
                                   pb[k][:, 0:256].rearrange("p (m c) -> p m c", m=SUPER), ACT.Copy
                                   ).then_inc(s["y_out"], 1)
            n4 = 0
            for mh in range(2):
                for h in range(HALVES):
                    for jq in range(4):
                        act.wait_ge(s["t4"], n4 + 1)
                        dst = yT[:, h, :].rearrange("p (c j) -> p j c", j=POS)[
                            :, 4 * jq:4 * jq + 4, mh * P:(mh + 1) * P]
                        act.activation(dst, wide(pb[4 + n4 % 4][:, :], 4), ACT.Copy
                                       ).then_inc(s["t4_out"], 1)
                        n4 += 1

        @block.vector
        def _(dve):
            dve.memset(gsb[:, :], 0.0).then_inc(s["zeroed"], 1)
            dve.memset(H[:, :], 0.0).then_inc(s["zeroed"], 1)
            dve.memset(u[:, :, :, 0:PAD], 0.0).then_inc(s["zeroed"], 1)
            dve.memset(rb[:, :, 16:64], 0.0).then_inc(s["zeroed"], 1)
            dve.memset(rc[:, :, 16:64], 0.0).then_inc(s["zeroed"], 1)
            dve.wait_ge(s["zeroed"], 5)
            dve.wait_ge(s["loaded"], 16 * len(loads))
            dve.tensor_copy(rb[:, :, 0:17], ab).then_inc(s["laid"], 1)
            dve.tensor_copy(rc[:, :, 0:16], ac[:, :, 0:16]).then_inc(s["laid"], 1)
            dve.tensor_copy(C0[:, :].unsqueeze(2), ac[:, :, 16:17]).then_inc(s["laid"], 1)
            dve.tensor_tensor(b_own[:, :].rearrange("p (g d) -> p g d", g=GROUPS),
                              ab[:, :, 16:17].to_broadcast([P, GROUPS, GC]),
                              own[:, :].unsqueeze(1).to_broadcast([P, GROUPS, GC]), ALU.mult).then_inc(s["own"], 1)
            dve.wait_ge(s["laid"], 3)
            dve.sem_inc(s["laid"], 1)

            def power(k, finished):
                for q in range(4):
                    finished(q)
                    dve.tensor_tensor(channel_form(diag[:, q * Q * P:(q + 1) * Q * P], Q), expanded(rc[:, quarter(q), 0:16]),
                                      own_block(Q), ALU.mult).then_inc(s["diag"], 1)

            power(0, lambda q: None)
            front.moments_of(dve, xs)
            dve.tensor_tensor(msq[:, :], front.var[:, :], front.rstd[:, :], ALU.mult).then_inc(s["msq"], 1)
            dve.wait_ge(s["msq"], 1)
            dve.tensor_tensor(msq[:, :], msq[:, :], front.rstd[:, :], ALU.mult).then_inc(s["msq"], 1)
            dve.wait_ge(s["msq"], 2)
            dve.tensor_scalar(msq[:, :], msq[:, :], RMS_EPS, None, ALU.add).then_inc(s["msq"], 1)
            for k in range(1, LEVELS + 1):
                power(k, lambda q: dve.wait_ge(s["lev_out"], counts(k - 1, q, 1)))
            dve.wait_ge(s["r2"], 1)

            def tokens(i, k):
                front.normalize(dve, xs, i, k)
                dve.wait_ge(front.normal, i + 1)
                for b in range(BATCH):
                    last = dve.tensor_scalar(hn[k][:, b * P:(b + 1) * P], front.xn[k][:, b * P:(b + 1) * P],
                                             r2[:, bass.ds(i * BATCH + b, 1)], None, ALU.mult)
                last.then_inc(s["hn"], 1)

            def convolved(i):
                for tap, before, after in ((2, "v0", "conv1"), (1, "conv1", "conv2"), (0, "conv2", "conv3")):
                    for h in range(HALVES):
                        dve.wait_ge(s[before], i * 2 + h + 1)
                        out = v[:, h, :, bass.ds(i * P, P)]
                        dve.scalar_tensor_tensor(out, u[:, h, :, bass.ds(i * P + tap, P)],
                                                 CW[:, h * TAPS + tap:h * TAPS + tap + 1], out, ALU.mult,
                                                 ALU.add).then_inc(s[after], 1)

            tokens(0, 0)
            tokens(1, 1)
            with dve.Fori(0, CHUNKS // 2 - 1) as i:
                for k in range(2):
                    convolved(i * 2 + k)
                    dve.wait_ge(s["kept"], at(i, 4, 2 * k + 1))
                    tokens(i * 2 + 2 + k, k)
            convolved(CHUNKS - 2)
            convolved(CHUNKS - 1)

            n2 = 0
            for mh in range(2):
                for gq in range(GROUPS // 4):
                    dve.wait_ge(s["t2"], n2 + 1)
                    dve.tensor_copy(u2[:, 4 * gq:4 * gq + 4, :].rearrange("p g (m c) -> p g c m", m=SUPER)[
                                        :, :, mh * COLS // 2:(mh + 1) * COLS // 2, :],
                                    pb[4 + n2 % 4][:, :].rearrange("p (g c m) -> p g c m", g=4, m=SUPER)
                                    ).then_inc(s["t2_out"], 1)
                    n2 += 1

            dve.sem_inc(s["xT"], AHEAD)
            dve.sem_inc(s["x_mm"], AHEAD)
            dve.sem_inc(s["x_out"], AHEAD)
            dve.wait_ge(s["t2_out"], n2)
            with dve.Fori(0, GROUPS // AHEAD) as i:
                for k in range(AHEAD):
                    dve.wait_ge(s["xT"], at(i, AHEAD, k + 1))
                    dve.tensor_tensor(channel_form(expB[k], SUPER),
                                      expanded(rb[:, bass.ds(i * AHEAD + k, 1), 16:80]
                                               .rearrange("p g (n s) -> p (g n) s", n=SUPER)),
                                      own_block(SUPER), ALU.mult).then_inc(s["expB"], 1)
                for k in range(AHEAD):
                    dve.wait_ge(s["x_mm"], at(i, AHEAD, AHEAD + k + 1))
                    dve.tensor_copy(h4[:, bass.ds(i * AHEAD + k, 1), :, 1:SUPERS + 1].rearrange("p g b s -> p (g b) s"),
                                    pb[4 + k][:, 0:COLS].rearrange("p (b s) -> p b s", b=BATCH)).then_inc(s["x_out"], 1)

            dve.wait_ge(s["x_out"], GROUPS + AHEAD)
            for j in range(SCANS):
                reach = 2 ** j
                n = SUPERS - reach
                for q in range(4):
                    dve.wait_ge(s["scan"], 4 * j + q + 1)
                    ends = h4[:, quarter(q), :, 1 + reach:1 + SUPERS].rearrange("p g b s -> p (g b) s")
                    dve.tensor_tensor(ends, pb[q][:, 0:Q * BATCH * n].rearrange("p (c s) -> p c s", s=n), ends,
                                      ALU.add).then_inc(s["scanned"], 1)
                if j < SCANS - 1:
                    power(LEVELS + j + 1, lambda q: dve.wait_ge(
                        s["lev_out"], counts(LEVELS + j, q, 0 if j < SCANS - 2 else 1)))

            dve.sem_inc(s["y_mm"], AHEAD)
            with dve.Fori(0, GROUPS // AHEAD) as i:
                for k in range(AHEAD):
                    dve.wait_ge(s["y_mm"], at(i, AHEAD, k + 1))
                    dve.tensor_tensor(channel_form(expO[k], SUPER),
                                      expanded(rc[:, bass.ds(i * AHEAD + k, 1), 16:80]
                                               .rearrange("p g (n s) -> p (g n) s", n=SUPER)),
                                      own_block(SUPER), ALU.mult).then_inc(s["expO"], 1)

            n3 = 0
            for mh in range(2):
                for gq in range(GROUPS // 4):
                    dve.wait_ge(s["t3"], n3 + 1)
                    dve.tensor_copy(tb[mh][:, gq * 512:(gq + 1) * 512], pb[n3 % 4][:, :]).then_inc(s["t3_out"], 1)
                    n3 += 1
            for c in range(CHUNKS):
                dve.wait_ge(s["w_mm"], c + 1)
                xc = xs[:, c * WIDE:(c + 1) * WIDE]
                dve.tensor_tensor(xc, pb[c % 2][:, :], xc, ALU.add).then_inc(s["w_out"], 1)


def store_phase(nc, xs, out):
    with ExitStack() as ctx:
        S = Scope(nc, ctx, "store")
        stored = S.sem("stored")
        block = ctx.enter_context(nc.Block())
        out_view = out.rearrange("b (c p) f -> p c b f", p=P)

        @block.sync
        def _(sp):
            for c in range(CHUNKS):
                sp.dma_start(out_view[:, c], xs[:, c * WIDE:(c + 1) * WIDE].rearrange("p (b f) -> p b f", b=BATCH)
                             ).then_inc(stored, 16)
            sp.wait_ge(stored, 16 * CHUNKS)


def build(nc, t, out):
    with ExitStack() as ctx:
        xs = ctx.enter_context(nc.sbuf_tensor("xs", [P, CHUNKS * WIDE], F32))
        attention_phase(nc, xs, t["x"], t["wq"], t["wk"], t["wv"], t["wg"], t["bg"], t["wo"], t["decay_all"],
                        t["decay_pair"], t["ident"], t["lag"], t["causal"], t["tpos"], t["left"])
        mixture_phase(nc, xs, "moe0", HID0, ACT.Gelu, None, t["router0"], t["m0w1"], t["m0w2"], t["ident"], t["rank"])
        scratch = nc.dram_tensor("responses", (GC * GROUPS * (POS - 1 + 64),), F32, kind="Internal").ap()
        state_space_phase(nc, xs, scratch, t["norm_w"], t["win"], t["b_in"], t["conv_w"], t["conv_b"], t["a_rows_c"],
                          t["a_cols_b"], t["wout"], t["b_out"], t["ident"], t["own"])
        mixture_phase(nc, xs, "moe1", HID1, ACT.Silu, CAPACITY, t["router1"], t["m1w1"], t["m1w2"], t["ident"], t["rank"],
                      t["m1b1"], t["m1b2"], t["before"], t["restart"])
        store_phase(nc, xs, out)


def laid_out(i):
    def T(w):
        return np.ascontiguousarray(np.swapaxes(w, -1, -2))

    def pair_rows(w, n):
        return np.ascontiguousarray(w.reshape(n, P, -1).transpose(1, 0, 2).reshape(P, -1))

    def by_group(matrices, vectors):
        both = np.concatenate([matrices, vectors.reshape(D_IN, STATES, 1)], axis=2)
        return np.ascontiguousarray(both.reshape(GROUPS, P, STATES + 1).transpose(1, 0, 2))

    a = {k: np.asarray(v) for k, v in i.items()}
    dl = a["L0_attn_decay_log"]
    s_, t_ = np.meshgrid(np.arange(P), np.arange(P), indexing="ij")
    return {
        "x": a["L0_attn_x"],
        "wq": T(a["L0_attn_W_Q"]), "wk": T(a["L0_attn_W_K"]), "wv": T(a["L0_attn_W_V"]), "wg": T(a["L0_attn_W_g_w"]),
        "bg": T(a["L0_attn_W_g_b"].reshape(PAIRS, P)), "wo": pair_rows(T(a["L0_attn_W_O"]), PAIRS),
        "decay_all": np.ascontiguousarray(np.broadcast_to(dl[None], (P, HEADS))),
        "decay_pair": T(np.repeat(dl.reshape(PAIRS, 2), DK, axis=1)),
        "ident": np.eye(P, dtype=np.float32),
        "lag": np.maximum(t_ - s_, 0).astype(np.float32), "causal": (t_ >= s_).astype(np.float32),
        "tpos": np.broadcast_to(np.arange(1, P + 1, dtype=np.float32), (P, P)).copy(),
        "norm_w": a["L1_attn_norm_w"].reshape(D, 1), "win": a["L1_attn_Win"],
        "b_in": T(a["L1_attn_b_in"].reshape(HALVES, P)), "conv_b": T(a["L1_attn_conv_b"].reshape(HALVES, P)),
        "conv_w": pair_rows(a["L1_attn_conv_w"].reshape(D_IN, TAPS), HALVES),
        "a_rows_c": by_group(a["L1_attn_A"], a["L1_attn_Cm"]), "a_cols_b": by_group(T(a["L1_attn_A"]), a["L1_attn_Bm"]),
        "wout": pair_rows(a["L1_attn_Wout"], HALVES),
        "b_out": np.broadcast_to(a["L1_attn_b_out"][None], (P, D)).copy(),
        "own": np.repeat(np.eye(GC, dtype=np.float32), POS, axis=0),
        "router0": T(a["L0_ffn_router_w"]), "m0w1": T(a["L0_ffn_w1"].reshape(-1, D)),
        "m0w2": pair_rows(T(a["L0_ffn_w2"]).reshape(-1, D), EXPERTS * HID0 // P),
        "router1": a["L1_ffn_router_w"],
        "m1w1": pair_rows(np.concatenate([a["L1_ffn_w1"], a["L1_ffn_sw1"][None]]).reshape(-1, HID1), EXPERTS + 1),
        "m1w2": pair_rows(np.concatenate([a["L1_ffn_w2"], a["L1_ffn_sw2"][None]]).reshape(-1, D),
                          (EXPERTS + 1) * HID1 // P),
        "m1b1": T(np.concatenate([a["L1_ffn_b1"], a["L1_ffn_sb1"][None]]).reshape(-1, P)),
        "m1b2": np.concatenate([a["L1_ffn_b2"], a["L1_ffn_sb2"][None]]),
        "rank": np.broadcast_to(np.repeat(np.arange(EXPERTS, 0, -1), TILES).astype(np.float32),
                                (P, EXPERTS * TILES)).copy(),
        "before": (s_ < t_).astype(np.float32),
        "restart": np.broadcast_to((np.arange(2 * EXPERTS * TILES) % TILES != 0).astype(np.float32),
                                   (P, 2 * EXPERTS * TILES)).copy(),
        "left": np.arange(P - 1, -1, -1, dtype=np.float32).reshape(P, 1),
    }


def kernel(**inputs):
    import concourse.bacc as bacc
    from concourse.bass_utils import run_bass_kernel_spmd

    nc = bacc.Bacc("TRN2", target_bir_lowering=False, num_devices=1)
    arrays = laid_out(inputs)
    t = {n: nc.dram_tensor(n, a.shape, mybir.dt.from_np(a.dtype), kind="ExternalInput").ap()
         for n, a in arrays.items()}
    out = nc.dram_tensor("out", (BATCH, SEQ, D), F32, kind="ExternalOutput").ap()
    build(nc, t, out)
    r = run_bass_kernel_spmd(nc, [arrays], core_ids=[0])
    return r.results[0]["out"]
```

```python
from contextlib import ExitStack

import numpy as np
import concourse.bass as bass
from concourse import mybir

F32 = mybir.dt.float32
U32 = mybir.dt.uint32
ALU = mybir.AluOpType
ACT = mybir.ActivationFunctionType
AX = mybir.AxisListType

P = 128
BATCH, SEQ, D = 4, 1024, 128
CHUNKS = SEQ // P
WIDE = BATCH * P
HEADS, DK = 8, 64
HD = HEADS * DK
PAIRS = HEADS // 2
LN_EPS = 1e-5
DEN_EPS = 1e-6


EARLY = 2
PROJECTIONS = [(w, p) for p in range(PAIRS) for w in "qkv"] + [("g", p) for p in range(PAIRS)]


def at(i, per_turn, k):
    return i * per_turn + k


def wide(ap, n=BATCH):
    return ap.rearrange("p (b f) -> p b f", b=n)


class Scope:

    def __init__(self, nc, ctx, name):
        self.nc, self.ctx, self.name = nc, ctx, name

    def sb(self, name, cols, parts=P):
        return self.ctx.enter_context(self.nc.sbuf_tensor(f"{self.name}_{name}", [parts, cols], F32))

    def bank(self, name):
        return self.ctx.enter_context(self.nc.psum_tensor(f"{self.name}_{name}", [P, 512], F32))

    def sem(self, name):
        return self.ctx.enter_context(self.nc.semaphore(f"{self.name}_{name}"))


TILES = BATCH * CHUNKS


class Statistics:

    def __init__(self, S):
        self.stats = S.sb("stats", 6 * TILES)
        self.mean, self.var, self.vpe, self.rstd, self.mhalf, self.apart = (
            S.sb(n, TILES) for n in "mean var vpe rstd mhalf apart".split())

    def of_chunk(self, dve, xs, i):
        for b in range(BATCH):
            last = dve.bn_stats(self.stats[:, bass.ds(i * 6 * BATCH + 6 * b, 6)], xs[:, bass.ds(i * WIDE + b * P, P)])
        return last


class Front:

    def __init__(self, S, ident, of, turns=2):
        self.ident, self.of = ident, of
        self.xn = [S.sb(f"xn{k}", WIDE) for k in range(turns)]
        self.turn = [S.bank(f"turn{k}") for k in range(turns)]
        self.filled, self.moments, self.rstd_ready, self.normal, self.turned, self.held = (
            S.sem(n) for n in "filled moments rstd_ready normal turned held".split())

    def inverse_deviation(self, pool, parts=(slice(0, 2 * BATCH), slice(2 * BATCH, TILES))):
        pool.memset(self.of.mhalf[:, :], -0.5).then_inc(self.filled, 1)
        pool.wait_ge(self.filled, 1)
        for tiles in parts:
            self.power(pool, 0, tiles)

    def power(self, pool, n, tiles):
        pool.wait_ge(self.moments, at(n, 7, 7))
        pool.sem_inc(self.held, 1)
        pool.tensor_tensor(self.of.rstd[:, tiles], self.of.vpe[:, tiles], self.of.mhalf[:, tiles], ALU.pow
                           ).then_inc(self.rstd_ready, 1)

    def moments_of(self, dve, n=0, tiles=slice(0, TILES)):
        mean, var, vpe, apart = (t[:, tiles] for t in (self.of.mean, self.of.var, self.of.vpe, self.of.apart))
        by_tile = self.of.stats[:, :].rearrange("p (t s) -> p t s", s=6)
        mean_even, var_even, mean_odd, var_odd = (by_tile[:, tiles, k] for k in (1, 2, 4, 5))
        dve.tensor_tensor(apart, mean_even, mean_odd, ALU.subtract).then_inc(self.moments, 1)
        dve.tensor_tensor(mean, mean_even, mean_odd, ALU.add).then_inc(self.moments, 1)
        dve.tensor_tensor(var, var_even, var_odd, ALU.add).then_inc(self.moments, 1)
        dve.wait_ge(self.moments, at(n, 7, 3))
        dve.scalar_tensor_tensor(apart, apart, 0.25, apart, ALU.mult, ALU.mult).then_inc(self.moments, 1)
        dve.tensor_scalar(mean, mean, 0.5, None, ALU.mult).then_inc(self.moments, 1)
        dve.wait_ge(self.moments, at(n, 7, 5))
        dve.scalar_tensor_tensor(var, var, 1.0 / D, apart, ALU.mult, ALU.add).then_inc(self.moments, 1)
        dve.wait_ge(self.moments, at(n, 7, 6))
        dve.tensor_scalar(vpe, var, LN_EPS, None, ALU.add).then_inc(self.moments, 1)

    def normalize(self, dve, xs, i, k):
        for b in range(BATCH):
            last = dve.tensor_scalar(self.xn[k][:, b * P:(b + 1) * P], xs[:, bass.ds(i * WIDE + b * P, P)],
                                     self.of.mean[:, bass.ds(i * BATCH + b, 1)], self.of.rstd[:, bass.ds(i * BATCH + b, 1)],
                                     ALU.subtract, ALU.mult)
        last.then_inc(self.normal, 1)

    def transpose(self, pe, i, k):
        pe.wait_ge(self.normal, i + 1)
        for b in range(BATCH):
            mm = pe.transpose(self.turn[k][:, b * P:(b + 1) * P], self.xn[k][:, b * P:(b + 1) * P], self.ident[:, :])
        mm.then_inc(self.turned, 1)


def attention_phase(nc, xs, of, x, wq, wk, wv, wg, bg, wo, decay_all, decay_pair, ident_d, lag_d, causal_d, tpos_d, left_d,
                    cleared):
    with ExitStack() as ctx:
        S = Scope(nc, ctx, "attn")
        ident, lag, causal, tpos = S.sb("ident", P), S.sb("lag", P), S.sb("causal", P), S.sb("tpos", P)
        left = S.sb("left", 1)
        WQ, WK, WV, WG, WO = (S.sb(n, HD) for n in ("WQ", "WK", "WV", "WG", "WO"))
        half_bg, bgc = S.sb("half_bg", PAIRS), S.sb("bgc", PAIRS)
        dl = S.sb("dl", HEADS + PAIRS)
        tmp, lg = S.sb("tmp", HEADS + PAIRS), S.sb("lg", HEADS + PAIRS)
        mask = S.sb("mask", HEADS * P)
        qpow = S.sb("qpow", PAIRS * P)
        kpow = S.sb("kpow", HEADS)
        gchunk = S.sb("gchunk", PAIRS)
        xT = S.sb("xT", WIDE)
        e = [S.sb(f"e{k}", WIDE) for k in range(2)]
        r = [S.sb(f"r{k}", WIDE) for k in range(2)]
        qT, kT, qd, gate = (S.sb(n, PAIRS * WIDE) for n in ("qT", "kT", "qd", "gate"))
        kd = S.sb("kd", BATCH * HD)
        v1 = S.sb("v1", BATCH * HEADS * (DK + 1))
        a = [S.sb(f"a{k}", WIDE) for k in range(4)]
        state = S.sb("state", PAIRS * BATCH * 2 * (DK + 1))
        den, rden = S.sb("den", BATCH), S.sb("rden", BATCH)
        y, yT = S.sb("y", BATCH * HD), S.sb("yT", PAIRS * WIDE)
        proj = [S.bank(f"proj{k}") for k in range(2)]
        score = [S.bank(f"score{k}") for k in range(2)]
        av = [S.bank(f"av{k}") for k in range(2)]
        front = Front(S, ident, of, 1)
        turn, stp = front.turn[0], S.bank("stp")

        into = proj + av
        names = ("loaded tables_in first_in x_loaded stat neg_abs exped logged lg_ready tables gmul xT proj "
                 "zeroed cleared exp phi gate v ktr kd qd score a av den rden y stp state ytr yT out res").split()
        s = {n: S.sem(n) for n in names}
        x_view = x.rearrange("b (c p) f -> p c b f", p=P)
        cleared_views = [q.rearrange("(p r) f -> p (r f)", p=P) for q in cleared]
        CLEAR = cleared_views[0].shape[1] // CHUNKS
        zero = S.sb("zero", CLEAR)
        v4 = v1[:, :].rearrange("p (b h j) -> p b h j", b=BATCH, h=HEADS)
        y3, kd3 = wide(y[:, :]), wide(kd[:, :])
        st5 = state[:, :].rearrange("p (q b h j) -> p q b h j", q=PAIRS, b=BATCH, h=2)
        NSETUP = 14
        NTABLES, NWEIGHTS = 8, 5

        block = ctx.enter_context(nc.Block())

        @block.sync
        def _(sp):
            for c in range(CHUNKS):
                if c == 1:
                    sp.wait_ge(s["loaded"], 16 * NWEIGHTS)
                sp.dma_start(xs[:, c * WIDE:(c + 1) * WIDE].rearrange("p (b f) -> p b f", b=BATCH),
                             x_view[:, c]).then_inc(s["x_loaded" if c else "first_in"], 16)
            sp.wait_ge(s["zeroed"], 1)
            for view in cleared_views:
                for c in range(CHUNKS):
                    sp.dma_start(view[:, c * CLEAR:(c + 1) * CLEAR], zero[:, :]).then_inc(s["cleared"], 16)
            sp.wait_ge(s["cleared"], 16 * CHUNKS * len(cleared_views))

        @block.scalar
        def _(act):
            for dst, src in ((dl[:, 0:HEADS], decay_all), (dl[:, HEADS:], decay_pair), (lag[:, :], lag_d),
                             (causal[:, :], causal_d), (tpos[:, :], tpos_d), (left[:, :], left_d),
                             (bgc[:, :], bg), (ident[:, :], ident_d)):
                act.dma_start(dst, src).then_inc(s["tables_in"], 16)
            for dst, src in ((WQ, wq), (WK, wk), (WV, wv), (WG, wg), (WO, wo)):
                act.dma_start(dst[:, :], src).then_inc(s["loaded"], 16)
            act.wait_ge(s["neg_abs"], 1)
            act.activation(tmp[:, :], tmp[:, :], ACT.Exp).then_inc(s["exped"], 1)
            act.wait_ge(s["exped"], 1)
            act.activation(tmp[:, :], tmp[:, :], ACT.Ln, bias=1.0).then_inc(s["logged"], 1)
            act.wait_ge(front.turned, 1)
            act.activation(xT[:, :], turn[:, :], ACT.Copy).then_inc(s["xT"], 1)
            act.wait_ge(s["lg_ready"], 1)
            for h in range(HEADS):
                act.activation(mask[:, h * P:(h + 1) * P], lag[:, :], ACT.Exp,
                               scale=lg[:, h:h + 1]).then_inc(s["tables"], 1)
            for p in range(PAIRS):
                act.activation(qpow[:, p * P:(p + 1) * P], tpos[:, :], ACT.Exp,
                               scale=lg[:, HEADS + p:HEADS + p + 1]).then_inc(s["tables"], 1)
            act.activation(kpow[:, :], lg[:, 0:HEADS], ACT.Exp, scale=left[:, 0:1]).then_inc(s["tables"], 1)
            act.activation(gchunk[:, :], lg[:, HEADS:], ACT.Exp, scale=float(P)).then_inc(s["tables"], 1)

            def token_columns(i):
                act.wait_ge(front.turned, at(i, 1, 1))
                act.activation(xT[:, :], turn[:, :], ACT.Copy).then_inc(s["xT"], 1)

            def turn_of(i, last):
                k = 0
                for n, (what, p) in enumerate(PROJECTIONS):
                    act.wait_ge(s["proj"], at(i, 16, n + 1))
                    bank = into[n % 4]
                    if what in "qk":
                        if k >= 2:
                            act.wait_ge(s["phi"], at(i, 8, k - 1))
                        act.activation(e[k % 2][:, :], bank[:, :], ACT.Exp)
                        act.activation(r[k % 2][:, :], bank[:, :], ACT.Relu).then_inc(s["exp"], 1)
                        k += 1
                    elif what == "g":
                        act.activation(gate[:, p * WIDE:(p + 1) * WIDE], bank[:, :], ACT.Tanh,
                                       bias=half_bg[:, p:p + 1], scale=0.5).then_inc(s["gate"], 1)
                    else:
                        act.activation(v4[:, p, :, 0:DK], bank[:, :].rearrange("p (h j) -> p h j", h=HEADS),
                                       ACT.Copy).then_inc(s["v"], 1)
                if not last:
                    token_columns(i + 1)

            act.wait_ge(s["gmul"], 2)
            with act.Fori(0, CHUNKS - 1) as i:
                turn_of(i, False)
            turn_of(CHUNKS - 1, True)

        @block.gpsimd
        def _(pool):
            front.inverse_deviation(pool, (slice(0, BATCH),))
            pool.memset(zero[:, :], 0.0).then_inc(s["zeroed"], 1)
            pool.wait_ge(s["tables"], NSETUP)

            def turn_of(i, last):
                for p in range(PAIRS):
                    pool.wait_ge(s["phi"], at(i, 8, 2 * p + 1))
                    pool.tensor_tensor(wide(qd[:, p * WIDE:(p + 1) * WIDE]), wide(qT[:, p * WIDE:(p + 1) * WIDE]),
                                       qpow[:, p * P:(p + 1) * P].unsqueeze(1).to_broadcast([P, BATCH, P]),
                                       ALU.mult).then_inc(s["qd"], 1)
                if not last:
                    front.power(pool, i + 1, bass.ds((i + 1) * BATCH, BATCH))

            with pool.Fori(0, CHUNKS - 1) as i:
                turn_of(i, False)
            turn_of(CHUNKS - 1, True)

        @block.tensor
        def _(pe):
            def token_columns(i):
                front.transpose(pe, i, 0)

            def project(i, numbers):
                pe.wait_ge(s["xT"], at(i, 1, 1))
                for n in numbers:
                    what, p = PROJECTIONS[n]
                    if n >= 4:
                        before, b = PROJECTIONS[n - 4]
                        if before == "v":
                            pe.wait_ge(s["v"], at(i, 4, b + 1))
                        elif before == "g":
                            pe.wait_ge(s["gate"], at(i, 4, b + 1))
                        else:
                            pe.wait_ge(s["exp"], at(i, 8, 2 * b + 1 + (before == "k")))
                    if what == "v":
                        pe.matmul(into[n % 4][:, :], xT[:, p * P:(p + 1) * P], WV[:, :], start=True,
                                  stop=True).then_inc(s["proj"], 1)
                    else:
                        W = {"q": WQ, "k": WK, "g": WG}[what]
                        pe.matmul(into[n % 4][:, :], W[:, p * P:(p + 1) * P], xT[:, :], start=True,
                                  stop=True).then_inc(s["proj"], 1)

            def turn_of(i, last):
                project(i, range(EARLY, len(PROJECTIONS)))

                def keys_turned(p):
                    if p == 1:
                        pe.wait_ge(s["kd"], at(i, 4, 1))
                    elif p >= 2:
                        pe.wait_ge(s["yT"], at(i, 4, p - 1))
                    for b in range(BATCH):
                        mm = pe.transpose(turn[:, b * P:(b + 1) * P],
                                          kT[:, p * WIDE + b * P:p * WIDE + (b + 1) * P], ident[:, :])
                    mm.then_inc(s["ktr"], 1)

                def outputs_turned(p):
                    pe.wait_ge(s["y"], at(i, 8, 2 * p + 2))
                    if p < PAIRS - 1:
                        pe.wait_ge(s["kd"], at(i, 4, p + 2))
                    elif not last:
                        pe.wait_ge(s["xT"], at(i, 1, 2))
                    else:
                        pe.wait_ge(s["yT"], at(i, 4, 3))
                    for b in range(BATCH):
                        mm = pe.transpose(turn[:, b * P:(b + 1) * P], y3[:, b, p * P:(p + 1) * P], ident[:, :])
                    mm.then_inc(s["ytr"], 1)

                def scores(h):
                    p, lo = h // 2, DK * (h % 2)
                    if h >= 2:
                        pe.wait_ge(s["a"], at(i, 8, h - 1))
                    pe.wait_ge(s["phi"], at(i, 8, 2 * p + 2))
                    for b in range(BATCH):
                        cols = slice(p * WIDE + b * P, p * WIDE + (b + 1) * P)
                        mm = pe.matmul(score[h % 2][:, b * P:(b + 1) * P], kT[lo:lo + DK, cols], qT[lo:lo + DK, cols],
                                       start=True, stop=True)
                    mm.then_inc(s["score"], 1)

                def values(p, half):
                    pe.wait_ge(s["a"], at(i, 8, 2 * p + 2))
                    if half == 0:
                        pe.wait_ge(s["qd"], at(i, 4, p + 1))
                    if p == 0:
                        pe.wait_ge(s["v"], at(i, 4, 4))
                        pe.wait_ge(s["gate"], at(i, 4, 4))
                        pe.wait_ge(s["state"], at(i, 4, 1))
                    else:
                        pe.wait_ge(s["y"], at(i, 8, 2 * p + half - 1))
                    for b in range(2 * half, 2 * half + 2):
                        lo = (b % 2) * 2 * (DK + 1)
                        pe.matmul(av[half][:, lo:lo + 2 * (DK + 1)], qd[:, p * WIDE + b * P:p * WIDE + (b + 1) * P],
                                  st5[:, p, b].rearrange("p h j -> p (h j)"), start=True, stop=False,
                                  skip_group_check=True)
                        for h in (2 * p, 2 * p + 1):
                            at_head = lo + (h % 2) * (DK + 1)
                            mm = pe.matmul(av[half][:, at_head:at_head + DK + 1], a[h % 4][:, b * P:(b + 1) * P],
                                           v4[:, b, h, :], start=False, stop=(h % 2 == 1), skip_group_check=True)
                    mm.then_inc(s["av"], 1)

                def new_state(p):
                    pe.wait_ge(s["kd"], at(i, 4, p + 1))
                    if p == 0:
                        pe.wait_ge(s["res"], i + 1)
                    else:
                        pe.wait_ge(s["state"], at(i, 4, 1 + p))
                    for h in (2 * p, 2 * p + 1):
                        lo = DK * (h % 2)
                        for b in range(BATCH):
                            mm = pe.matmul(stp[lo:lo + DK, b * (DK + 1):(b + 1) * (DK + 1)],
                                           kd3[:, b, h * DK:(h + 1) * DK], v4[:, b, h, :], start=True, stop=True)
                    mm.then_inc(s["stp"], 1)

                scores(0)
                scores(1)
                keys_turned(0)
                for p in range(PAIRS):
                    values(p, 0)
                    if p < PAIRS - 1:
                        scores(2 * p + 2)
                    if p >= 1:
                        outputs_turned(p - 1)
                    values(p, 1)
                    if p < PAIRS - 1:
                        scores(2 * p + 3)
                        keys_turned(p + 1)
                    elif not last:
                        pe.wait_ge(s["yT"], at(i, 4, 3))
                        token_columns(i + 1)
                    new_state(p)
                outputs_turned(PAIRS - 1)
                if not last:
                    project(i + 1, range(EARLY))
                pe.wait_ge(s["state"], at(i, 4, 5))
                pe.wait_ge(s["yT"], at(i, 4, 4))
                for b in range(BATCH):
                    for p in range(PAIRS):
                        cols = slice(p * WIDE + b * P, p * WIDE + (b + 1) * P)
                        mm = pe.matmul(stp[:, b * P:(b + 1) * P], yT[:, cols], WO[:, p * P:(p + 1) * P],
                                       start=(p == 0), stop=(p == PAIRS - 1))
                mm.then_inc(s["out"], 1)

            pe.wait_ge(s["tables_in"], 16 * NTABLES)
            pe.wait_ge(s["loaded"], 16 * NWEIGHTS)
            token_columns(0)
            project(0, range(EARLY))
            with pe.Fori(0, CHUNKS - 1) as i:
                turn_of(i, False)
            turn_of(CHUNKS - 1, True)

        @block.vector
        def _(dve):
            dve.memset(v1[:, :], 1.0)
            dve.memset(state[:, :], 0.0).then_inc(s["state"], 1)
            dve.wait_ge(s["first_in"], 16)
            of.of_chunk(dve, xs, 0).then_inc(s["stat"], 1)
            dve.wait_ge(s["stat"], 1)
            front.moments_of(dve, 0, slice(0, BATCH))
            dve.wait_ge(s["tables_in"], 16 * NTABLES)
            dve.tensor_scalar(tmp[:, :], dl[:, :], -1.0, None, ALU.mult).then_inc(s["gmul"], 1)
            dve.wait_ge(s["gmul"], 1)
            dve.tensor_tensor(tmp[:, :], tmp[:, :], dl[:, :], ALU.min).then_inc(s["neg_abs"], 1)
            dve.tensor_scalar(half_bg[:, :], bgc[:, :], 0.5, None, ALU.mult).then_inc(s["gmul"], 1)
            dve.wait_ge(front.rstd_ready, 1)
            front.normalize(dve, xs, 0, 0)
            dve.wait_ge(s["logged"], 1)
            dve.scalar_tensor_tensor(lg[:, :], dl[:, :], 0.0, tmp[:, :], ALU.min, ALU.subtract).then_inc(s["lg_ready"], 1)
            dve.wait_ge(s["tables"], NSETUP)
            m3 = wide(mask[:, :], HEADS)
            dve.tensor_tensor(m3, m3, causal[:, :].unsqueeze(1).to_broadcast([P, HEADS, P]), ALU.mult).then_inc(s["gmul"], 1)

            def turn_of(i, last):
                for k in range(2 * PAIRS):
                    dst = kT if k % 2 else qT
                    p = k // 2
                    dve.wait_ge(s["exp"], at(i, 8, k + 1))
                    dve.scalar_tensor_tensor(dst[:, p * WIDE:(p + 1) * WIDE], e[k % 2][:, :], 1.0, r[k % 2][:, :],
                                             ALU.min, ALU.add).then_inc(s["phi"], 1)

                def weighted_keys(p):
                    dve.wait_ge(s["ktr"], at(i, 4, p + 1))
                    dve.tensor_tensor(kd3[:, :, p * P:(p + 1) * P].rearrange("p b (h j) -> p b h j", h=2),
                                      turn[:, :].rearrange("p (b h j) -> p b h j", b=BATCH, h=2),
                                      kpow[:, 2 * p:2 * p + 2].unsqueeze(1).unsqueeze(3).to_broadcast([P, BATCH, 2, DK]),
                                      ALU.mult).then_inc(s["kd"], 1)

                def gated(p):
                    dve.wait_ge(s["gate"], at(i, 4, p + 1))
                    dve.wait_ge(s["ytr"], at(i, 4, p + 1))
                    dve.scalar_tensor_tensor(yT[:, p * WIDE:(p + 1) * WIDE], gate[:, p * WIDE:(p + 1) * WIDE], 1.0,
                                             turn[:, :], ALU.add, ALU.mult).then_inc(s["yT"], 1)

                def masked(h):
                    dve.wait_ge(s["score"], at(i, 8, h + 1))
                    dve.tensor_tensor(wide(a[h % 4][:, :]), wide(score[h % 2][:, :]),
                                      mask[:, h * P:(h + 1) * P].unsqueeze(1).to_broadcast([P, BATCH, P]),
                                      ALU.mult).then_inc(s["a"], 1)

                def divided(p, half):
                    n = 2 * p + half
                    dve.wait_ge(s["av"], at(i, 8, n + 1))
                    o = av[half][:, 0:4 * (DK + 1)].rearrange("p (b h j) -> p b h j", b=2, h=2)
                    d3, r3 = (t[:, :].rearrange("p (b h) -> p b h", b=2) for t in (den, rden))
                    dve.tensor_scalar(d3, o[:, :, :, DK], DEN_EPS, 2.0, ALU.add, ALU.mult).then_inc(s["den"], 1)
                    dve.wait_ge(s["den"], at(i, 8, n + 1))
                    dve.reciprocal(rden[:, :], den[:, :]).then_inc(s["rden"], 1)
                    dve.wait_ge(s["rden"], at(i, 8, n + 1))
                    dve.tensor_tensor(y3[:, 2 * half:2 * half + 2, p * P:(p + 1) * P].rearrange("p b (h j) -> p b h j", h=2),
                                      o[:, :, :, 0:DK], r3.unsqueeze(3).to_broadcast([P, 2, 2, DK]), ALU.mult
                                      ).then_inc(s["y"], 1)

                masked(0)
                masked(1)
                weighted_keys(0)
                for p in range(PAIRS):
                    divided(p, 0)
                    if p < PAIRS - 1:
                        masked(2 * p + 2)
                    if p >= 1:
                        gated(p - 1)
                    divided(p, 1)
                    if p < PAIRS - 1:
                        masked(2 * p + 3)
                        weighted_keys(p + 1)
                    dve.wait_ge(s["stp"], at(i, 4, p + 1))
                    for h in range(2):
                        rows, st = slice(h * DK, (h + 1) * DK), st5[h * DK:(h + 1) * DK, p, :, h, :]
                        last_half = dve.scalar_tensor_tensor(
                            st, st, gchunk[rows, p:p + 1],
                            stp[rows, 0:BATCH * (DK + 1)].rearrange("p (b j) -> p b j", b=BATCH), ALU.mult, ALU.add)
                    last_half.then_inc(s["state"], 1)
                    if p == 0 and not last:
                        dve.wait_ge(s["x_loaded"], 16 * (CHUNKS - 1))
                        of.of_chunk(dve, xs, i + 1).then_inc(s["stat"], 1)
                        dve.wait_ge(s["stat"], at(i, 1, 2))
                        dve.sem_inc(front.held, 1)
                        front.moments_of(dve, i + 1, bass.ds((i + 1) * BATCH, BATCH))
                    if p == 1 and not last:
                        dve.wait_ge(front.rstd_ready, at(i, 1, 2))
                        front.normalize(dve, xs, i + 1, 0)
                gated(PAIRS - 1)
                dve.wait_ge(s["out"], at(i, 1, 1))
                xc = xs[:, bass.ds(i * WIDE, WIDE)]
                dve.tensor_tensor(xc, stp[:, :], xc, ALU.add).then_inc(s["res"], 1)
                dve.wait_ge(s["res"], i + 2)
                dve.sem_inc(front.held, 1)
                of.of_chunk(dve, xs, i)

            dve.sem_inc(s["res"], 1)
            with dve.Fori(0, CHUNKS - 1) as i:
                turn_of(i, False)
            turn_of(CHUNKS - 1, True)


EXPERTS = 8
HID0, HID1 = 256, 512
CAPACITY = int(np.ceil(2 * 1.25 * BATCH * SEQ / EXPERTS))
BIG = 3.0e38


def first_largest(dve, values, rank, best, eq, mask, chain):
    by_expert = lambda t: t.rearrange("p e n -> p n e")
    spread = lambda t: t.unsqueeze(1).to_broadcast([P, EXPERTS, TILES])
    chain(dve.tensor_reduce(best, by_expert(values), AX.X, ALU.max))
    chain(dve.tensor_tensor(eq, values, spread(best), ALU.is_equal))
    chain(dve.tensor_tensor(eq, eq, rank, ALU.mult))
    chain(dve.tensor_reduce(best, by_expert(eq), AX.X, ALU.max))
    chain(dve.tensor_tensor(mask, eq, spread(best), ALU.is_equal))


def mixture_phase(nc, xs, of, name, hidden, act_fn, router, w1, w2, ident_d, rank_d):
    with ExitStack() as ctx:
        S = Scope(nc, ctx, name)
        nexp = EXPERTS
        HB = hidden // P
        ident, rank = S.sb("ident", P), S.sb("rank", EXPERTS * TILES)
        R = S.sb("router", EXPERTS)
        W1, W2 = S.sb("W1", nexp * hidden), S.sb("W2", nexp * HB * P)
        XT = S.sb("XT", CHUNKS * WIDE)
        NE = EXPERTS * TILES
        logits, eq, rest = S.sb("logits", NE), S.sb("eq", NE), S.sb("rest", NE)
        masks, gates = S.sb("masks", 2 * NE), S.sb("gates", NE)
        best, second, w_a, w_b = (S.sb(n, TILES) for n in ("best", "second", "w_a", "w_b"))
        hT = [S.sb(f"hT{k}", HB * WIDE) for k in range(2)]
        xc = [S.sb(f"xc{k}", WIDE) for k in range(2)]
        gcol = S.sb("gcol", BATCH * nexp)
        front = Front(S, ident, of)
        hid = [S.bank(f"hid{k}") for k in range(3)]
        outp = [S.bank(f"outp{k}") for k in range(2)]
        s = {n: S.sem(n) for n in "loaded columns whole lg_mm lg_out chain expd recip gcol hid act outp acc".split()}
        loads = [(ident, ident_d), (rank, rank_d), (R, router)]
        late = [(W1, w1), (W2, w2)]
        late_in = S.sem("late_in")

        by_tile = lambda t: t.rearrange("p (e n) -> p e n", e=EXPERTS)
        by_chunk = lambda t: t.rearrange("p (e b c) -> p b e c", e=EXPERTS, b=BATCH)
        g3 = gcol[:, :].rearrange("p (b e) -> p b e", b=BATCH)

        block = ctx.enter_context(nc.Block())

        @block.sync
        def _(sp):
            for dst, src in loads:
                sp.dma_start(dst[:, :], src).then_inc(s["loaded"], 16)
            for dst, src in late:
                sp.dma_start(dst[:, :], src).then_inc(late_in, 16)

        @block.gpsimd
        def _(pool):
            front.inverse_deviation(pool)

        @block.tensor
        def _(pe):
            pe.wait_ge(s["loaded"], 16 * len(loads))
            def logits_of(i, k):
                pe.wait_ge(s["columns"], at(i, 2, k + 1))
                pe.wait_ge(s["lg_out"], at(i, 2, k + 1))
                again = P // EXPERTS
                for b in range(BATCH):
                    mm = pe.matmul(outp[k][:, b * P:(b + 1) * P].rearrange("p (r e) -> p r e", r=again),
                                   xc[k][:, b * P:(b + 1) * P],
                                   R[:, :].unsqueeze(1).to_broadcast([P, again, EXPERTS]), start=True, stop=True)
                mm.then_inc(s["lg_mm"], 1)

            front.transpose(pe, 0, 0)
            with pe.Fori(0, CHUNKS // 2 - 1) as i:
                front.transpose(pe, i * 2 + 1, 1)
                logits_of(i, 0)
                front.transpose(pe, i * 2 + 2, 0)
                logits_of(i, 1)
            front.transpose(pe, CHUNKS - 1, 1)
            logits_of(CHUNKS // 2 - 1, 0)
            logits_of(CHUNKS // 2 - 1, 1)
            pe.wait_ge(s["whole"], CHUNKS)
            pe.wait_ge(s["lg_out"], CHUNKS + 2)
            pe.wait_ge(late_in, 16 * len(late))
            with pe.Fori(0, CHUNKS) as i:
                def hidden_of(e):
                    for m in range(HB):
                        k = e * HB + m
                        pe.wait_ge(s["act"], at(i, nexp * HB, k + 1))
                        pe.matmul(hid[k % 3][:, :], W1[:, (e * HB + m) * P:(e * HB + m + 1) * P],
                                  XT[:, bass.ds(i * WIDE, WIDE)], start=True, stop=True).then_inc(s["hid"], 1)

                def output_of(e):
                    pe.wait_ge(s["act"], at(i, nexp * HB, 3 + (e + 1) * HB))
                    pe.wait_ge(s["acc"], at(i, nexp, e + 1))
                    for b in range(BATCH):
                        for m in range(HB):
                            mm = pe.matmul(outp[e % 2][:, b * P:(b + 1) * P],
                                           hT[e % 2][:, m * WIDE + b * P:m * WIDE + (b + 1) * P],
                                           W2[:, (e * HB + m) * P:(e * HB + m + 1) * P],
                                           start=(m == 0), stop=(m == HB - 1))
                    mm.then_inc(s["outp"], 1)

                hidden_of(0)
                for e in range(1, nexp):
                    hidden_of(e)
                    output_of(e - 1)
                output_of(nexp - 1)

        @block.scalar
        def _(act):
            act.sem_inc(s["lg_mm"], 2)
            act.sem_inc(s["act"], 3)
            with act.Fori(0, CHUNKS // 2) as i:
                for k in range(2):
                    act.wait_ge(front.turned, at(i, 2, k + 1))
                    act.activation(XT[:, bass.ds(i * 2 * WIDE + k * WIDE, WIDE)], front.turn[k][:, :], ACT.Copy
                                   ).then_inc(s["whole"], 1)
                    act.wait_ge(s["lg_mm"], at(i, 2, k + 1))
                    act.activation(xc[k][:, :], front.turn[k][:, :], ACT.Copy).then_inc(s["columns"], 1)
            act.wait_ge(s["expd"], 1)
            act.activation(w_b[:, :], w_b[:, :], ACT.Exp).then_inc(s["recip"], 1)
            with act.Fori(0, CHUNKS) as i:
                for e in range(nexp):
                    for m in range(HB):
                        k = e * HB + m
                        act.wait_ge(s["hid"], at(i, nexp * HB, k + 1))
                        if m == 0:
                            act.wait_ge(s["acc"], at(i, nexp, e + 1))
                        act.activation(hT[e % 2][:, m * WIDE:(m + 1) * WIDE], hid[k % 3][:, :], act_fn
                                       ).then_inc(s["act"], 1)

        @block.vector
        def _(dve):
            count = [0]

            def chain(ins):
                count[0] += 1
                ins.then_inc(s["chain"], 1)
                dve.wait_ge(s["chain"], count[0])

            dve.sem_inc(s["lg_out"], 2)
            dve.sem_inc(s["acc"], 2)
            front.moments_of(dve)
            dve.wait_ge(front.rstd_ready, 1)
            front.normalize(dve, xs, 0, 0)
            front.normalize(dve, xs, 1, 1)
            dve.wait_ge(front.rstd_ready, 2)

            def logits_kept(i, k):
                dve.wait_ge(s["lg_mm"], at(i, 2, k + 3))
                dve.tensor_copy(by_chunk(logits[:, :])[:, :, :, bass.ds(i * 2 + k, 1)],
                                wide(outp[k][:, :])[:, :, 0:EXPERTS].unsqueeze(3)).then_inc(s["lg_out"], 1)

            with dve.Fori(0, CHUNKS // 2 - 1) as i:
                for k in range(2):
                    dve.wait_ge(front.turned, at(i, 2, k + 1))
                    front.normalize(dve, xs, i * 2 + 2 + k, k)
                    logits_kept(i, k)
            for k in range(2):
                logits_kept(CHUNKS // 2 - 1, k)
            dve.wait_ge(s["loaded"], 16 * len(loads))
            dve.wait_ge(s["lg_out"], CHUNKS + 2)
            L, EQ, RK = by_tile(logits[:, :]), by_tile(eq[:, :]), by_tile(rank[:, :])
            M1, M2 = by_tile(masks[:, 0:NE]), by_tile(masks[:, NE:])
            RS, G = by_tile(rest[:, :]), by_tile(gates[:, :])
            experts_inside = lambda t: t.rearrange("p e n -> p n e")
            spread = lambda t: t[:, :].unsqueeze(1).to_broadcast([P, EXPERTS, TILES])
            first_largest(dve, L, RK, best[:, :], EQ, M1, chain)
            chain(dve.scalar_tensor_tensor(RS, M1, -BIG, L, ALU.mult, ALU.add))
            first_largest(dve, RS, RK, second[:, :], EQ, M2, chain)
            chain(dve.tensor_reduce(best[:, :], experts_inside(L), AX.X, ALU.max))
            chain(dve.tensor_reduce(second[:, :], experts_inside(RS), AX.X, ALU.max))
            dve.tensor_tensor(w_b[:, :], second[:, :], best[:, :], ALU.subtract).then_inc(s["expd"], 1)
            dve.wait_ge(s["recip"], 1)
            chain(dve.tensor_scalar(w_a[:, :], w_b[:, :], 1.0, None, ALU.add))
            chain(dve.reciprocal(w_a[:, :], w_a[:, :]))
            chain(dve.tensor_tensor(w_b[:, :], w_a[:, :], w_b[:, :], ALU.mult))
            chain(dve.tensor_tensor(G, M1, spread(w_a), ALU.mult))
            chain(dve.tensor_tensor(RS, M2, spread(w_b), ALU.mult))
            chain(dve.tensor_tensor(G, G, RS, ALU.add))

            with dve.Fori(0, CHUNKS) as i:
                dve.wait_ge(s["acc"], at(i, nexp, 2))
                dve.tensor_copy(g3[:, :, 0:EXPERTS].unsqueeze(3), by_chunk(gates[:, :])[:, :, :, bass.ds(i, 1)]
                                ).then_inc(s["gcol"], 1)
                dve.wait_ge(s["gcol"], at(i, 1, 1))
                for e in range(nexp):
                    dve.wait_ge(s["outp"], at(i, nexp, e + 1))
                    dve.wait_ge(s["acc"], at(i, nexp, e + 2))
                    for b in range(BATCH):
                        xb = xs[:, bass.ds(i * WIDE + b * P, P)]
                        last = dve.scalar_tensor_tensor(xb, outp[e % 2][:, b * P:(b + 1) * P],
                                                        gcol[:, b * nexp + e:b * nexp + e + 1], xb, ALU.mult, ALU.add)
                    last.then_inc(s["acc"], 1)
                dve.wait_ge(s["acc"], at(i, nexp, nexp + 2))
                dve.sem_inc(front.held, 1)
                of.of_chunk(dve, xs, i)


GROUP = 2 * P
SLOT_TURNS = CAPACITY // GROUP
SLOTS = EXPERTS * CAPACITY
assert CAPACITY % GROUP == 0 and SEQ <= (SLOT_TURNS - 1) * GROUP
SHARED_WEIGHT = 0.1


def routed_phase(nc, xs, of, queue_in, queue_out, out, router, w1, w2, b1, b2, sw1, sw2, sb1, sb2, ident_d, rank_d, before_d,
                 restart_d, place_d):
    with ExitStack() as ctx:
        S = Scope(nc, ctx, "routed")
        HB = HID1 // P
        NE = EXPERTS * TILES
        ident, rank, R = S.sb("ident", P), S.sb("rank", NE), S.sb("router", EXPERTS)
        before, restart = S.sb("before", P), S.sb("restart", 2 * NE)
        place = S.sb("place", NE)
        SW1, SW2, SB1, SB2 = S.sb("SW1", HID1), S.sb("SW2", HB * P), S.sb("SB1", HB), S.sb("SB2", P)
        W1, W2, B1, B2 = (S.sb("W1", EXPERTS * HID1), S.sb("W2", EXPERTS * HB * P), S.sb("B1", EXPERTS * HB),
                          S.sb("B2", EXPERTS * P))
        XN, XT = S.sb("XN", CHUNKS * WIDE), S.sb("XT", CHUNKS * WIDE)
        shared = S.sb("shared", CHUNKS * WIDE)
        logits, eq, rest = S.sb("logits", NE), S.sb("eq", NE), S.sb("rest", NE)
        masks, incl, pos = S.sb("masks", 2 * NE), S.sb("incl", 2 * NE), S.sb("pos", 2 * NE)
        ones, zero = S.sb("ones", P), S.sb("zero", D, 1)
        best, second, w_a, w_b = (S.sb(n, TILES) for n in ("best", "second", "w_a", "w_b"))
        slot_f = S.sb("slot_f", 2 * TILES)
        slot = ctx.enter_context(nc.sbuf_tensor("routed_slot", [P, 2 * TILES], U32))
        hT = [S.sb(f"hT{k}", HB * WIDE) for k in range(2)]
        xc = [S.sb(f"xc{k}", WIDE) for k in range(2)]
        rows = [S.sb(f"rows{k}", GROUP) for k in range(4)]
        cols = [S.sb(f"cols{k}", GROUP) for k in range(2)]
        outs = [S.sb(f"outs{k}", GROUP) for k in range(4)]
        gathered = [XN, XT]
        front = Front(S, ident, of)
        banks = [S.bank(f"hid{k}") for k in range(4)]
        outp = [S.bank(f"outp{k}") for k in range(2)]
        s = {n: S.sem(n) for n in ("loaded shared_in late_in columns kept whole lg_mm lg_out chain expd exped masked prefix slots "
                                   "s_hid s_act s_outp s_evac s_added dump_zero dumped dispatched "
                                   "e_turned e_cols e_hid e_act e_outp e_outs saved outs_free combined stored").split()}
        fetched = [S.sem(f"fetched{k}") for k in range(4)]
        arrivals = [0, 0, 0, 0, 1, 1, 2, 3]
        arrived = [S.sem(f"arrived{c}") for c in range(4)]

        loads = [(ident, ident_d), (R, router), (rank, rank_d), (before, before_d), (restart, restart_d),
                 (place, place_d)]
        shared_loads = [(SW1, sw1), (SW2, sw2), (SB1, sb1), (SB2, sb2)]
        late = [(W1, w1), (W2, w2), (B1, b1), (B2, b2)]

        by_tile = lambda t: t.rearrange("p (e n) -> p e n", e=EXPERTS)
        by_chunk = lambda t: t.rearrange("p (e b c) -> p b e c", e=EXPERTS, b=BATCH)

        block = ctx.enter_context(nc.Block())
        out_view = out.rearrange("b (c p) f -> p c b f", p=P)

        @block.sync
        def _(sp):
            for dst, src in loads:
                sp.dma_start(dst[:, :], src).then_inc(s["loaded"], 16)
            for dst, src in shared_loads:
                sp.dma_start(dst[:, :], src).then_inc(s["shared_in"], 16)
            for dst, src in late:
                sp.dma_start(dst[:, :], src).then_inc(s["late_in"], 16)
            sp.wait_ge(s["dump_zero"], 1)
            sp.dma_start(queue_out[SLOTS:SLOTS + 1, :], zero[:, :]).then_inc(s["dumped"], 16)
            sp.wait_ge(s["dispatched"], 16 * 2 * TILES)
            with sp.Fori(0, SLOT_TURNS) as i:
                for e in range(EXPERTS):
                    sp.wait_ge(s["e_turned"], at(i, EXPERTS, e + 1))
                    sp.dma_start(wide(rows[e % 4][:, :], 2), queue_in[bass.ds(i * GROUP + e * CAPACITY, GROUP), :]
                                 .rearrange("(j p) f -> p j f", p=P)).then_inc(fetched[e % 4], 16)
            for c in range(CHUNKS):
                sp.wait_ge(s["combined"], c + 1)
                sp.dma_start(out_view[:, c], wide(xs[:, c * WIDE:(c + 1) * WIDE])).then_inc(s["stored"], 16)
            sp.wait_ge(s["stored"], 16 * CHUNKS)

        @block.gpsimd
        def _(pool):
            front.inverse_deviation(pool)
            with pool.Fori(0, CHUNKS // 2) as i:
                for k in range(2):
                    pool.wait_ge(front.normal, at(i, 2, k + 1))
                    pool.sem_inc(front.held, 1)
                    pool.tensor_copy(XN[:, bass.ds(i * 2 * WIDE + k * WIDE, WIDE)], front.xn[k][:, :]
                                     ).then_inc(s["kept"], 1)
            pool.wait_ge(s["kept"], CHUNKS)
            pool.wait_ge(s["slots"], 2)
            for choice in range(2):
                for b in range(BATCH):
                    for c in range(CHUNKS):
                        n = choice * TILES + b * CHUNKS + c
                        pool.indirect_dma_start(queue_in, bass.IndirectOffsetOnAxis(slot[:, n:n + 1], 0),
                                                XN[:, c * WIDE + b * P:c * WIDE + (b + 1) * P], None,
                                                bounds_check=SLOTS - 1, oob_is_err=False
                                                ).then_inc(s["dispatched"], 16)
            def saved(i):
                for e in range(EXPERTS):
                    pool.wait_ge(s["e_outs"], at(i, EXPERTS, 2 + e + 1))
                    pool.sem_inc(front.held, 1)
                    pool.dma_start(queue_out[bass.ds(i * GROUP + e * CAPACITY, GROUP), :]
                                   .rearrange("(j p) f -> p j f", p=P), wide(outs[e % 4][:, :], 2)
                                   ).then_inc(s["saved"], 16)
                    pool.wait_ge(s["saved"], at(i, 16 * EXPERTS, 16 * (e + 1)))
                    pool.sem_inc(s["outs_free"], 1)

            def gather(choice, b, c):
                n = choice * TILES + b * CHUNKS + c
                pool.indirect_dma_start(gathered[choice][:, c * WIDE + b * P:c * WIDE + (b + 1) * P], None,
                                        queue_out, bass.IndirectOffsetOnAxis(slot[:, n:n + 1], 0)
                                        ).then_inc(arrived[arrivals[c]], 16)

            with pool.Fori(0, SLOT_TURNS - 1) as i:
                saved(i)
            pool.wait_ge(s["dumped"], 16)
            pool.wait_ge(s["dispatched"], 16 * 2 * TILES)
            pool.wait_ge(s["s_outp"], 4 + 2 * CHUNKS)
            for c in range(CHUNKS):
                gather(0, 0, c)
            saved(SLOT_TURNS - 1)
            for c in range(CHUNKS):
                for b in range(BATCH):
                    for choice in range(2):
                        if b or choice:
                            gather(choice, b, c)

        @block.tensor
        def _(pe):
            pe.wait_ge(s["loaded"], 16 * len(loads))

            def logits_of(i, k):
                pe.wait_ge(s["columns"], at(i, 2, k + 1))
                pe.wait_ge(s["lg_out"], at(i, 2, k + 1))
                again = P // EXPERTS
                for b in range(BATCH):
                    mm = pe.matmul(outp[k][:, b * P:(b + 1) * P].rearrange("p (r e) -> p r e", r=again),
                                   xc[k][:, b * P:(b + 1) * P],
                                   R[:, :].unsqueeze(1).to_broadcast([P, again, EXPERTS]), start=True, stop=True)
                mm.then_inc(s["lg_mm"], 1)

            front.transpose(pe, 0, 0)
            with pe.Fori(0, CHUNKS // 2 - 1) as i:
                front.transpose(pe, i * 2 + 1, 1)
                logits_of(i, 0)
                front.transpose(pe, i * 2 + 2, 0)
                logits_of(i, 1)
            front.transpose(pe, CHUNKS - 1, 1)
            logits_of(CHUNKS // 2 - 1, 0)
            logits_of(CHUNKS // 2 - 1, 1)

            def shared_pair(j):
                for t in range(2):
                    for m in range(HB):
                        pe.wait_ge(s["s_act"], at(j, 2 * HB, t * HB + m + 1))
                        pe.matmul(banks[m % 2][:, :], SW1[:, m * P:(m + 1) * P],
                                  XT[:, bass.ds(j * 2 * WIDE + t * WIDE, WIDE)], start=True, stop=True
                                  ).then_inc(s["s_hid"], 1)
                for t in range(2):
                    pe.wait_ge(s["s_act"], at(j, 2 * HB, 2 + (t + 1) * HB))
                    for half in range(2):
                        pe.wait_ge(s["s_evac"], at(j, 4, 2 * t + half + 1))
                        for b in range(2 * half, 2 * half + 2):
                            for m in range(HB):
                                mm = pe.matmul(outp[half][:, (b % 2) * P:(b % 2 + 1) * P],
                                               hT[t][:, m * WIDE + b * P:m * WIDE + (b + 1) * P],
                                               SW2[:, m * P:(m + 1) * P], start=(m == 0), stop=(m == HB - 1))
                        mm.then_inc(s["s_outp"], 1)

            pe.wait_ge(s["shared_in"], 16 * len(shared_loads))
            pe.wait_ge(s["whole"], CHUNKS)
            pe.wait_ge(s["lg_out"], CHUNKS + 2)
            pe.wait_ge(s["masked"], 1)
            pe.matmul(front.turn[0][:, :], before[:, :], masks[:, :], start=True, stop=True)
            pe.matmul(front.turn[1][:, :], ones[:, :], masks[:, :], start=True, stop=True).then_inc(s["prefix"], 1)
            with pe.Fori(0, CHUNKS // 2) as j:
                shared_pair(j)

            pe.wait_ge(s["late_in"], 16 * len(late))
            pe.wait_ge(s["s_act"], 2 + CHUNKS * HB)
            pe.wait_ge(s["s_evac"], 2 + 2 * CHUNKS)
            def turned(i, e):
                pe.wait_ge(fetched[e % 4], at(i, 16 * EXPERTS // 4, 16 * (e // 4 + 1)))
                pe.wait_ge(s["e_cols"], at(i, EXPERTS, e + 1))
                for j in range(2):
                    mm = pe.transpose(front.turn[e % 2][:, j * P:(j + 1) * P], rows[e % 4][:, j * P:(j + 1) * P],
                                      ident[:, :])
                mm.then_inc(s["e_turned"], 1)

            def hidden_of(i, e):
                pe.wait_ge(s["e_cols"], at(i, EXPERTS, 2 + e + 1))
                for h in range(HB // 2):
                    q = e * HB // 2 + h
                    pe.wait_ge(s["e_act"], at(i, EXPERTS * HB // 2, q + 1))
                    for m in (2 * h, 2 * h + 1):
                        mm = pe.matmul(banks[q % 4][:, (m % 2) * GROUP:(m % 2 + 1) * GROUP],
                                       W1[:, (e * HB + m) * P:(e * HB + m + 1) * P], cols[e % 2][:, :],
                                       start=True, stop=True)
                    mm.then_inc(s["e_hid"], 1)

            def output_of(i, e):
                pe.wait_ge(s["e_act"], at(i, EXPERTS * HB // 2, 4 + (e + 1) * HB // 2))
                pe.wait_ge(s["e_outs"], at(i, EXPERTS, e + 1))
                for j in range(2):
                    for m in range(HB):
                        mm = pe.matmul(outp[e % 2][:, j * P:(j + 1) * P],
                                       hT[e % 2][:, m * GROUP + j * P:m * GROUP + (j + 1) * P],
                                       W2[:, (e * HB + m) * P:(e * HB + m + 1) * P],
                                       start=(m == 0), stop=(m == HB - 1))
                mm.then_inc(s["e_outp"], 1)

            def slot_turn(i, last):
                for e in range(EXPERTS):
                    hidden_of(i, e)
                    if e + 2 < EXPERTS:
                        turned(i, e + 2)
                    elif not last:
                        turned(i + 1, e + 2 - EXPERTS)
                    if e:
                        output_of(i, e - 1)
                output_of(i, EXPERTS - 1)

            turned(0, 0)
            turned(0, 1)
            with pe.Fori(0, SLOT_TURNS - 1) as i:
                slot_turn(i, False)
            slot_turn(SLOT_TURNS - 1, True)

        @block.scalar
        def _(act):
            act.sem_inc(s["lg_mm"], 2)
            with act.Fori(0, CHUNKS // 2) as i:
                for k in range(2):
                    act.wait_ge(front.turned, at(i, 2, k + 1))
                    act.activation(XT[:, bass.ds(i * 2 * WIDE + k * WIDE, WIDE)], front.turn[k][:, :], ACT.Copy
                                   ).then_inc(s["whole"], 1)
                    act.wait_ge(s["lg_mm"], at(i, 2, k + 1))
                    act.activation(xc[k][:, :], front.turn[k][:, :], ACT.Copy).then_inc(s["columns"], 1)
            act.wait_ge(s["expd"], 1)
            act.activation(logits[:, :], logits[:, :], ACT.Exp).then_inc(s["exped"], 1)

            act.sem_inc(s["s_act"], 2)
            act.sem_inc(s["s_evac"], 2)
            act.sem_inc(s["s_outp"], 4)
            with act.Fori(0, CHUNKS // 2) as j:
                for t in range(2):
                    act.wait_ge(s["s_outp"], at(j, 4, 2 * t + 2))
                    for m in range(HB):
                        act.wait_ge(s["s_hid"], at(j, 2 * HB, t * HB + m + 1))
                        act.activation(hT[t][:, m * WIDE:(m + 1) * WIDE], banks[m % 2][:, :], ACT.Silu,
                                       bias=SB1[:, m:m + 1]).then_inc(s["s_act"], 1)
                for t in range(2):
                    for half in range(2):
                        act.wait_ge(s["s_outp"], at(j, 4, 4 + 2 * t + half + 1))
                        act.activation(shared[:, bass.ds(j * 2 * WIDE + t * WIDE + half * 2 * P, 2 * P)],
                                       outp[half][:, 0:2 * P], ACT.Copy).then_inc(s["s_evac"], 1)

            act.sem_inc(s["e_act"], 4)
            act.sem_inc(s["e_outp"], 2)
            act.wait_ge(s["s_outp"], 4 + 2 * CHUNKS)
            with act.Fori(0, SLOT_TURNS) as i:
                for e in range(EXPERTS):
                    act.wait_ge(s["e_outp"], at(i, EXPERTS, e + 1))
                    for h in range(HB // 2):
                        q = e * HB // 2 + h
                        act.wait_ge(s["e_hid"], at(i, EXPERTS * HB // 2, 4 + q + 1))
                        for m in (2 * h, 2 * h + 1):
                            last = act.activation(hT[e % 2][:, m * GROUP:(m + 1) * GROUP],
                                                  banks[q % 4][:, (m % 2) * GROUP:(m % 2 + 1) * GROUP], ACT.Silu,
                                                  bias=B1[:, e * HB + m:e * HB + m + 1])
                        last.then_inc(s["e_act"], 1)

        @block.vector
        def _(dve):
            count = [0]

            def chain(ins):
                count[0] += 1
                ins.then_inc(s["chain"], 1)
                dve.wait_ge(s["chain"], count[0])

            dve.sem_inc(s["lg_out"], 2)
            dve.memset(zero[:, :], 0.0).then_inc(s["dump_zero"], 1)
            chain(dve.memset(ones[:, :], 1.0))
            front.moments_of(dve)
            dve.wait_ge(front.rstd_ready, 1)
            front.normalize(dve, xs, 0, 0)
            front.normalize(dve, xs, 1, 1)
            dve.wait_ge(front.rstd_ready, 2)

            def logits_kept(i, k):
                dve.wait_ge(s["lg_mm"], at(i, 2, k + 3))
                dve.tensor_copy(by_chunk(logits[:, :])[:, :, :, bass.ds(i * 2 + k, 1)],
                                wide(outp[k][:, :])[:, :, 0:EXPERTS].unsqueeze(3)).then_inc(s["lg_out"], 1)

            with dve.Fori(0, CHUNKS // 2 - 1) as i:
                for k in range(2):
                    dve.wait_ge(front.turned, at(i, 2, k + 1))
                    dve.wait_ge(s["kept"], at(i, 2, k + 1))
                    front.normalize(dve, xs, i * 2 + 2 + k, k)
                    logits_kept(i, k)
            for k in range(2):
                logits_kept(CHUNKS // 2 - 1, k)
            dve.wait_ge(s["loaded"], 16 * len(loads))
            dve.wait_ge(s["lg_out"], CHUNKS + 2)
            L, EQ, RK = by_tile(logits[:, :]), by_tile(eq[:, :]), by_tile(rank[:, :])
            M1, M2 = by_tile(masks[:, 0:NE]), by_tile(masks[:, NE:])
            RS = by_tile(rest[:, :])
            experts_inside = lambda t: t.rearrange("p e n -> p n e")
            spread = lambda t: t[:, :].unsqueeze(1).to_broadcast([P, EXPERTS, TILES])
            chain(dve.tensor_reduce(best[:, :], experts_inside(L), AX.X, ALU.max))
            dve.tensor_tensor(L, L, spread(best), ALU.subtract).then_inc(s["expd"], 1)
            dve.wait_ge(s["exped"], 1)
            chain(dve.tensor_reduce(w_a[:, :], experts_inside(L), AX.X, ALU.add))
            chain(dve.reciprocal(w_a[:, :], w_a[:, :]))
            chain(dve.tensor_tensor(L, L, spread(w_a), ALU.mult))
            first_largest(dve, L, RK, best[:, :], EQ, M1, chain)
            chain(dve.tensor_tensor(RS, L, M1, ALU.mult))
            chain(dve.tensor_tensor(RS, L, RS, ALU.subtract))
            first_largest(dve, RS, RK, second[:, :], EQ, M2, chain)
            dve.sem_inc(s["masked"], 1)
            dve.wait_ge(s["prefix"], 1)
            within, totals = front.turn[0], front.turn[1]
            chain(dve.tensor_tensor_scan(incl[:, :], restart[:, :], totals[:, :], 0.0, ALU.mult, ALU.add))
            chain(dve.tensor_tensor(pos[:, :], incl[:, :], totals[:, :], ALU.subtract))
            chain(dve.tensor_tensor(pos[:, :], pos[:, :], within[:, :], ALU.add))
            taken = eq[:, 0:EXPERTS]
            chain(dve.tensor_scalar(taken, incl[:, TILES - 1:NE:TILES], float(CAPACITY), None, ALU.min))
            P2 = by_tile(pos[:, NE:])
            chain(dve.tensor_tensor(P2, P2, taken.unsqueeze(2).to_broadcast([P, EXPERTS, TILES]), ALU.add))
            chain(dve.scalar_tensor_tensor(masks[:, :], pos[:, :], float(CAPACITY), masks[:, :], ALU.is_lt, ALU.mult))
            both = lambda t: t.rearrange("p (c n) -> p c n", c=2)
            chain(dve.tensor_tensor(both(pos[:, :]), both(pos[:, :]),
                                    place[:, :].unsqueeze(1).to_broadcast([P, 2, NE]), ALU.add))
            chain(dve.tensor_tensor(pos[:, :], pos[:, :], masks[:, :], ALU.mult))
            for choice in range(2):
                chain(dve.tensor_reduce(slot_f[:, choice * TILES:(choice + 1) * TILES],
                                        experts_inside(by_tile(pos[:, choice * NE:(choice + 1) * NE])), AX.X, ALU.add))
            chain(dve.tensor_scalar(slot_f[:, :], slot_f[:, :], float(SLOTS), None, ALU.add))
            dve.tensor_copy(slot[:, :], slot_f[:, :]).then_inc(s["slots"], 2)
            chain(dve.tensor_tensor(RS, L, M1, ALU.mult))
            chain(dve.tensor_reduce(w_a[:, :], experts_inside(RS), AX.X, ALU.add))
            chain(dve.tensor_tensor(RS, L, M2, ALU.mult))
            chain(dve.tensor_reduce(w_b[:, :], experts_inside(RS), AX.X, ALU.add))
            chain(dve.tensor_tensor(best[:, :], w_a[:, :], w_b[:, :], ALU.add))
            chain(dve.tensor_scalar(best[:, :], best[:, :], float(np.finfo(np.float32).eps), None, ALU.max))
            chain(dve.reciprocal(best[:, :], best[:, :]))
            chain(dve.tensor_tensor(w_a[:, :], w_a[:, :], best[:, :], ALU.mult))
            chain(dve.tensor_tensor(w_b[:, :], w_b[:, :], best[:, :], ALU.mult))

            dve.wait_ge(s["shared_in"], 16 * len(shared_loads))
            with dve.Fori(0, CHUNKS) as i:
                sh, xc_ = shared[:, bass.ds(i * WIDE, WIDE)], xs[:, bass.ds(i * WIDE, WIDE)]
                dve.wait_ge(s["s_evac"], at(i, 2, 2 + 2))
                dve.tensor_tensor(wide(sh), wide(sh), SB2[:, :].unsqueeze(1).to_broadcast([P, BATCH, P]),
                                  ALU.add).then_inc(s["s_added"], 1)
                dve.wait_ge(s["s_added"], at(i, 2, 1))
                dve.scalar_tensor_tensor(xc_, sh, SHARED_WEIGHT, xc_, ALU.mult, ALU.add).then_inc(s["s_added"], 1)

            dve.sem_inc(s["e_turned"], 4)
            dve.sem_inc(s["e_cols"], 2)
            dve.sem_inc(s["e_hid"], 4)
            dve.sem_inc(s["e_outs"], 2)
            dve.sem_inc(s["outs_free"], 4)
            dve.wait_ge(s["late_in"], 16 * len(late))
            def columns_of(i, e):
                dve.wait_ge(s["e_turned"], at(i, EXPERTS, 4 + e + 1))
                dve.wait_ge(s["e_hid"], at(i, EXPERTS * HB // 2, (e + 1) * HB // 2))
                dve.tensor_copy(cols[e % 2][:, :], front.turn[e % 2][:, 0:GROUP]).then_inc(s["e_cols"], 1)

            def kept_of(i, e):
                dve.wait_ge(s["e_outp"], at(i, EXPERTS, 2 + e + 1))
                dve.wait_ge(s["outs_free"], at(i, EXPERTS, e + 1))
                dve.tensor_tensor(wide(outs[e % 4][:, :], 2), wide(outp[e % 2][:, 0:GROUP], 2),
                                  B2[:, e * P:(e + 1) * P].unsqueeze(1).to_broadcast([P, 2, P]), ALU.add
                                  ).then_inc(s["e_outs"], 1)

            def slot_turn(i, last):
                for e in range(EXPERTS):
                    if e + 2 < EXPERTS:
                        columns_of(i, e + 2)
                    elif not last:
                        columns_of(i + 1, e + 2 - EXPERTS)
                    if e:
                        kept_of(i, e - 1)
                kept_of(i, EXPERTS - 1)

            columns_of(0, 0)
            columns_of(0, 1)
            with dve.Fori(0, SLOT_TURNS - 1) as i:
                slot_turn(i, False)
            slot_turn(SLOT_TURNS - 1, True)

            for c in range(CHUNKS):
                dve.wait_ge(arrived[arrivals[c]], arrivals.count(arrivals[c]) * 16 * 2 * BATCH)
                for choice, weight in ((0, w_a), (1, w_b)):
                    if choice:
                        dve.wait_ge(s["chain"], count[0])
                    for b in range(BATCH):
                        xb = xs[:, c * WIDE + b * P:c * WIDE + (b + 1) * P]
                        last = dve.scalar_tensor_tensor(xb, gathered[choice][:, c * WIDE + b * P:c * WIDE + (b + 1) * P],
                                                        weight[:, b * CHUNKS + c:b * CHUNKS + c + 1], xb, ALU.mult,
                                                        ALU.add)
                    if choice == 0:
                        count[0] += 1
                        last.then_inc(s["chain"], 1)
                last.then_inc(s["combined"], 1)


D_IN, STATES, TAPS = 256, 16, 4
POS = 16
GC = P // POS
GROUPS = D_IN // GC
HALVES = D_IN // P
SUPER = 4
SUPERS = SEQ // (SUPER * POS)
COLS = BATCH * SUPERS
LEVELS = 6
SCANS = 4
AHEAD = 4
RMS_EPS = 1e-6


def state_space_phase(nc, xs, of, scratch, norm_w, win, b_in, conv_w, conv_b, a_rows_c, a_cols_b, wout, b_out,
                      ident_d, own_d):
    with ExitStack() as ctx:
        S = Scope(nc, ctx, "ssm")
        PAD = TAPS - 1
        ident, own = S.sb("ident", P), S.sb("own", GC)
        NW, WIN, BIN = S.sb("NW", 1), S.sb("WIN", D_IN), S.sb("BIN", HALVES)
        CW, CB, WOUT, BOUT = S.sb("CW", HALVES * TAPS), S.sb("CB", HALVES), S.sb("WOUT", HALVES * D), S.sb("BOUT", D)
        RB, RC = S.sb("RB", GROUPS * (16 + 64)), S.sb("RC", GROUPS * (16 + 65))
        AB, AC = S.sb("AB", GROUPS * (STATES + 1)), S.sb("AC", GROUPS * (STATES + 1))
        big_a, big_b = S.sb("big_a", HALVES * BATCH * (SEQ + PAD)), S.sb("big_b", HALVES * BATCH * SEQ)
        turn_buf = S.sb("turn_buf", 2 * GROUPS * P)
        diag = S.sb("diag", GROUPS * P)
        TW = S.sb("TW", GROUPS * SUPER * POS)
        STARTS = BATCH * (SUPERS + 1)
        H = S.sb("H", GROUPS * (STARTS + 16))
        b_own = S.sb("b_own", GROUPS * GC)
        gsb = S.sb("gsb", GROUPS * (POS - 1 + 64), GC)
        hn, hT = ([S.sb(f"{n}{k}", WIDE) for k in range(2)] for n in ("hn", "hT"))
        msq, r2 = S.sb("msq", TILES), S.sb("r2", TILES)
        front = Front(S, ident, of)
        pb = front.turn + [S.bank(f"pb{k}") for k in range(2, 8)]

        u = big_a[:, :].rearrange("p (h b t) -> p h b t", h=HALVES, b=BATCH)
        u2 = big_a[:, 0:GROUPS * 256].rearrange("p (g c) -> p g c", g=GROUPS)
        yT = big_a[:, 0:HALVES * BATCH * SEQ].rearrange("p (h t) -> p h t", h=HALVES)
        v = big_b[:, :].rearrange("p (h b t) -> p h b t", h=HALVES, b=BATCH)
        ys = big_b[:, :].rearrange("p (g c) -> p g c", g=GROUPS)
        diagT = turn_buf[:, 0:GROUPS * P]
        tb = [turn_buf[:, k * GROUPS * P:(k + 1) * GROUPS * P] for k in range(2)]
        expB, weightX, expO, expT = ([turn_buf[:, (AHEAD * n + k) * 512:(AHEAD * n + k + 1) * 512]
                                      for k in range(AHEAD)] for n in range(4))
        rb = RB[:, :].rearrange("p (g n) -> p g n", g=GROUPS)
        rc = RC[:, :].rearrange("p (g n) -> p g n", g=GROUPS)
        h3 = H[:, :].rearrange("p (g n) -> p g n", g=GROUPS)
        h4 = h3[:, :, 0:STARTS].rearrange("p g (b s) -> p g b s", b=BATCH)
        tw = TW[:, :].rearrange("p (g n) -> p g n", g=GROUPS)
        ab = AB[:, :].rearrange("p (g n) -> p g n", g=GROUPS)
        ac = AC[:, :].rearrange("p (g n) -> p g n", g=GROUPS)
        g3 = gsb[:, :].rearrange("p (g n) -> p g n", g=GROUPS)

        power_loads = [(AB[:, :], a_cols_b), (AC[:, :], a_rows_c), (own[:, :], own_d)]
        loads = [(ident[:, :], ident_d), (NW[:, :], norm_w), (WIN[:, :], win),
                 (BIN[:, :], b_in), (CW[:, :], conv_w), (CB[:, :], conv_b), (WOUT[:, :], wout), (BOUT[:, :], b_out)]
        s = {n: S.sem(n) for n in ("powers_in loaded laid diag diagT lev_mm lev_out own g_mm g_out g_saved windows zeroed msq r2 hn hT "
                                   "u_mm u v0 conv1 conv2 conv3 kept t1 t1_out t2 t2_out expB xT xW x_mm x_out "
                                   "scan scanned expO expT y_mm y_out t3 t3_out t4 t4_out w_mm w_out").split()}

        def own_block(n):
            return own[:, :].unsqueeze(1).unsqueeze(3).to_broadcast([P, n, GC, 16])

        def expanded(ap):
            return ap.unsqueeze(2).to_broadcast([P, ap.shape[1], GC, 16])

        def channel_form(ap, n):
            return ap.rearrange("p (n d s) -> p n d s", n=n, d=GC)

        block = ctx.enter_context(nc.Block())
        Q = 4
        NQ = GROUPS // Q

        @block.sync
        def _(sp):
            for dst, src in power_loads:
                sp.dma_start(dst, src).then_inc(s["powers_in"], 16)
            for dst, src in loads:
                sp.dma_start(dst, src).then_inc(s["loaded"], 16)
            sp.wait_ge(s["g_out"], 4)
            width = POS - 1 + 64
            sp.dma_start(scratch.rearrange("(d g n) -> d g n", d=GC, g=GROUPS), g3).then_inc(s["g_saved"], 16)
            sp.wait_ge(s["g_saved"], 16)
            for d in range(GC):
                window = bass.AP(tensor=scratch.tensor, offset=scratch.offset + d * GROUPS * width,
                                 ap=[[1, POS], [width, GROUPS], [1, 64]])
                sp.dma_start(tw[d * POS:(d + 1) * POS, :, :], window).then_inc(s["windows"], 16)

        STEPS = {(1 + n // 2, 3 + 4 * (n % 2)): n for n in range(CHUNKS + 2)}
        assert max(STEPS) == (LEVELS - 1, NQ - 1)

        def of_batch(q):
            return slice(q * Q, (q + 1) * Q)

        def counts(step, q, side):
            return 2 * NQ * step + 2 * q + side + 1 if step < LEVELS else 2 * NQ * LEVELS + NQ * (step - LEVELS) + q + 1

        @block.gpsimd
        def _(pool):
            front.inverse_deviation(pool)
            pool.wait_ge(s["laid"], 3)

            def transposed_power(k, after=lambda q: None):
                for q in range(NQ):
                    if k:
                        pool.wait_ge(s["lev_out"], counts(k - 1, q, 1))
                    if k > LEVELS:
                        pool.wait_ge(s["scanned"], NQ * (k - 1 - LEVELS) + q + 1)
                    source = rb[:, of_batch(q), 0:16] if k <= LEVELS else h3[:, of_batch(q), STARTS:]
                    pool.tensor_tensor(channel_form(diagT[:, q * Q * P:(q + 1) * Q * P], Q), expanded(source),
                                       own_block(Q), ALU.mult).then_inc(s["diagT"], 1)
                    after(q)

            def kept(i):
                xc = xs[:, i * WIDE:(i + 1) * WIDE]
                pool.wait_ge(front.normal, i + 1)
                pool.wait_ge(s["hn"], i + 1)
                pool.tensor_tensor(xc, xc, front.xn[i % 2][:, :], ALU.add).then_inc(s["kept"], 1)
                pool.wait_ge(s["kept"], 2 * i + 1)
                pool.tensor_tensor(wide(xc), wide(xc), BOUT[:, :].unsqueeze(1).to_broadcast([P, BATCH, D]),
                                   ALU.add).then_inc(s["kept"], 1)

            transposed_power(0)
            pool.wait_ge(s["msq"], 3)
            pool.tensor_tensor(r2[:, :], msq[:, :], of.mhalf[:, :], ALU.pow).then_inc(s["r2"], 1)
            for k in range(1, LEVELS):
                transposed_power(k, lambda q: kept(STEPS[k - 1, q]) if (k - 1, q) in STEPS else None)
            pool.wait_ge(s["x_out"], GROUPS + AHEAD)
            for k in range(LEVELS, LEVELS + SCANS - 1):
                transposed_power(k)
            pool.wait_ge(s["windows"], 16 * GC)
            with pool.Fori(0, GROUPS // AHEAD) as i:
                for k in range(AHEAD):
                    pool.wait_ge(s["y_mm"], at(i, AHEAD, k + 1))
                    pool.sem_inc(front.held, 1)
                    pool.tensor_tensor(channel_form(expT[k], SUPER),
                                       expanded(TW[:, bass.ds(i * AHEAD * 64 + k * 64, 64)]
                                                .rearrange("p (n s) -> p n s", n=SUPER)),
                                       own_block(SUPER), ALU.mult).then_inc(s["expT"], 1)

        @block.tensor
        def _(pe):

            def power_batch(k, q, side):
                weights, vectors, bank = ((diag, rb, pb[q % 4]), (diagT, rc, pb[4 + q % 4]))[side]
                if q >= 4:
                    pe.wait_ge(s["lev_out"], counts(k, q - 4, side))
                elif side == 1 and k:
                    pe.wait_ge(s["lev_out"], counts(k - 1, q + 4, side))
                for g in range(q * Q, (q + 1) * Q):
                    mm = pe.matmul(bank[:, (g % Q) * P:(g % Q + 1) * P].rearrange("p (r n) -> p r n", r=2),
                                   weights[:, g * P:(g + 1) * P],
                                   vectors[:, g, 0:64].unsqueeze(1).to_broadcast([P, 2, 64]), start=True, stop=True)
                mm.then_inc(s["lev_mm"], 1)

            def columns(i, k):
                pe.wait_ge(s["hn"], i + 1)
                for b in range(BATCH):
                    mm = pe.transpose(front.turn[k][:, b * P:(b + 1) * P], hn[k][:, b * P:(b + 1) * P], ident[:, :])
                mm.then_inc(front.turned, 1)

            def input_product(i, k):
                pe.wait_ge(s["hT"], i + 1)
                for h in range(HALVES):
                    pe.wait_ge(s["u"], i * 2 + h + 1)
                    pe.matmul(pb[4 + h][:, :], WIN[:, h * P:(h + 1) * P], hT[k][:, :], start=True,
                              stop=True).then_inc(s["u_mm"], 1)

            step = None
            for k in range(LEVELS):
                for q in range(NQ):
                    pe.wait_ge(s["diag"], NQ * k + q + 1)
                    if k and q < 4:
                        pe.wait_ge(s["lev_out"], counts(k - 1, q + 4, 0))
                    if step is not None and q % 4 == 0 and step < CHUNKS:
                        pe.wait_ge(s["hT"], step + 1)
                    power_batch(k, q, 0)
                    pe.wait_ge(s["diagT"], NQ * k + q + 1)
                    if step and q % 4 < HALVES and step <= CHUNKS:
                        pe.wait_ge(s["u"], 2 * step + q % 4 + 1)
                    power_batch(k, q, 1)
                    step = STEPS.get((k, q), step)
                    if (k, q) in STEPS:
                        pe.wait_ge(s["lev_out"], counts(k, q - 2, 1))
                        if step == 0:
                            pe.wait_ge(s["loaded"], 16 * len(loads))
                        if step < CHUNKS:
                            columns(step, step % 2)
                        if 0 < step <= CHUNKS:
                            input_product(step - 1, (step - 1) % 2)
            pe.wait_ge(s["own"], 1)
            pe.wait_ge(s["lev_out"], counts(LEVELS - 1, NQ - 1, 1))
            for q in range(4):
                for g in range(q * 8, (q + 1) * 8):
                    mm = pe.matmul(pb[q][0:GC, (g % 8) * 64:(g % 8 + 1) * 64], b_own[:, g * GC:(g + 1) * GC],
                                   rc[:, g, 16:80], start=True, stop=True)
                mm.then_inc(s["g_mm"], 1)

            pe.wait_ge(s["g_out"], 4)
            pe.wait_ge(s["conv3"], HALVES * CHUNKS)
            v_blocks = big_b[:, :].rearrange("p (h c j) -> p h j c", h=HALVES, j=POS)
            n1 = n2 = 0
            for mh in range(2):
                for h in range(HALVES):
                    for jq in range(4):
                        if n1 >= 4:
                            pe.wait_ge(s["t1_out"], n1 - 3)
                        for k in range(4):
                            mm = pe.transpose(pb[n1 % 4][:, k * P:(k + 1) * P],
                                              v_blocks[:, h, 4 * jq + 3 - k, mh * P:(mh + 1) * P], ident[:, :])
                        mm.then_inc(s["t1"], 1)
                        n1 += 1
            for mh in range(2):
                for gq in range(GROUPS // 4):
                    pe.wait_ge(s["t1_out"], 8 * (mh + 1))
                    if n2 >= 4:
                        pe.wait_ge(s["t2_out"], n2 - 3)
                    for k in range(4):
                        g = 4 * gq + k
                        mm = pe.transpose(pb[4 + n2 % 4][:, k * P:(k + 1) * P], tb[mh][:, g * P:(g + 1) * P], ident[:, :])
                    mm.then_inc(s["t2"], 1)
                    n2 += 1

            def input_weights(i, k):
                pe.wait_ge(s["expB"], at(i, AHEAD, k + 1))
                pe.wait_ge(s["xW"], at(i, AHEAD, k + 1))
                for m in range(SUPER):
                    mm = pe.transpose(pb[k][:, m * P:(m + 1) * P], expB[k][:, m * P:(m + 1) * P], ident[:, :])
                mm.then_inc(s["xT"], 1)

            def own_part(i, k):
                pe.wait_ge(s["xW"], at(i, AHEAD, AHEAD + k + 1))
                pe.wait_ge(s["x_out"], at(i, AHEAD, k + 1))
                for m in range(SUPER):
                    r = SUPER - 1 - m
                    mm = pe.matmul(pb[4 + k][:, 0:2 * COLS].rearrange("p (r n) -> p r n", r=2),
                                   weightX[k][:, r * P:(r + 1) * P],
                                   big_a[:, bass.ds(i * AHEAD * 256 + k * 256 + m * COLS, COLS)].unsqueeze(1)
                                   .to_broadcast([P, 2, COLS]), start=(m == 0), stop=(m == SUPER - 1))
                mm.then_inc(s["x_mm"], 1)

            pe.wait_ge(s["t2_out"], n2)
            for k in range(AHEAD):
                input_weights(0, k)
            with pe.Fori(0, GROUPS // AHEAD - 1) as i:
                for k in range(AHEAD):
                    own_part(i, k)
                    input_weights(i + 1, k)
            for k in range(AHEAD):
                own_part(GROUPS // AHEAD - 1, k)

            pe.wait_ge(s["x_out"], GROUPS + AHEAD)
            for j in range(SCANS):
                k = LEVELS + j
                n = SUPERS - 2 ** j
                again = P // (BATCH * n)
                for q in range(NQ):
                    pe.wait_ge(s["diag"], NQ * k + q + 1)
                    if NQ * j + q >= 4:
                        pe.wait_ge(s["scanned"], NQ * j + q - 3)
                    for g in range(q * Q, (q + 1) * Q):
                        if j < SCANS - 2:
                            mm = pe.matmul(pb[q % 4][:, (g % Q) * P:(g % Q) * P + STARTS + 16],
                                           diag[:, g * P:(g + 1) * P], h3[:, g, :], start=True, stop=True)
                            continue
                        out = pb[q % 4][:, (g % Q) * P:(g % Q) * P + again * BATCH * n]
                        mm = pe.matmul(out.rearrange("p (r b s) -> p r b s", r=again, b=BATCH), diag[:, g * P:(g + 1) * P],
                                       h4[:, g, :, 1:1 + n].unsqueeze(1).to_broadcast([P, again, BATCH, n]),
                                       start=True, stop=True)
                    mm.then_inc(s["scan"], 1)
                    if j < SCANS - 1:
                        pe.wait_ge(s["diagT"], NQ * k + q + 1)
                        power_batch(k, q, 1)

            pe.wait_ge(s["scanned"], NQ * SCANS)
            with pe.Fori(0, GROUPS // AHEAD) as i:
                for k in range(AHEAD):
                    pe.wait_ge(s["expT"], at(i, AHEAD, k + 1))
                    pe.wait_ge(s["y_out"], at(i, AHEAD, k + 1))
                    for m in range(SUPER):
                        n = (SUPER - m) * COLS
                        pe.matmul(pb[k][:, m * COLS:SUPER * COLS], expT[k][:, m * P:(m + 1) * P],
                                  big_a[:, bass.ds(i * AHEAD * 256 + k * 256, n)], start=(m == 0), stop=False,
                                  skip_group_check=True)
                    pe.wait_ge(s["expO"], at(i, AHEAD, k + 1))
                    for m in range(SUPER):
                        mm = pe.matmul(pb[k][:, m * COLS:(m + 1) * COLS], expO[k][:, m * P:(m + 1) * P],
                                       h4[:, bass.ds(i * AHEAD + k, 1), :, 0:SUPERS].rearrange("p g b s -> p (g b) s"),
                                       start=False, stop=(m == SUPER - 1), skip_group_check=True)
                    mm.then_inc(s["y_mm"], 1)

            pe.wait_ge(s["y_out"], GROUPS + AHEAD)
            n3 = n4 = 0
            for mh in range(2):
                for gq in range(GROUPS // 4):
                    if n3 >= 4:
                        pe.wait_ge(s["t3_out"], n3 - 3)
                    for k in range(4):
                        mm = pe.transpose(pb[n3 % 4][:, k * P:(k + 1) * P],
                                          ys[:, 4 * gq + k, mh * P:(mh + 1) * P], ident[:, :])
                    mm.then_inc(s["t3"], 1)
                    n3 += 1
            for mh in range(2):
                rows = tb[mh].rearrange("p (h d j) -> p h j d", h=HALVES, j=POS)
                pe.wait_ge(s["t3_out"], 8 * (mh + 1))
                for h in range(HALVES):
                    for jq in range(4):
                        if n4 >= 4:
                            pe.wait_ge(s["t4_out"], n4 - 3)
                        for k in range(4):
                            mm = pe.transpose(pb[4 + n4 % 4][:, k * P:(k + 1) * P], rows[:, h, 4 * jq + k, :], ident[:, :])
                        mm.then_inc(s["t4"], 1)
                        n4 += 1
            pe.wait_ge(s["t4_out"], n4)
            for c in range(CHUNKS):
                if c >= 2:
                    pe.wait_ge(s["w_out"], c - 1)
                for b in range(BATCH):
                    t0 = b * SEQ + c * P
                    for h in range(HALVES):
                        mm = pe.matmul(pb[c % 2][:, b * P:(b + 1) * P], yT[:, h, t0:t0 + P],
                                       WOUT[:, h * D:(h + 1) * D], start=(h == 0), stop=(h == HALVES - 1))
                mm.then_inc(s["w_mm"], 1)

        @block.scalar
        def _(act):

            def squared(k, q, side):
                n = 2 ** k if k < LEVELS else 0
                act.wait_ge(s["lev_mm"], counts(k, q, side))
                act.wait_ge(s["diagT"] if side == 0 else s["diag"], NQ * k + q + 1)
                dst, bank = (rb, pb[q % 4]) if side == 0 else (rc, pb[4 + q % 4])
                first = 16 + n
                src = bank[:, :].rearrange("p (g n) -> p g n", g=Q)
                if n:
                    act.activation(dst[:, of_batch(q), first:first + n], src[:, :, 16:16 + n], ACT.Copy)
                if k == LEVELS - 1 and side == 0:
                    act.wait_ge(s["zeroed"], 5)
                    act.activation(h3[:, of_batch(q), STARTS:], src[:, :, 0:16], ACT.Copy)
                if k == LEVELS:
                    act.activation(dst[:, of_batch(q), 80:81], src[:, :, 16:17], ACT.Copy)
                act.activation(dst[:, of_batch(q), 0:16], src[:, :, 0:16], ACT.Copy).then_inc(s["lev_out"], 1)

            def columns(i, k):
                act.wait_ge(front.turned, i + 1)
                act.wait_ge(s["u_mm"], i * 2 + 2)
                act.activation(hT[k][:, :], front.turn[k][:, :], ACT.Copy, scale=NW[:, 0:1]).then_inc(s["hT"], 1)

            def channels(i):
                for h in range(HALVES):
                    act.wait_ge(s["u_mm"], i * 2 + h + 5)
                    act.activation(u[:, h, :, bass.ds(i * P + PAD, P)], wide(pb[4 + h][:, :]), ACT.Identity,
                                   bias=BIN[:, h:h + 1]).then_inc(s["u"], 1)
                for h in range(HALVES):
                    act.wait_ge(s["u"], i * 2 + h + 3)
                    act.activation(v[:, h, :, bass.ds(i * P, P)], u[:, h, :, bass.ds(i * P + PAD, P)], ACT.Identity,
                                   bias=CB[:, h:h + 1], scale=CW[:, h * TAPS + PAD:h * TAPS + PAD + 1]
                                   ).then_inc(s["v0"], 1)

            act.sem_inc(s["u"], 2)
            act.sem_inc(s["u_mm"], 4)
            for k in range(LEVELS):
                for q in range(NQ):
                    squared(k, q, 0)
                    squared(k, q, 1)
                    step = STEPS.get((k, q))
                    if step is not None and step < CHUNKS:
                        columns(step, step % 2)
                    if step and step <= CHUNKS:
                        channels(step - 1)
            act.wait_ge(s["zeroed"], 5)
            for q in range(4):
                act.wait_ge(s["g_mm"], q + 1)
                act.activation(g3[:, q * 8:(q + 1) * 8, POS - 1:],
                               pb[q][0:GC, :].rearrange("p (g n) -> p g n", g=8), ACT.Copy).then_inc(s["g_out"], 1)

            n1 = 0
            for mh in range(2):
                for h in range(HALVES):
                    for jq in range(4):
                        act.wait_ge(s["t1"], n1 + 1)
                        dst = tb[mh].rearrange("p (h d j) -> p h j d", h=HALVES, j=POS)[:, h, 12 - 4 * jq:16 - 4 * jq, :]
                        act.activation(dst, wide(pb[n1 % 4][:, :], 4), ACT.Copy).then_inc(s["t1_out"], 1)
                        n1 += 1

            act.sem_inc(s["xW"], AHEAD)
            with act.Fori(0, GROUPS // AHEAD) as i:
                for k in range(AHEAD):
                    act.wait_ge(s["xT"], at(i, AHEAD, AHEAD + k + 1))
                    act.wait_ge(s["x_mm"], at(i, AHEAD, k + 1))
                    act.activation(weightX[k], pb[k][:, :], ACT.Copy).then_inc(s["xW"], 1)
            for k in range(LEVELS, LEVELS + SCANS - 1):
                for q in range(NQ):
                    squared(k, q, 1)
            act.sem_inc(s["y_out"], AHEAD)
            with act.Fori(0, GROUPS // AHEAD) as i:
                for k in range(AHEAD):
                    act.wait_ge(s["y_mm"], at(i, AHEAD, AHEAD + k + 1))
                    act.activation(big_b[:, bass.ds(i * AHEAD * 256 + k * 256, 256)].rearrange("p (c m) -> p m c", m=SUPER),
                                   pb[k][:, 0:256].rearrange("p (m c) -> p m c", m=SUPER), ACT.Copy
                                   ).then_inc(s["y_out"], 1)
            n4 = 0
            for mh in range(2):
                for h in range(HALVES):
                    for jq in range(4):
                        act.wait_ge(s["t4"], n4 + 1)
                        dst = yT[:, h, :].rearrange("p (c j) -> p j c", j=POS)[
                            :, 4 * jq:4 * jq + 4, mh * P:(mh + 1) * P]
                        act.activation(dst, wide(pb[4 + n4 % 4][:, :], 4), ACT.Copy
                                       ).then_inc(s["t4_out"], 1)
                        n4 += 1

        @block.vector
        def _(dve):
            front.moments_of(dve)
            dve.memset(rb[:, :, 17:64], 0.0).then_inc(s["zeroed"], 1)
            dve.memset(rc[:, :, 17:64], 0.0).then_inc(s["zeroed"], 1)
            dve.wait_ge(s["powers_in"], 16 * len(power_loads))
            dve.tensor_copy(rb[:, :, 0:17], ab).then_inc(s["laid"], 1)
            dve.tensor_copy(rc[:, :, 0:17], ac).then_inc(s["laid"], 1)
            dve.tensor_tensor(b_own[:, :].rearrange("p (g d) -> p g d", g=GROUPS),
                              ab[:, :, 16:17].to_broadcast([P, GROUPS, GC]),
                              own[:, :].unsqueeze(1).to_broadcast([P, GROUPS, GC]), ALU.mult).then_inc(s["own"], 1)
            dve.wait_ge(s["zeroed"], 2)
            dve.wait_ge(s["laid"], 2)
            dve.sem_inc(s["laid"], 1)

            def power(k, finished, after=lambda q: None):
                for q in range(NQ):
                    finished(q)
                    dve.tensor_tensor(channel_form(diag[:, q * Q * P:(q + 1) * Q * P], Q), expanded(rc[:, of_batch(q), 0:16]),
                                      own_block(Q), ALU.mult).then_inc(s["diag"], 1)
                    after(q)

            power(0, lambda q: None)
            dve.memset(gsb[:, :], 0.0).then_inc(s["zeroed"], 1)
            dve.memset(H[:, :], 0.0).then_inc(s["zeroed"], 1)
            dve.memset(u[:, :, :, 0:PAD], 0.0).then_inc(s["zeroed"], 1)
            dve.wait_ge(s["zeroed"], 5)
            dve.wait_ge(s["loaded"], 16 * len(loads))
            dve.wait_ge(front.rstd_ready, 2)
            dve.tensor_tensor(msq[:, :], of.var[:, :], of.rstd[:, :], ALU.mult).then_inc(s["msq"], 1)
            dve.wait_ge(s["msq"], 1)
            dve.tensor_tensor(msq[:, :], msq[:, :], of.rstd[:, :], ALU.mult).then_inc(s["msq"], 1)
            dve.wait_ge(s["msq"], 2)
            dve.tensor_scalar(msq[:, :], msq[:, :], RMS_EPS, None, ALU.add).then_inc(s["msq"], 1)
            def tokens(i, k):
                front.normalize(dve, xs, i, k)
                dve.wait_ge(front.normal, i + 1)
                for b in range(BATCH):
                    last = dve.tensor_scalar(hn[k][:, b * P:(b + 1) * P], front.xn[k][:, b * P:(b + 1) * P],
                                             r2[:, bass.ds(i * BATCH + b, 1)], None, ALU.mult)
                last.then_inc(s["hn"], 1)

            def convolved(i):
                for tap, before, after in ((2, "v0", "conv1"), (1, "conv1", "conv2"), (0, "conv2", "conv3")):
                    for h in range(HALVES):
                        dve.wait_ge(s[before], i * 2 + h + 1)
                        out = v[:, h, :, bass.ds(i * P, P)]
                        dve.scalar_tensor_tensor(out, u[:, h, :, bass.ds(i * P + tap, P)],
                                                 CW[:, h * TAPS + tap:h * TAPS + tap + 1], out, ALU.mult,
                                                 ALU.add).then_inc(s[after], 1)

            def token_step(n):
                if n + 1 < CHUNKS:
                    if n >= 1:
                        dve.wait_ge(s["kept"], 2 * (n - 1) + 1)
                        dve.wait_ge(front.turned, n)
                    tokens(n + 1, (n + 1) % 2)
                if n >= 2:
                    convolved(n - 2)

            for k in range(1, LEVELS + 1):
                power(k, lambda q: dve.wait_ge(s["lev_out"], counts(k - 1, q, 1)),
                      lambda q: token_step(STEPS[k - 1, q]) if (k - 1, q) in STEPS else None)
                if k == 1:
                    dve.wait_ge(s["r2"], 1)
                    tokens(0, 0)
            n2 = 0
            for mh in range(2):
                for gq in range(GROUPS // 4):
                    dve.wait_ge(s["t2"], n2 + 1)
                    dve.tensor_copy(u2[:, 4 * gq:4 * gq + 4, :].rearrange("p g (m c) -> p g c m", m=SUPER)[
                                        :, :, mh * COLS // 2:(mh + 1) * COLS // 2, :],
                                    pb[4 + n2 % 4][:, :].rearrange("p (g c m) -> p g c m", g=4, m=SUPER)
                                    ).then_inc(s["t2_out"], 1)
                    n2 += 1

            dve.sem_inc(s["xT"], AHEAD)
            dve.sem_inc(s["x_mm"], AHEAD)
            dve.sem_inc(s["x_out"], AHEAD)
            dve.wait_ge(s["t2_out"], n2)
            def impulses(i, k):
                dve.wait_ge(s["xT"], at(i, AHEAD, k + 1))
                dve.tensor_tensor(channel_form(expB[k], SUPER),
                                  expanded(rb[:, bass.ds(i * AHEAD + k, 1), 16:80]
                                           .rearrange("p g (n s) -> p (g n) s", n=SUPER)),
                                  own_block(SUPER), ALU.mult).then_inc(s["expB"], 1)

            def end_states(i, k):
                dve.wait_ge(s["x_mm"], at(i, AHEAD, AHEAD + k + 1))
                dve.tensor_copy(h4[:, bass.ds(i * AHEAD + k, 1), :, 1:SUPERS + 1].rearrange("p g b s -> p (g b) s"),
                                pb[4 + k][:, 0:COLS].rearrange("p (b s) -> p b s", b=BATCH)).then_inc(s["x_out"], 1)

            for k in range(AHEAD):
                impulses(0, k)
            with dve.Fori(0, GROUPS // AHEAD - 1) as i:
                for k in range(AHEAD):
                    impulses(i + 1, k)
                    end_states(i, k)
            for k in range(AHEAD):
                end_states(GROUPS // AHEAD - 1, k)

            dve.wait_ge(s["x_out"], GROUPS + AHEAD)
            for j in range(SCANS):
                reach = 2 ** j
                n = SUPERS - reach
                for q in range(NQ):
                    dve.wait_ge(s["scan"], NQ * j + q + 1)
                    ends = h4[:, of_batch(q), :, 1 + reach:1 + SUPERS]
                    results = wide(pb[q % 4][:, :], Q)
                    if j < SCANS - 2:
                        moved = results[:, :, 0:STARTS].rearrange("p g (b s) -> p g b s", b=BATCH)[:, :, :, 1:1 + n]
                        dve.wait_ge(s["diagT"], NQ * (LEVELS + j) + q + 1)
                        dve.tensor_copy(h3[:, of_batch(q), STARTS:], results[:, :, STARTS:STARTS + 16])
                    else:
                        moved = results[:, :, 0:BATCH * n].rearrange("p g (b s) -> p g b s", b=BATCH)
                    dve.tensor_tensor(ends, moved, ends,
                                      ALU.add).then_inc(s["scanned"], 1)
                if j < SCANS - 1:
                    power(LEVELS + j + 1, lambda q: dve.wait_ge(s["lev_out"], counts(LEVELS + j, q, 1)))

            dve.sem_inc(s["y_mm"], AHEAD)
            with dve.Fori(0, GROUPS // AHEAD) as i:
                for k in range(AHEAD):
                    dve.wait_ge(s["y_mm"], at(i, AHEAD, k + 1))
                    dve.tensor_tensor(channel_form(expO[k], SUPER),
                                      expanded(rc[:, bass.ds(i * AHEAD + k, 1), 17:81]
                                               .rearrange("p g (n s) -> p (g n) s", n=SUPER)),
                                      own_block(SUPER), ALU.mult).then_inc(s["expO"], 1)

            n3 = 0
            for mh in range(2):
                for gq in range(GROUPS // 4):
                    dve.wait_ge(s["t3"], n3 + 1)
                    dve.tensor_copy(tb[mh][:, gq * 512:(gq + 1) * 512], pb[n3 % 4][:, :]).then_inc(s["t3_out"], 1)
                    n3 += 1
            for c in range(CHUNKS):
                dve.wait_ge(s["w_mm"], c + 1)
                xc = xs[:, c * WIDE:(c + 1) * WIDE]
                dve.tensor_tensor(xc, pb[c % 2][:, :], xc, ALU.add).then_inc(s["w_out"], 1)
                dve.wait_ge(s["w_out"], c + 1)
                of.of_chunk(dve, xs, c)


def build(nc, t, out):
    with ExitStack() as ctx:
        xs = ctx.enter_context(nc.sbuf_tensor("xs", [P, CHUNKS * WIDE], F32))
        of = Statistics(Scope(nc, ctx, "norm"))
        queue_in = nc.dram_tensor("queue_in", (SLOTS, D), F32, kind="Internal").ap()
        queue_out = nc.dram_tensor("queue_out", (SLOTS + 1, D), F32, kind="Internal").ap()
        attention_phase(nc, xs, of, t["x"], t["wq"], t["wk"], t["wv"], t["wg"], t["bg"], t["wo"], t["decay_all"],
                        t["decay_pair"], t["ident"], t["lag"], t["causal"], t["tpos"], t["left"],
                        [queue_in, queue_out[0:SLOTS, :]])
        mixture_phase(nc, xs, of, "moe0", HID0, ACT.Gelu, t["router0"], t["m0w1"], t["m0w2"], t["ident"], t["rank"])
        scratch = nc.dram_tensor("responses", (GC * GROUPS * (POS - 1 + 64),), F32, kind="Internal").ap()
        state_space_phase(nc, xs, of, scratch, t["norm_w"], t["win"], t["b_in"], t["conv_w"], t["conv_b"], t["a_rows_c"],
                          t["a_cols_b"], t["wout"], t["b_out"], t["ident"], t["own"])
        routed_phase(nc, xs, of, queue_in, queue_out, out, t["router1"], t["m1w1"], t["m1w2"], t["m1b1"], t["m1b2"], t["sw1"],
                     t["sw2"], t["sb1"], t["sb2"], t["ident"], t["rank"], t["before"], t["restart"], t["place"])


def laid_out(i):
    def T(w):
        return np.ascontiguousarray(np.swapaxes(w, -1, -2))

    def pair_rows(w, n):
        return np.ascontiguousarray(w.reshape(n, P, -1).transpose(1, 0, 2).reshape(P, -1))

    def by_group(matrices, vectors):
        both = np.concatenate([matrices, vectors.reshape(D_IN, STATES, 1)], axis=2)
        return np.ascontiguousarray(both.reshape(GROUPS, P, STATES + 1).transpose(1, 0, 2))

    a = {k: np.asarray(v) for k, v in i.items()}
    dl = a["L0_attn_decay_log"]
    s_, t_ = np.meshgrid(np.arange(P), np.arange(P), indexing="ij")
    return {
        "x": a["L0_attn_x"],
        "wq": T(a["L0_attn_W_Q"]), "wk": T(a["L0_attn_W_K"]), "wv": T(a["L0_attn_W_V"]), "wg": T(a["L0_attn_W_g_w"]),
        "bg": T(a["L0_attn_W_g_b"].reshape(PAIRS, P)), "wo": pair_rows(T(a["L0_attn_W_O"]), PAIRS),
        "decay_all": np.ascontiguousarray(np.broadcast_to(dl[None], (P, HEADS))),
        "decay_pair": T(np.repeat(dl.reshape(PAIRS, 2), DK, axis=1)),
        "ident": np.eye(P, dtype=np.float32),
        "lag": np.maximum(t_ - s_, 0).astype(np.float32), "causal": (t_ >= s_).astype(np.float32),
        "tpos": np.broadcast_to(np.arange(1, P + 1, dtype=np.float32), (P, P)).copy(),
        "norm_w": a["L1_attn_norm_w"].reshape(D, 1), "win": a["L1_attn_Win"],
        "b_in": T(a["L1_attn_b_in"].reshape(HALVES, P)), "conv_b": T(a["L1_attn_conv_b"].reshape(HALVES, P)),
        "conv_w": pair_rows(a["L1_attn_conv_w"].reshape(D_IN, TAPS), HALVES),
        "a_rows_c": by_group(a["L1_attn_A"], a["L1_attn_Cm"]), "a_cols_b": by_group(T(a["L1_attn_A"]), a["L1_attn_Bm"]),
        "wout": pair_rows(a["L1_attn_Wout"], HALVES),
        "b_out": np.broadcast_to(a["L1_attn_b_out"][None], (P, D)).copy(),
        "own": np.repeat(np.eye(GC, dtype=np.float32), POS, axis=0),
        "router0": T(a["L0_ffn_router_w"]), "m0w1": T(a["L0_ffn_w1"].reshape(-1, D)),
        "m0w2": pair_rows(T(a["L0_ffn_w2"]).reshape(-1, D), EXPERTS * HID0 // P),
        "router1": a["L1_ffn_router_w"],
        "m1w1": pair_rows(a["L1_ffn_w1"].reshape(-1, HID1), EXPERTS),
        "m1w2": pair_rows(a["L1_ffn_w2"].reshape(-1, D), EXPERTS * HID1 // P),
        "m1b1": T(a["L1_ffn_b1"].reshape(-1, P)),
        "m1b2": np.broadcast_to(a["L1_ffn_b2"].reshape(1, -1), (P, EXPERTS * D)).copy(),
        "sw1": a["L1_ffn_sw1"], "sw2": pair_rows(a["L1_ffn_sw2"], HID1 // P),
        "sb1": T(a["L1_ffn_sb1"].reshape(-1, P)), "sb2": np.broadcast_to(a["L1_ffn_sb2"][None], (P, D)).copy(),
        "place": np.broadcast_to((np.repeat(np.arange(EXPERTS) * CAPACITY, TILES) - SLOTS).astype(np.float32),
                                 (P, EXPERTS * TILES)).copy(),
        "rank": np.broadcast_to(np.repeat(np.arange(EXPERTS, 0, -1), TILES).astype(np.float32),
                                (P, EXPERTS * TILES)).copy(),
        "before": (s_ < t_).astype(np.float32),
        "restart": np.broadcast_to((np.arange(2 * EXPERTS * TILES) % TILES != 0).astype(np.float32),
                                   (P, 2 * EXPERTS * TILES)).copy(),
        "left": np.arange(P - 1, -1, -1, dtype=np.float32).reshape(P, 1),
    }


def kernel(**inputs):
    import concourse.bacc as bacc
    from concourse.bass_utils import run_bass_kernel_spmd

    nc = bacc.Bacc("TRN2", target_bir_lowering=False, num_devices=1)
    arrays = laid_out(inputs)
    t = {n: nc.dram_tensor(n, a.shape, mybir.dt.from_np(a.dtype), kind="ExternalInput").ap()
         for n, a in arrays.items()}
    out = nc.dram_tensor("out", (BATCH, SEQ, D), F32, kind="ExternalOutput").ap()
    build(nc, t, out)
    r = run_bass_kernel_spmd(nc, [arrays], core_ids=[0])
    return r.results[0]["out"]
```
